# Optimizing a Trainium2 kernel written in Bass

```python
import numpy as np
import jax
import jax.numpy as jnp

def _softmax(x, axis=-1):
    return jax.nn.softmax(x, axis=axis)

def _gelu(x):
    return jax.nn.gelu(x, approximate=True)

def _silu(x):
    return jax.nn.silu(x)

def _sigmoid(x):
    return jax.nn.sigmoid(x)

def _layernorm(x, axis=-1, eps=1e-05):
    m = jnp.mean(x, axis=axis, keepdims=True)
    v = jnp.var(x, axis=axis, keepdims=True)
    return (x - m) / jnp.sqrt(v + eps)

def _scatter_add(tgt, idx, src, axis=0):
    return tgt.at[idx].add(src)

def _segment_sum(src, seg, n):
    return jax.ops.segment_sum(src, seg, n)
kernel_name = 'mk_flamingo_gated_d2_seqx_r4_206e28'

def setup_inputs(seed: int=0):
    np.random.seed(seed)
    _w = jnp.asarray

    def _rec_inputs():
        import jax
        import jax.numpy as jnp
        _rk = jax.random.key(seed)
        x = -0.0002928 + 1 * jax.random.normal(jax.random.fold_in(_rk, 1), (8, 256, 256), jnp.float32)
        _lenS = 256 - jax.random.randint(jax.random.fold_in(_rk, 7), (8,), 0, max(1, 256 // 4) + 1, jnp.int32)
        _lenS2 = 256 - jax.random.randint(jax.random.fold_in(_rk, 8), (8,), 0, max(1, 256 // 4) + 1, jnp.int32)
        _ctx_1024P = jax.random.normal(jax.random.fold_in(_rk, 11), (8, 16, 256), jnp.float32)
        _ctx_1024c = jax.random.dirichlet(jax.random.fold_in(_rk, 511), 0.3 * jnp.ones((16,), jnp.float32), (8, 256))
        _ctx_1024t = jnp.einsum('bsk,bkd->bsd', _ctx_1024c, _ctx_1024P)
        _ctx_1024t = _ctx_1024t * jax.lax.rsqrt(jnp.mean(jnp.square(_ctx_1024t)) + 1e-12) * 0.953939
        ctx_1024 = -1.39393e-06 + 0.999914 * (_ctx_1024t + 0.3 * jax.random.normal(jax.random.fold_in(_rk, 611), (8, 256, 256), jnp.float32))
        _validS = jnp.arange(256)[None, :] < _lenS[:, None]
        _validS2 = jnp.arange(256)[None, :] < _lenS2[:, None]
        _causal = jnp.tril(jnp.ones((256, 256), dtype=bool))
        mask_1x1xSxS2_ik0 = jnp.where(jnp.broadcast_to(_validS2[0:1, None, None, :], (1, 1, 256, 256)), 0, 1).astype(jnp.int32)
        mask_1x1xSxS2_if1 = jnp.where(jnp.ones((1, 1, 256, 256), dtype=bool), 1, 0).astype(jnp.int32)
        mask_BxS2_bf1 = jnp.ones((8, 256), dtype=bool)
        _g = jax.random.normal(jax.random.fold_in(_rk, 9001), (2, 2), jnp.float32)
        _g = jnp.sign(_g) * jnp.maximum(jnp.abs(_g), 1.0) + (_g == 0) * 1.0
        g_xattn = _g[0]
        g_ffn = _g[1]
        return (x, ctx_1024, mask_1x1xSxS2_ik0, mask_1x1xSxS2_if1, mask_BxS2_bf1, g_xattn, g_ffn)
    x, ctx_1024, mask_1x1xSxS2_ik0, mask_1x1xSxS2_if1, mask_BxS2_bf1, g_xattn, g_ffn = _rec_inputs()

    def _L0_xattn_setup():
        import jax, jax.numpy as jnp
        import numpy as np
        B, S, D, H, FF = (2, 512, 256, 16, 1024)
        DK = D // H
        EPS = 1e-05

        def layer_norm(x, g, b):
            mu = jnp.mean(x, axis=-1, keepdims=True)
            var = jnp.mean(jnp.square(x - mu), axis=-1, keepdims=True)
            return (x - mu) * jax.lax.rsqrt(var + EPS) * g + b

        def mha(q, k, v, wq, bq, wk, bk, wv, bv, wo, bo, mask):
            b, s, d = q.shape
            Q = (q @ wq + bq).reshape(b, s, H, DK).transpose(0, 2, 1, 3)
            K = (k @ wk + bk).reshape(b, s, H, DK).transpose(0, 2, 1, 3)
            V = (v @ wv + bv).reshape(b, s, H, DK).transpose(0, 2, 1, 3)
            att = jnp.einsum('bhqd,bhkd->bhqk', Q, K)
            if mask is not None:
                att = jnp.where(mask == 0, jnp.float32(-1000000000.0), att)
            att = jax.nn.softmax(att, axis=-1)
            out = jnp.einsum('bhqk,bhkd->bhqd', att, V)
            out = out.transpose(0, 2, 1, 3).reshape(b, s, d)
            return out @ wo + bo
        key = jax.random.key(seed)
        ks = jax.random.split(key, 32)
        p = lambda i, shape: jax.random.normal(ks[i], shape, dtype=jnp.float32) * 0.02
        inp = {'x': jax.random.normal(ks[0], (B, S, D), dtype=jnp.float32), 'enc_out': jax.random.normal(ks[1], (B, S, D), dtype=jnp.float32), 'tgt_mask': jnp.tril(jnp.ones((S, S), dtype=jnp.int32))[None, None], 'src_mask': jnp.ones((1, 1, S, S), dtype=jnp.int32), 'm1_wq': p(2, (D, D)), 'm1_bq': jnp.zeros((D,)), 'm1_wk': p(3, (D, D)), 'm1_bk': jnp.zeros((D,)), 'm1_wv': p(4, (D, D)), 'm1_bv': jnp.zeros((D,)), 'm1_wo': p(5, (D, D)), 'm1_bo': jnp.zeros((D,)), 'ln1_g': jnp.ones((D,)), 'ln1_b': jnp.zeros((D,)), 'm2_wq': p(6, (D, D)), 'm2_bq': jnp.zeros((D,)), 'm2_wk': p(7, (D, D)), 'm2_bk': jnp.zeros((D,)), 'm2_wv': p(8, (D, D)), 'm2_bv': jnp.zeros((D,)), 'm2_wo': p(9, (D, D)), 'm2_bo': jnp.zeros((D,)), 'ln2_g': jnp.ones((D,)), 'ln2_b': jnp.zeros((D,)), 'ff_w1': p(10, (D, FF)), 'ff_b1': jnp.zeros((FF,)), 'ff_w2': p(11, (FF, D)), 'ff_b2': jnp.zeros((D,)), 'ln3_g': jnp.ones((D,)), 'ln3_b': jnp.zeros((D,))}
        return inp
    _L0_xattn_all = _L0_xattn_setup()
    _L0_xattn_in = {k: v for k, v in _L0_xattn_all.items() if k in ('m1_wq', 'm1_bq', 'm1_wk', 'm1_bk', 'm1_wv', 'm1_bv', 'm1_wo', 'm1_bo', 'ln1_g', 'ln1_b', 'm2_wq', 'm2_bq', 'm2_wk', 'm2_bk', 'm2_wv', 'm2_bv', 'm2_wo', 'm2_bo', 'ln2_g', 'ln2_b', 'ff_w1', 'ff_b1', 'ff_w2', 'ff_b2', 'ln3_g', 'ln3_b')}
    del _L0_xattn_all

    def _L0_ffn_setup():
        import jax, jax.numpy as jnp
        import numpy as np
        D_MODEL, D_FF, N_EXPERTS, TOP_K = (256, 1024, 8, 2)
        B, S = (4, 512)

        def _moe_forward(x, W1, b1, W2, b2, Wg, bg):
            b, s, d = x.shape
            xt = x.reshape(-1, d)
            T = xt.shape[0]
            router_logits = xt @ Wg + bg
            routing_weights = jax.nn.softmax(router_logits, axis=1)
            topk_w, topk_idx = jax.lax.top_k(routing_weights, TOP_K)
            topk_w = topk_w / jnp.sum(topk_w, axis=1, keepdims=True)
            combine = jnp.zeros((T, N_EXPERTS), dtype=xt.dtype)
            combine = combine.at[jnp.arange(T)[:, None], topk_idx].add(topk_w)
            out = jnp.zeros_like(xt)
            for e in range(N_EXPERTS):
                h = jax.nn.relu(xt @ W1[e] + b1[e])
                y = h @ W2[e] + b2[e]
                out = out + combine[:, e:e + 1] * y
            return out.reshape(b, s, d)
        key = jax.random.key(seed)
        ks = jax.random.split(key, 7)
        scale = 0.02
        x = jax.random.normal(ks[0], (B, S, D_MODEL), dtype=jnp.float32)
        W1 = jax.random.normal(ks[1], (N_EXPERTS, D_MODEL, D_FF), dtype=jnp.float32) * scale
        b1 = jnp.zeros((N_EXPERTS, D_FF), dtype=jnp.float32)
        W2 = jax.random.normal(ks[2], (N_EXPERTS, D_FF, D_MODEL), dtype=jnp.float32) * scale
        b2 = jnp.zeros((N_EXPERTS, D_MODEL), dtype=jnp.float32)
        Wg = jax.random.normal(ks[3], (D_MODEL, N_EXPERTS), dtype=jnp.float32) * scale
        bg = jnp.zeros((N_EXPERTS,), dtype=jnp.float32)
        return {'x': x, 'W1': W1, 'b1': b1, 'W2': W2, 'b2': b2, 'Wg': Wg, 'bg': bg}
    _L0_ffn_all = _L0_ffn_setup()
    _L0_ffn_in = {k: v for k, v in _L0_ffn_all.items() if k in ('W1', 'b1', 'W2', 'b2', 'Wg', 'bg')}
    del _L0_ffn_all

    def _L1_xattn_setup():
        import jax, jax.numpy as jnp
        import numpy as np
        GAMMA = 10.0
        BASE = 10000.0
        SCALE = 64 ** (-0.5)
        NUM_HEADS = 16

        def _larope(t, seq_len):
            B, H, L, D = t.shape
            inv_freq = 1.0 / BASE ** (jnp.arange(0, D, 2, dtype=jnp.float32) / D)
            pos = GAMMA * (jnp.arange(L, dtype=jnp.float32) / float(seq_len))
            ang = pos[:, None] * inv_freq
            cos = jnp.cos(ang)
            sin = jnp.sin(ang)
            te, to = (t[..., 0::2], t[..., 1::2])
            re = te * cos - to * sin
            ro = te * sin + to * cos
            return jnp.stack([re, ro], axis=-1).reshape(t.shape)
        key = jax.random.key(seed)
        ks = jax.random.split(key, 8)
        B, Lq, Lk, D = (8, 512, 128, 256)
        s = D ** (-0.5)
        return {'x': jax.random.normal(ks[0], (B, Lq, D), jnp.float32), 'context': jax.random.normal(ks[1], (B, Lk, D), jnp.float32), 'context_mask': jnp.ones((B, Lk), dtype=bool), 'Wq': jax.random.normal(ks[2], (D, D), jnp.float32) * s, 'bq': jnp.zeros((D,), jnp.float32), 'Wkv': jax.random.normal(ks[3], (D, 2 * D), jnp.float32) * s, 'bkv': jnp.zeros((2 * D,), jnp.float32), 'Wo': jax.random.normal(ks[4], (D, D), jnp.float32) * s, 'bo': jnp.zeros((D,), jnp.float32)}
    _L1_xattn_all = _L1_xattn_setup()
    _L1_xattn_in = {k: v for k, v in _L1_xattn_all.items() if k in ('Wq', 'bq', 'Wkv', 'bkv', 'Wo', 'bo')}
    del _L1_xattn_all

    def _L1_ffn_setup():
        import jax, jax.numpy as jnp
        import numpy as np
        D_MODEL = 256
        D_FF = 1024
        N_EXPERTS = 8
        INIT_SCALE = 0.1

        def _trunc_normal(key, shape, std):
            return std * jax.random.truncated_normal(key, -2.0, 2.0, shape, dtype=jnp.float32)
        key = jax.random.key(seed)
        ks = jax.random.split(key, 5)
        x = jax.random.normal(ks[0], (4, 256, D_MODEL), dtype=jnp.float32)
        router_W = _trunc_normal(ks[1], (D_MODEL, N_EXPERTS), INIT_SCALE / np.sqrt(D_MODEL))
        router_b = jnp.zeros((N_EXPERTS,), dtype=jnp.float32)
        W1 = _trunc_normal(ks[2], (N_EXPERTS, D_MODEL, D_FF), INIT_SCALE / np.sqrt(D_MODEL))
        b1 = jnp.zeros((N_EXPERTS, D_FF), dtype=jnp.float32)
        W2 = _trunc_normal(ks[3], (N_EXPERTS, D_FF, D_MODEL), INIT_SCALE / np.sqrt(D_FF))
        b2 = jnp.zeros((N_EXPERTS, D_MODEL), dtype=jnp.float32)
        return {'x': x, 'router_W': router_W, 'router_b': router_b, 'W1': W1, 'b1': b1, 'W2': W2, 'b2': b2}
    _L1_ffn_all = _L1_ffn_setup()
    _L1_ffn_in = {k: v for k, v in _L1_ffn_all.items() if k in ('router_W', 'router_b', 'W1', 'b1', 'W2', 'b2')}
    del _L1_ffn_all
    return {'x': x, 'ctx_1024': ctx_1024, 'mask_1x1xSxS2_ik0': mask_1x1xSxS2_ik0, 'mask_1x1xSxS2_if1': mask_1x1xSxS2_if1, 'mask_BxS2_bf1': mask_BxS2_bf1, 'g_xattn': g_xattn, 'g_ffn': g_ffn, 'L0_xattn_m1_wq': _L0_xattn_in['m1_wq'], 'L0_xattn_m1_bq': _L0_xattn_in['m1_bq'], 'L0_xattn_m1_wk': _L0_xattn_in['m1_wk'], 'L0_xattn_m1_bk': _L0_xattn_in['m1_bk'], 'L0_xattn_m1_wv': _L0_xattn_in['m1_wv'], 'L0_xattn_m1_bv': _L0_xattn_in['m1_bv'], 'L0_xattn_m1_wo': _L0_xattn_in['m1_wo'], 'L0_xattn_m1_bo': _L0_xattn_in['m1_bo'], 'L0_xattn_ln1_g': _L0_xattn_in['ln1_g'], 'L0_xattn_ln1_b': _L0_xattn_in['ln1_b'], 'L0_xattn_m2_wq': _L0_xattn_in['m2_wq'], 'L0_xattn_m2_bq': _L0_xattn_in['m2_bq'], 'L0_xattn_m2_wk': _L0_xattn_in['m2_wk'], 'L0_xattn_m2_bk': _L0_xattn_in['m2_bk'], 'L0_xattn_m2_wv': _L0_xattn_in['m2_wv'], 'L0_xattn_m2_bv': _L0_xattn_in['m2_bv'], 'L0_xattn_m2_wo': _L0_xattn_in['m2_wo'], 'L0_xattn_m2_bo': _L0_xattn_in['m2_bo'], 'L0_xattn_ln2_g': _L0_xattn_in['ln2_g'], 'L0_xattn_ln2_b': _L0_xattn_in['ln2_b'], 'L0_xattn_ff_w1': _L0_xattn_in['ff_w1'], 'L0_xattn_ff_b1': _L0_xattn_in['ff_b1'], 'L0_xattn_ff_w2': _L0_xattn_in['ff_w2'], 'L0_xattn_ff_b2': _L0_xattn_in['ff_b2'], 'L0_xattn_ln3_g': _L0_xattn_in['ln3_g'], 'L0_xattn_ln3_b': _L0_xattn_in['ln3_b'], 'L0_ffn_W1': _L0_ffn_in['W1'], 'L0_ffn_b1': _L0_ffn_in['b1'], 'L0_ffn_W2': _L0_ffn_in['W2'], 'L0_ffn_b2': _L0_ffn_in['b2'], 'L0_ffn_Wg': _L0_ffn_in['Wg'], 'L0_ffn_bg': _L0_ffn_in['bg'], 'L1_xattn_Wq': _L1_xattn_in['Wq'], 'L1_xattn_bq': _L1_xattn_in['bq'], 'L1_xattn_Wkv': _L1_xattn_in['Wkv'], 'L1_xattn_bkv': _L1_xattn_in['bkv'], 'L1_xattn_Wo': _L1_xattn_in['Wo'], 'L1_xattn_bo': _L1_xattn_in['bo'], 'L1_ffn_router_W': _L1_ffn_in['router_W'], 'L1_ffn_router_b': _L1_ffn_in['router_b'], 'L1_ffn_W1': _L1_ffn_in['W1'], 'L1_ffn_b1': _L1_ffn_in['b1'], 'L1_ffn_W2': _L1_ffn_in['W2'], 'L1_ffn_b2': _L1_ffn_in['b2']}

def reference(x, ctx_1024, mask_1x1xSxS2_ik0, mask_1x1xSxS2_if1, mask_BxS2_bf1, g_xattn, g_ffn, L0_xattn_m1_wq, L0_xattn_m1_bq, L0_xattn_m1_wk, L0_xattn_m1_bk, L0_xattn_m1_wv, L0_xattn_m1_bv, L0_xattn_m1_wo, L0_xattn_m1_bo, L0_xattn_ln1_g, L0_xattn_ln1_b, L0_xattn_m2_wq, L0_xattn_m2_bq, L0_xattn_m2_wk, L0_xattn_m2_bk, L0_xattn_m2_wv, L0_xattn_m2_bv, L0_xattn_m2_wo, L0_xattn_m2_bo, L0_xattn_ln2_g, L0_xattn_ln2_b, L0_xattn_ff_w1, L0_xattn_ff_b1, L0_xattn_ff_w2, L0_xattn_ff_b2, L0_xattn_ln3_g, L0_xattn_ln3_b, L0_ffn_W1, L0_ffn_b1, L0_ffn_W2, L0_ffn_b2, L0_ffn_Wg, L0_ffn_bg, L1_xattn_Wq, L1_xattn_bq, L1_xattn_Wkv, L1_xattn_bkv, L1_xattn_Wo, L1_xattn_bo, L1_ffn_router_W, L1_ffn_router_b, L1_ffn_W1, L1_ffn_b1, L1_ffn_W2, L1_ffn_b2):
    import jax
    import jax.numpy as jnp

    def _L0_xattn_ref(x, enc_out, tgt_mask, src_mask, m1_wq, m1_bq, m1_wk, m1_bk, m1_wv, m1_bv, m1_wo, m1_bo, ln1_g, ln1_b, m2_wq, m2_bq, m2_wk, m2_bk, m2_wv, m2_bv, m2_wo, m2_bo, ln2_g, ln2_b, ff_w1, ff_b1, ff_w2, ff_b2, ln3_g, ln3_b):
        import jax, jax.numpy as jnp
        import numpy as np
        B, S, D, H, FF = (2, 512, 256, 16, 1024)
        DK = D // H
        EPS = 1e-05

        def layer_norm(x, g, b):
            mu = jnp.mean(x, axis=-1, keepdims=True)
            var = jnp.mean(jnp.square(x - mu), axis=-1, keepdims=True)
            return (x - mu) * jax.lax.rsqrt(var + EPS) * g + b

        def mha(q, k, v, wq, bq, wk, bk, wv, bv, wo, bo, mask):
            b, s, d = q.shape
            Q = (q @ wq + bq).reshape(b, s, H, DK).transpose(0, 2, 1, 3)
            K = (k @ wk + bk).reshape(b, s, H, DK).transpose(0, 2, 1, 3)
            V = (v @ wv + bv).reshape(b, s, H, DK).transpose(0, 2, 1, 3)
            att = jnp.einsum('bhqd,bhkd->bhqk', Q, K)
            if mask is not None:
                att = jnp.where(mask == 0, jnp.float32(-1000000000.0), att)
            att = jax.nn.softmax(att, axis=-1)
            out = jnp.einsum('bhqk,bhkd->bhqd', att, V)
            out = out.transpose(0, 2, 1, 3).reshape(b, s, d)
            return out @ wo + bo
        x1 = mha(x, x, x, m1_wq, m1_bq, m1_wk, m1_bk, m1_wv, m1_bv, m1_wo, m1_bo, tgt_mask)
        x2 = layer_norm(x + x1, ln1_g, ln1_b)
        x3 = mha(x2, enc_out, enc_out, m2_wq, m2_bq, m2_wk, m2_bk, m2_wv, m2_bv, m2_wo, m2_bo, src_mask)
        x4 = layer_norm(x2 + x3, ln2_g, ln2_b)
        x5 = jax.nn.relu(x4 @ ff_w1 + ff_b1) @ ff_w2 + ff_b2
        return layer_norm(x4 + x5, ln3_g, ln3_b)

    def _L0_ffn_ref(x, W1, b1, W2, b2, Wg, bg):
        import jax, jax.numpy as jnp
        import numpy as np
        D_MODEL, D_FF, N_EXPERTS, TOP_K = (256, 1024, 8, 2)
        B, S = (4, 512)

        def _moe_forward(x, W1, b1, W2, b2, Wg, bg):
            b, s, d = x.shape
            xt = x.reshape(-1, d)
            T = xt.shape[0]
            router_logits = xt @ Wg + bg
            routing_weights = jax.nn.softmax(router_logits, axis=1)
            topk_w, topk_idx = jax.lax.top_k(routing_weights, TOP_K)
            topk_w = topk_w / jnp.sum(topk_w, axis=1, keepdims=True)
            combine = jnp.zeros((T, N_EXPERTS), dtype=xt.dtype)
            combine = combine.at[jnp.arange(T)[:, None], topk_idx].add(topk_w)
            out = jnp.zeros_like(xt)
            for e in range(N_EXPERTS):
                h = jax.nn.relu(xt @ W1[e] + b1[e])
                y = h @ W2[e] + b2[e]
                out = out + combine[:, e:e + 1] * y
            return out.reshape(b, s, d)
        return _moe_forward(x, W1, b1, W2, b2, Wg, bg)

    def _L1_xattn_ref(x, context, context_mask, Wq, bq, Wkv, bkv, Wo, bo):
        import jax, jax.numpy as jnp
        import numpy as np
        GAMMA = 10.0
        BASE = 10000.0
        SCALE = 64 ** (-0.5)
        NUM_HEADS = 16

        def _larope(t, seq_len):
            B, H, L, D = t.shape
            inv_freq = 1.0 / BASE ** (jnp.arange(0, D, 2, dtype=jnp.float32) / D)
            pos = GAMMA * (jnp.arange(L, dtype=jnp.float32) / float(seq_len))
            ang = pos[:, None] * inv_freq
            cos = jnp.cos(ang)
            sin = jnp.sin(ang)
            te, to = (t[..., 0::2], t[..., 1::2])
            re = te * cos - to * sin
            ro = te * sin + to * cos
            return jnp.stack([re, ro], axis=-1).reshape(t.shape)
        B, Lq, D = x.shape
        Lk = context.shape[1]
        H = NUM_HEADS
        hd = D // H
        q = x @ Wq + bq
        kv = context @ Wkv + bkv
        k, v = jnp.split(kv, 2, axis=-1)
        q = q.reshape(B, Lq, H, hd).transpose(0, 2, 1, 3)
        k = k.reshape(B, Lk, H, hd).transpose(0, 2, 1, 3)
        v = v.reshape(B, Lk, H, hd).transpose(0, 2, 1, 3)
        q = _larope(q, Lq)
        k = _larope(k, Lk)
        scores = jnp.einsum('bhqd,bhkd->bhqk', q, k) * SCALE
        scores = jnp.where(context_mask[:, None, None, :], scores, -jnp.inf)
        attn = jax.nn.softmax(scores, axis=-1)
        out = jnp.einsum('bhqk,bhkd->bhqd', attn, v)
        out = out.transpose(0, 2, 1, 3).reshape(B, Lq, H * hd)
        return out @ Wo + bo

    def _L1_ffn_ref(x, router_W, router_b, W1, b1, W2, b2):
        import jax, jax.numpy as jnp
        import numpy as np
        D_MODEL = 256
        D_FF = 1024
        N_EXPERTS = 8
        INIT_SCALE = 0.1

        def _trunc_normal(key, shape, std):
            return std * jax.random.truncated_normal(key, -2.0, 2.0, shape, dtype=jnp.float32)
        logits = jnp.einsum('bsd,de->bse', x.astype(jnp.float32), router_W) + router_b
        probs = jax.nn.softmax(logits, axis=-1)
        top1 = jnp.argmax(probs, axis=-1)
        mask = jax.nn.one_hot(top1, N_EXPERTS, dtype=x.dtype)
        gates = mask * probs.astype(x.dtype)
        h = jax.nn.relu(jnp.einsum('bsd,edf->besf', x, W1) + b1[:, None, :])
        y = jnp.einsum('besf,efd->besd', h, W2) + b2[:, None, :]
        out = jnp.einsum('bse,besd->bsd', gates, y)
        return out
    x = x + jnp.tanh(g_xattn[0]) * _L0_xattn_ref(_layernorm(x, axis=-1), ctx_1024, mask_1x1xSxS2_ik0, mask_1x1xSxS2_if1, L0_xattn_m1_wq, L0_xattn_m1_bq, L0_xattn_m1_wk, L0_xattn_m1_bk, L0_xattn_m1_wv, L0_xattn_m1_bv, L0_xattn_m1_wo, L0_xattn_m1_bo, L0_xattn_ln1_g, L0_xattn_ln1_b, L0_xattn_m2_wq, L0_xattn_m2_bq, L0_xattn_m2_wk, L0_xattn_m2_bk, L0_xattn_m2_wv, L0_xattn_m2_bv, L0_xattn_m2_wo, L0_xattn_m2_bo, L0_xattn_ln2_g, L0_xattn_ln2_b, L0_xattn_ff_w1, L0_xattn_ff_b1, L0_xattn_ff_w2, L0_xattn_ff_b2, L0_xattn_ln3_g, L0_xattn_ln3_b)
    x = x + jnp.tanh(g_ffn[0]) * _L0_ffn_ref(_layernorm(x, axis=-1), L0_ffn_W1, L0_ffn_b1, L0_ffn_W2, L0_ffn_b2, L0_ffn_Wg, L0_ffn_bg)
    x = x + jnp.tanh(g_xattn[1]) * _L1_xattn_ref(_layernorm(x, axis=-1), ctx_1024, mask_BxS2_bf1, L1_xattn_Wq, L1_xattn_bq, L1_xattn_Wkv, L1_xattn_bkv, L1_xattn_Wo, L1_xattn_bo)
    x = x + jnp.tanh(g_ffn[1]) * _L1_ffn_ref(_layernorm(x, axis=-1), L1_ffn_router_W, L1_ffn_router_b, L1_ffn_W1, L1_ffn_b1, L1_ffn_W2, L1_ffn_b2)
    return x

_drawn_inputs = setup_inputs


def setup_inputs(seed=0):
    import zlib

    import numpy as np

    out = dict(_drawn_inputs(seed))
    spreads = {'g_ffn': (-1.0, 0.6),
     'L0_xattn_m1_bq': (0.0, 0.8),
     'L0_xattn_m1_bk': (0.0, 0.8),
     'L0_xattn_m1_bv': (0.0, 0.496),
     'L0_xattn_m1_bo': (0.0, 0.1),
     'L0_xattn_ln1_g': (1.0, 0.2),
     'L0_xattn_ln1_b': (0.0, 0.1),
     'L0_xattn_m2_bq': (0.0, 0.8),
     'L0_xattn_m2_bk': (0.0, 0.8),
     'L0_xattn_m2_bv': (0.0, 0.568),
     'L0_xattn_m2_bo': (0.0, 0.1),
     'L0_xattn_ln2_g': (1.0, 0.2),
     'L0_xattn_ln2_b': (0.0, 0.1),
     'L0_xattn_ff_b1': (0.0, 0.428),
     'L0_xattn_ff_b2': (0.0, 0.1),
     'L0_xattn_ln3_g': (1.0, 0.2),
     'L0_xattn_ln3_b': (0.0, 0.1),
     'L0_ffn_b1': (0.0, 0.617),
     'L0_ffn_b2': (0.0, 0.272),
     'L0_ffn_bg': (0.0, 0.31),
     'L1_xattn_bq': (0.0, 0.8),
     'L1_xattn_bkv': (0.0, 0.1),
     'L1_xattn_bo': (0.0, 0.1),
     'L1_ffn_router_b': (0.0, 0.8),
     'L1_ffn_b1': (0.0, 0.8),
     'L1_ffn_b2': (0.0, 0.8)}
    factors = {'L0_xattn_m1_wq': 8.0,
     'L0_xattn_m1_wk': 8.0,
     'L0_xattn_m1_wv': 5.023,
     'L0_xattn_m1_wo': 3.092,
     'L0_xattn_m2_wq': 8.0,
     'L0_xattn_m2_wk': 8.0,
     'L1_ffn_router_W': 8.0,
     'L1_ffn_W1': 8.0,
     'L1_ffn_W2': 8.0}
    for name, (base, spread) in spreads.items():
        noise = np.random.default_rng([zlib.crc32(name.encode()), seed]).standard_normal(out[name].shape)
        drawn = base * np.exp(spread * noise) if base else spread * noise
        out[name] = jnp.asarray(drawn.astype(out[name].dtype))
    for name, factor in factors.items():
        out[name] = (out[name] * factor).astype(out[name].dtype)
    return out
```

```python
import concourse.bass as bass
from concourse import mybir
from contextlib import ExitStack, contextmanager

F32 = mybir.dt.float32
BF16 = mybir.dt.bfloat16
I32 = mybir.dt.int32
U32 = mybir.dt.uint32
U8 = mybir.dt.uint8
ACT = mybir.ActivationFunctionType
ALU = mybir.AluOpType
AXX = mybir.AxisListType.X

P = 128
B, SEQ, D = 8, 256, 256
H = 16
DK = D // H
NU = SEQ // P
NC = D // P
T = B * SEQ
NT = T // P
FF = 1024
NF = FF // P
NE = 8
EPS = 1e-5
NEG = -1.0e9
OFF = -1.0e30

Q_PARTS = (0, 0, 1, 0, 1, 2)
K_PARTS = (0, 1, 0, 2, 1, 0)
ROWS = len(Q_PARTS) * DK
ROW_KEY = ROWS
ROW_MAX = ROWS + 1
ROWS_ALL = ROWS + 3
VW = DK + 1
QUADS = H // 4


@contextmanager
def stage_semaphores(nc, tag):
    taken = []

    def sem(n):
        taken.append(nc.alloc_semaphore(f"{tag}_{n}"))
        return taken[-1]

    yield sem
    nc.clear_and_free_semaphores(taken)
    nc.all_engine_barrier()


NORM_STEPS = 8


def norm_tiles(sb):
    return {"stats": sb("stats", [P, NU, 6]), "mv": sb("mv", [P, NU, 2]), "ve": sb("ve", [P, NU]), "std": sb("std", [P, NU]),
            "r0": sb("r0", [P, NU]), "r1": sb("r1", [P, NU]), "r2": sb("r2", [P, NU]), "r3": sb("r3", [P, NU]), "rstd": sb("rstd", [P, NU])}


def norm_rows(nc, dve, x, y, t, step, std_done, n, waited):
    base = NORM_STEPS * n

    def after(i, ins):
        ins.then_inc(step, 1)
        dve.wait_ge(step, base + i)

    for u in range(NU):
        ins = nc.vector.bn_stats(t["stats"][:, u, :], x[:, u, :])
    after(1, ins)
    dve.sem_inc(waited, 1)
    for u in range(NU):
        ins = nc.vector.bn_aggr(t["mv"][:, u, :], t["stats"][:, u, :])
    after(2, ins)
    nc.vector.tensor_scalar(t["ve"][:, :], t["mv"][:, :, 1], EPS, None, ALU.add).then_inc(step, 1)
    dve.wait_ge(std_done, n + 1)
    after(4, nc.vector.reciprocal(t["r0"][:, :], t["std"][:, :]))
    after(5, nc.vector.tensor_tensor(t["r1"][:, :], t["r0"][:, :], t["ve"][:, :], ALU.mult))
    after(6, nc.vector.tensor_tensor(t["r2"][:, :], t["r1"][:, :], t["r0"][:, :], ALU.mult))
    after(7, nc.vector.tensor_scalar(t["r3"][:, :], t["r2"][:, :], -0.5, 1.5, ALU.mult, ALU.add))
    after(8, nc.vector.tensor_tensor(t["rstd"][:, :], t["r0"][:, :], t["r3"][:, :], ALU.mult))
    for u in range(NU):
        ins = nc.vector.tensor_scalar(y[:, u, :], x[:, u, :], t["mv"][:, u, 0:1], t["rstd"][:, u:u + 1],
                                      ALU.subtract, ALU.mult)
    return ins


def norm_root(nc, act, t, step, std_done, n):
    act.wait_ge(step, NORM_STEPS * n + 3)
    nc.scalar.activation(t["std"][:, :], t["ve"][:, :], ACT.Sqrt).then_inc(std_done, 1)


def sequence_rows(a, n):
    if len(a.shape) == 3 and a.shape[0] == B:
        return a[n].rearrange("(u p) d -> p u d", p=P)
    return a[:, bass.ds(n * NU, NU), :]


def first_norm(nc, x, X, Y):
    with ExitStack() as ctx:
        sb = lambda n, s, d=F32: ctx.enter_context(nc.sbuf_tensor(f"ln_{n}", s, d))
        sem = ctx.enter_context(stage_semaphores(nc, "ln"))
        yb = sb("yb", [P, 2, NU, D])
        xb = sb("xb", [P, 2, NU, D])
        t = norm_tiles(sb)
        loaded, x_kept, stored = ([sem(f"{n}{p}") for p in range(2)] for n in ("loaded", "x_kept", "stored"))
        step, std_done, normed, waited, waited_sp = sem("step"), sem("std_done"), sem("normed"), sem("waited"), sem("waited_sp")
        block = ctx.enter_context(nc.Block())

        @block.sync
        def _(sp):
            def load(n, p):
                sp.dma_start(xb[:, p, :, :], sequence_rows(x, n)).then_inc(loaded[p], 16)

            load(0, 0)
            load(1, 1)
            with sp.Fori(0, B // 2 - 1) as j:
                for p in range(2):
                    n = 2 * j + p
                    sp.wait_ge(normed, n + 1)
                    sp.sem_inc(waited_sp, 1)
                    sp.dma_start(sequence_rows(Y, n), yb[:, p, :, :]).then_inc(stored[p], 16)
                    sp.dma_start(sequence_rows(X, n), xb[:, p, :, :]).then_inc(x_kept[p], 16)
                    sp.wait_ge(x_kept[p], 16 * (j + 1))
                    sp.sem_inc(waited_sp, 1)
                    load(n + 2, p)
            for p in range(2):
                n = B - 2 + p
                sp.wait_ge(normed, n + 1)
                sp.dma_start(sequence_rows(Y, n), yb[:, p, :, :]).then_inc(stored[p], 16)
                sp.dma_start(sequence_rows(X, n), xb[:, p, :, :]).then_inc(x_kept[p], 16)
            for p in range(2):
                sp.wait_ge(stored[p], 16 * (B // 2))
                sp.wait_ge(x_kept[p], 16 * (B // 2))

        @block.scalar
        def _(act):
            with act.Fori(0, B) as n:
                norm_root(nc, act, t, step, std_done, n)

        @block.vector
        def _(dve):
            def norm(n, p, k):
                dve.wait_ge(loaded[p], 16 * (k + 1))
                norm_rows(nc, dve, xb[:, p], yb[:, p], t, step, std_done, n, waited).then_inc(normed, 1)

            norm(0, 0, 0)
            norm(1, 1, 0)
            with dve.Fori(1, B // 2) as j:
                for p in range(2):
                    dve.wait_ge(stored[p], 16 * j)
                    norm(2 * j + p, p, j)


def mask_setup(nc, mask, ident, Bm, BmT, R, tag):
    with ExitStack() as ctx:
        sb = lambda n, s, d: ctx.enter_context(nc.sbuf_tensor(f"{tag}_{n}", s, d))
        sem = ctx.enter_context(stage_semaphores(nc, tag))
        mi = sb("mi", [P, NU, SEQ], I32)
        keep = sb("keep", [P, NU, SEQ], F32)
        rowkeep = sb("rowkeep", [P, NU], F32)
        bias = sb("bias", [P, NU, SEQ], F32)
        rowtile = sb("rowtile", [P, NU, P], F32)
        pT = [ctx.enter_context(nc.psum_tensor(f"{tag}_pT{k}", [P, 512], F32)) for k in range(2)]
        loaded, step, turned = sem("loaded"), sem("step"), sem("turned")
        block = ctx.enter_context(nc.Block())

        @block.sync
        def _(sp):
            sp.dma_start(mi[:, :, :], mask[0, 0].rearrange("(u p) k -> p u k", p=P)).then_inc(loaded, 16)

        @block.vector
        def _(dve):
            dve.wait_ge(loaded, 16)
            nc.vector.tensor_scalar(keep[:, :, :], mi[:, :, :], 0.0, None, ALU.not_equal).then_inc(step, 1)
            dve.wait_ge(step, 1)
            nc.vector.tensor_reduce(rowkeep[:, :], keep[:, :, :], AXX, ALU.max).then_inc(step, 1)
            dve.wait_ge(step, 2)
            nc.vector.tensor_scalar(bias[:, :, :], keep[:, :, :], 1.0, -NEG, ALU.subtract, ALU.mult).then_inc(step, 1)
            dve.wait_ge(step, 3)
            for u in range(NU):
                nc.vector.tensor_scalar(Bm[:, u * SEQ:(u + 1) * SEQ], bias[:, u, :], rowkeep[:, u:u + 1], None, ALU.mult)
                nc.vector.tensor_scalar(keep[:, u, :], bias[:, u, :], rowkeep[:, u:u + 1], None, ALU.mult)
                ins = nc.vector.tensor_scalar(rowtile[:, u, :], bias[:, u, 0:P], 0.0, rowkeep[:, u:u + 1], ALU.mult, ALU.add)
            ins.then_inc(step, 1)
            dve.wait_ge(turned, 1)
            nc.vector.tensor_copy(BmT[:, :], pT[0][:, :])
            nc.vector.tensor_copy(R[:, :], pT[1][:, 0:SEQ])

        @block.tensor
        def _(pe):
            pe.wait_ge(step, 4)
            for kt in range(NU):
                for u in range(NU):
                    nc.tensor.transpose(pT[0][:, kt * SEQ + u * P:kt * SEQ + (u + 1) * P],
                                        keep[:, u, kt * P:(kt + 1) * P], ident[:, :])
            for u in range(NU):
                ins = nc.tensor.transpose(pT[1][:, u * P:(u + 1) * P], rowtile[:, u, :], ident[:, :])
            ins.then_inc(turned, 1)


def attention(nc, tag, c, src, ctx_in, w, out_ao, mask=None, rope=None):
    cross = ctx_in is not None
    masked = mask is not None
    with ExitStack() as ctx:
        sb = lambda n, s, d=F32: ctx.enter_context(nc.sbuf_tensor(f"{tag}_{n}", s, d))
        sem = ctx.enter_context(stage_semaphores(nc, tag))
        pair = lambda n: [sem(n + "0"), sem(n + "1")]
        bank = lambda n: ctx.enter_context(nc.psum_tensor(f"{tag}_{n}", [P, 512], F32))

        yb = sb("yb", [P, 2, NU, D])
        yT = sb("yT", [P, NC, SEQ])
        cin = sb("cin", [P, 2, NU, D]) if cross else None
        cT = sb("cT", [P, NC, SEQ]) if cross else yT
        wq, wk, wv = sb("wq", [P, NC, D]), sb("wk", [P, NC, D]), sb("wv", [P, NC, D])
        bq, bk, bv = sb("bq", [P, NC]), sb("bk", [P, NC]), sb("bv", [P, D])
        fq, fk = sb("fq", [P, NC * SEQ]), sb("fk", [P, NC * SEQ])
        rq, rk = sb("rq", [P, NC * SEQ]), sb("rk", [P, NC * SEQ])
        pq, pk = sb("pq", [P, 3, NC, SEQ], BF16), sb("pk", [P, 3, NC, SEQ], BF16)
        QS, KS = sb("QS", [P, 2, H, SEQ], BF16), sb("KS", [P, 2, H, SEQ], BF16)
        V = sb("V", [P, 2, NU, H * VW + 32])
        PT = sb("PT", [P, 4, NU * SEQ])
        OTS = sb("OTS", [P, 2, SEQ])
        AO = sb("AO", [P, 2, NU, D])
        rec = sb("rec", [P, NU, 4])
        mx = sb("mx", [P, NU, H])
        MQ = sb("MQ", [P, NU, 2 * H], BF16)
        MT = sb("MT", [2 * H, SEQ], BF16)
        if rope:
            wqs, wks = sb("wqs", [P, NC, D]), sb("wks", [P, NC, D])
            bqs, bks = sb("bqs", [P, NC]), sb("bks", [P, NC])
            tq, tk = sb("tq", [P, NC * SEQ]), sb("tk", [P, NC * SEQ])
            mcu, mcf = sb("mcu", [P, 2, NU], U8), sb("mcf", [P, 2, NU])
            cosq, sinq, cosk, sink = (sb(n, [P, SEQ]) for n in ("cosq", "sinq", "cosk", "sink"))
        bankS = [bank("S0"), bank("S1")]
        bankT = [bank("T0"), bank("T1")]
        bankO = [bank("O0"), bank("O1")]
        bankA, bankB = bank("A"), bank("B")
        bankB16 = bankB[:, 0:P].bitcast(BF16)

        dram = lambda n, s: nc.dram_tensor(f"{tag}_{n}", s, BF16, kind="Internal").ap()
        q_dram, k_dram = dram("q_dram", (2, 3, D, SEQ)), dram("k_dram", (2, 3, D, SEQ))
        m_dram = dram("m_dram", (2, H, SEQ))

        w_loaded, ready0, waited = sem("w_loaded"), sem("ready0"), sem("waited")
        x_loaded, c_loaded, stacked, max_rows = pair("x_loaded"), pair("c_loaded"), pair("stacked"), pair("max_rows")
        ao_stored, mc_loaded = pair("ao_stored"), pair("mc_loaded")
        spread, m_spread = pair("spread"), sem("m_spread")
        t_ready, tc_ready, t_out, tc_out = sem("t_ready"), sem("tc_ready"), sem("t_out"), sem("tc_out")
        q_ready, k_ready, v_ready = sem("q_ready"), sem("k_ready"), sem("v_ready")
        q_out, k_out, v_out = sem("q_out"), sem("k_out"), sem("v_out")
        qr_ready, kr_ready, qr_out, kr_out = sem("qr_ready"), sem("kr_ready"), sem("qr_out"), sem("kr_out")
        f_sum = sem("f_sum")
        part1, part2, part3, rest1 = sem("part1"), sem("part2"), sem("part3"), sem("rest1")
        s_ready, max_done, m_step, mt_ready, mt_out = sem("s_ready"), sem("max_done"), sem("m_step"), sem("mt_ready"), sem("mt_out")
        st_ready, exp_done, pv_done = sem("st_ready"), sem("exp_done"), sem("pv_done")
        ot_out, ot_turned, rec_done, head_norm = sem("ot_out"), sem("ot_turned"), sem("rec_done"), sem("head_norm")
        mc_step = sem("mc_step")
        N_W = 6 + 4 * bool(rope) + 4 * bool(rope)

        def steps(eng, body, first):
            first()
            with eng.Fori(0, B // 2 - 1) as j:
                body(2 * j, 0, j, True, True)
                body(2 * j + 1, 1, j, True, True)
            body(B - 2, 0, B // 2 - 1, True, False)
            body(B - 1, 1, B // 2 - 1, False, False)

        block = ctx.enter_context(nc.Block())

        @block.sync
        def _(sp):
            def wait(semaphore, value):
                sp.wait_ge(semaphore, value)
                if not isinstance(value, int):
                    sp.sem_inc(waited, 1)

            def load_x(n, p, k):
                if not (isinstance(n, int) and n < 2):
                    wait(t_ready, n - 1)
                sp.dma_start(yb[:, p, :, :], sequence_rows(src, n)).then_inc(x_loaded[p], 16)
                if cross:
                    if not (isinstance(n, int) and n < 2):
                        wait(tc_ready, n - 1)
                    sp.dma_start(cin[:, p, :, :], sequence_rows(ctx_in, n)).then_inc(c_loaded[p], 16)

            def stack(n, p, k):
                if not (isinstance(n, int) and n < 2):
                    wait(pv_done, 16 * n - 12)
                elif isinstance(n, int) and n == 0:
                    wait(ready0, 1)
                for side, (parts, dram, dst, which) in enumerate(((pq, q_dram, QS, Q_PARTS), (pk, k_dram, KS, K_PARTS))):
                    wait(part3, 2 * n + 1 + side)
                    sp.dma_start(dram[p].rearrange("s (c r) t -> r s c t", r=P), parts[:, :, :, :]).then_inc(spread[side], 16)
                    wait(spread[side], 16 * (n + 1))
                    for r, part in enumerate(which):
                        sp.dma_start(dst[r * DK:(r + 1) * DK, p, :, :],
                                     dram[p, part].rearrange("(h d) t -> d h t", d=DK)).then_inc(stacked[p], 16)
                if rope:
                    sp.dma_start(KS[ROW_KEY:ROW_KEY + 1, p, :, :],
                                 rope["key_off"][bass.ds(n, 1), :].unsqueeze(1).broadcast_to([1, H, SEQ])).then_inc(stacked[p], 16)
                    sp.dma_start(mcu[:, p, :], rope["keys"][bass.ds(n, 1), :].rearrange("o (u p) -> p (o u)", p=P),
                                 allow_slow_non_contiguous=True).then_inc(mc_loaded[p], 16)

            def first():
                for a, d in ((wq, w["wq"]), (wk, w["wk"]), (wv, w["wv"])):
                    sp.dma_start(a[:, :, :], d.rearrange("(c p) n -> p c n", p=P)).then_inc(w_loaded, 16)
                sp.dma_start(bq[:, :], w["bq"].rearrange("(c p) -> p c", p=P), allow_slow_non_contiguous=True).then_inc(w_loaded, 16)
                sp.dma_start(bk[:, :], w["bk"].rearrange("(c p) -> p c", p=P), allow_slow_non_contiguous=True).then_inc(w_loaded, 16)
                sp.dma_start(bv[:, :], w["bv"].partition_broadcast(P)).then_inc(w_loaded, 16)
                if rope:
                    for a, d in ((wqs, w["wqs"]), (wks, w["wks"])):
                        sp.dma_start(a[:, :, :], d.rearrange("(c p) n -> p c n", p=P)).then_inc(w_loaded, 16)
                    for a, d in ((bqs, w["bqs"]), (bks, w["bks"])):
                        sp.dma_start(a[:, :], d.rearrange("(c p) -> p c", p=P), allow_slow_non_contiguous=True).then_inc(w_loaded, 16)
                    for a, d in ((cosq, "cosq"), (sinq, "sinq"), (cosk, "cosk"), (sink, "sink")):
                        sp.dma_start(a[:, :], rope[d]).then_inc(w_loaded, 16)
                for n in range(2):
                    load_x(n, n, 0)
                stack(0, 0, 0)

            def body(n, p, k, project, load):
                if load:
                    load_x(n + 2, p, k + 1)
                wait(mt_out, n + 1)
                sp.dma_start(m_dram.rearrange("j h t -> (j h) t"), MT[:, :]).then_inc(m_spread, 16)
                wait(m_spread, 16 * (n + 1))
                sp.dma_start(QS[ROW_MAX:ROW_MAX + 2, p, :, :], m_dram).then_inc(max_rows[p], 16)
                if project:
                    stack(n + 1, 1 - p, k + p)
                wait(head_norm, QUADS * (n + 2))
                sp.dma_start(sequence_rows(out_ao, n), AO[:, p, :, :]).then_inc(ao_stored[p], 16)

            steps(sp, body, first)
            for p in range(2):
                wait(ao_stored[p], 16 + 16 * (B // 2))

        @block.tensor
        def _(pe):
            ident = c["ident"]
            identb = c["identb"]

            def turn(n, p, k):
                pe.wait_ge(x_loaded[p], 16 * (k + 1))
                if not (isinstance(n, int) and n == 0):
                    pe.wait_ge(v_out, n)
                    pe.wait_ge(head_norm, QUADS * n - 1)
                for cc in range(NC):
                    for u in range(NU):
                        ins = nc.tensor.transpose(bankA[:, cc * SEQ + u * P:cc * SEQ + (u + 1) * P],
                                                  yb[:, p, u, cc * P:(cc + 1) * P], ident[:, :])
                ins.then_inc(t_ready, 1)
                if cross:
                    pe.wait_ge(c_loaded[p], 16 * (k + 1))
                    if not (isinstance(n, int) and n == 0):
                        pe.wait_ge(kr_out if rope else k_out, n)
                        pe.wait_ge(head_norm, QUADS * n)
                    for cc in range(NC):
                        for u in range(NU):
                            ins = nc.tensor.transpose(bankB[:, cc * SEQ + u * P:cc * SEQ + (u + 1) * P],
                                                      cin[:, p, u, cc * P:(cc + 1) * P], ident[:, :])
                    ins.then_inc(tc_ready, 1)

            def turn_max(n, more):
                pe.wait_ge(m_step, 2 * n + 2)
                pe.wait_ge(head_norm, QUADS * (n + 1))
                if cross and more:
                    pe.wait_ge(tc_out, n + 2)
                for u in range(NU):
                    ins = nc.tensor.transpose(bankB16[0:2 * H, u * P:(u + 1) * P], MQ[:, u, :], identb[:, :])
                ins.then_inc(mt_ready, 1)

            def product(dst, wt, rhs, done):
                for cc in range(NC):
                    for kc in range(NC):
                        ins = nc.tensor.matmul(dst[:, cc * SEQ:(cc + 1) * SEQ], wt[:, kc, cc * P:(cc + 1) * P],
                                               rhs[:, kc, :], start=(kc == 0), stop=(kc == NC - 1))
                ins.then_inc(done, 1)

            def project(n, p, k):
                pe.wait_ge(t_out, n + 1)
                product(bankA, wq, yT, q_ready)
                if cross:
                    pe.wait_ge(tc_out, n + 1)
                if not (isinstance(n, int) and n == 0):
                    pe.wait_ge(mt_out, n)
                if rope:
                    product(bankB, wqs, yT, qr_ready)
                    pe.wait_ge(q_out, n + 1)
                    product(bankA, wk, cT, k_ready)
                    pe.wait_ge(qr_out, n + 1)
                    product(bankB, wks, cT, kr_ready)
                    pe.wait_ge(k_out, n + 1)
                else:
                    product(bankB, wk, cT, k_ready)
                    pe.wait_ge(q_out, n + 1)
                for u in range(NU):
                    for kc in range(NC):
                        ins = nc.tensor.matmul(bankA[:, u * D:(u + 1) * D], cT[:, kc, u * P:(u + 1) * P], wv[:, kc, :],
                                               start=(kc == 0), stop=(kc == NC - 1))
                ins.then_inc(v_ready, 1)

            rows = ROW_KEY + 1 if rope else ROWS

            def scores(n, p, k, h):
                if h == 0:
                    pe.wait_ge(stacked[p], 16 * (2 * len(Q_PARTS) + bool(rope)) * (k + 1))
                pe.wait_ge(max_done, H * n + h + 1)
                bk_ = bankS[h % 2]
                if masked:
                    nc.tensor.matmul(bk_[:, :], identb[:, :], mask[0][:, :], start=True, stop=False)
                for u in range(NU):
                    ins = nc.tensor.matmul(bk_[:, u * SEQ:(u + 1) * SEQ], QS[0:rows, p, h, u * P:(u + 1) * P],
                                           KS[0:rows, p, h, :], start=not masked, stop=(not masked or u == NU - 1))
                ins.then_inc(s_ready, 1)

            def scores_T(n, p, k, h):
                if h == 0:
                    pe.wait_ge(max_rows[p], 16 * (k + 1))
                pe.wait_ge(exp_done, H * n + h + 1)
                bk_ = bankT[h % 2]
                if masked:
                    nc.tensor.matmul(bk_[:, :], identb[:, :], mask[1][:, :], start=True, stop=False)
                for u in range(NU):
                    ins = nc.tensor.matmul(bk_[:, u * SEQ:(u + 1) * SEQ], KS[0:ROWS_ALL, p, h, u * P:(u + 1) * P],
                                           QS[0:ROWS_ALL, p, h, :], start=not masked, stop=(not masked or u == NU - 1))
                ins.then_inc(st_ready, 1)

            def values(n, p, k, h):
                pe.wait_ge(exp_done, H * n + h + 3)
                if h == 0:
                    pe.wait_ge(v_out, n + 1)
                if h % 4 == 0:
                    pe.wait_ge(ot_out, QUADS * n + h // 4 + 1)
                o = bankO[(h // 4) % 2][32 * (h % 4):32 * (h % 4) + 32, 0:SEQ]
                for u in range(NU):
                    ins = nc.tensor.matmul(o, V[:, p, u, h * VW:h * VW + 32], PT[:, h % 4, u * SEQ:(u + 1) * SEQ],
                                           start=(u == 0), stop=(u == NU - 1))
                ins.then_inc(pv_done, 1)

            def turn_out(n, g, more):
                pe.wait_ge(ot_out, QUADS * n + g + 3)
                if g == 0:
                    pe.wait_ge(head_norm, QUADS * n + 3)
                    if more:
                        pe.wait_ge(v_out, n + 2)
                elif g == 1:
                    pe.wait_ge(head_norm, QUADS * (n + 1))
                    pe.wait_ge(mt_out, n + 1)
                    if more:
                        pe.wait_ge(kr_out if rope else k_out, n + 2)
                else:
                    pe.wait_ge(head_norm, QUADS * (n + 1) + g - 1)
                bk_ = (bankA, bankB)[g % 2]
                for u in range(NU):
                    ins = nc.tensor.transpose(bk_[:, u * P:(u + 1) * P], OTS[:, g % 2, u * P:(u + 1) * P], ident[:, :])
                ins.then_inc(ot_turned, 1)

            def first():
                pe.wait_ge(w_loaded, 16 * N_W)
                pe.wait_ge(ready0, 1)
                turn(0, 0, 0)
                project(0, 0, 0)
                for h in range(H):
                    scores(0, 0, 0, h)

            def body(n, p, k, project_next, load):
                if project_next:
                    turn(n + 1, 1 - p, k + p)
                turn_max(n, project_next)
                if project_next:
                    project(n + 1, 1 - p, k + p)
                for h in range(H):
                    scores_T(n, p, k, h)
                    if h >= 1:
                        values(n, p, k, h - 1)
                    if h in (6, 10, 14):
                        turn_out(n, (h - 6) // 4, project_next)
                    if project_next and 6 <= h < 14:
                        scores(n + 1, 1 - p, k + p, 2 * (h - 6))
                        scores(n + 1, 1 - p, k + p, 2 * (h - 6) + 1)
                values(n, p, k, H - 1)
                turn_out(n, QUADS - 1, project_next)

            steps(pe, body, first)

        @block.scalar
        def _(act):
            def bring(n):
                act.wait_ge(t_ready, n + 1)
                if not (isinstance(n, int) and n == 0):
                    act.wait_ge(v_ready, n)
                nc.scalar.activation(yT[:, :, :].rearrange("p c t -> p (c t)"), bankA[:, :], ACT.Copy).then_inc(t_out, 1)
                if cross:
                    act.wait_ge(tc_ready, n + 1)
                    nc.scalar.activation(cT[:, :, :].rearrange("p c t -> p (c t)"), bankB[:, :], ACT.Copy).then_inc(tc_out, 1)

            def first_part(n, side, f, parts):
                if rope:
                    act.wait_ge(f_sum, 2 * n + 1 + side)
                else:
                    act.wait_ge((q_out, k_out)[side], n + 1)
                if not (isinstance(n, int) and n == 0):
                    act.wait_ge(s_ready, H * (n - 1) + 1)
                nc.scalar.activation(parts[:, 0, :, :].rearrange("p c t -> p (c t)"), f[:, :], ACT.Copy).then_inc(part1, 1)

            def second_part(n, side, r, parts):
                act.wait_ge(rest1, 2 * n + 1 + side)
                nc.scalar.activation(parts[:, 1, :, :].rearrange("p c t -> p (c t)"), r[:, :], ACT.Copy).then_inc(part2, 1)

            def keys(n):
                if rope:
                    return
                act.wait_ge(k_ready, n + 1)
                if not (isinstance(n, int) and n == 0):
                    act.wait_ge(rest1, 2 * n)
                for cc in range(NC):
                    ins = nc.scalar.activation(fk[:, cc * SEQ:(cc + 1) * SEQ], bankB[:, cc * SEQ:(cc + 1) * SEQ],
                                               ACT.Identity, bias=bk[:, cc:cc + 1])
                ins.then_inc(k_out, 1)

            def exps(n, h):
                act.wait_ge(st_ready, H * n + h + 1)
                act.wait_ge(pv_done, H * n + h + 1)
                nc.scalar.activation(PT[:, h % 4, :], bankT[h % 2][:, :], ACT.Exp).then_inc(exp_done, 1)

            def outputs(n, g):
                act.wait_ge(pv_done, H * n + 4 * g + 8)
                act.wait_ge(ot_turned, QUADS * n + g + 1)
                nc.scalar.activation(OTS[:, g % 2, :], bankO[g % 2][:, 0:SEQ], ACT.Copy).then_inc(ot_out, 1)

            def first():
                act.sem_inc(exp_done, 2)
                act.sem_inc(ot_out, 2)
                act.wait_ge(w_loaded, 16 * N_W)
                bring(0)
                first_part(0, 0, fq, pq)
                keys(0)
                first_part(0, 1, fk, pk)
                second_part(0, 0, rq, pq)
                second_part(0, 1, rk, pk)

            def body(n, p, k, project_next, load):
                if project_next:
                    bring(n + 1)
                    first_part(n + 1, 0, fq, pq)
                    keys(n + 1)
                    first_part(n + 1, 1, fk, pk)
                    second_part(n + 1, 0, rq, pq)
                for h in range(H):
                    exps(n, h)
                    if h == 0 and project_next:
                        second_part(n + 1, 1, rk, pk)
                    if h in (5, 9, 13):
                        outputs(n, (h - 5) // 4)
                outputs(n, QUADS - 1)

            steps(act, body, first)

        @block.gpsimd
        def _(pool):
            def split(n):
                if rope:
                    for side, (f, t) in enumerate(((fq, tq), (fk, tk))):
                        pool.wait_ge((qr_out, kr_out)[side], n + 1)
                        nc.gpsimd.tensor_tensor(f[:, :], f[:, :], t[:, :], ALU.add).then_inc(f_sum, 1)
                for side, (f, r, parts) in enumerate(((fq, rq, pq), (fk, rk, pk))):
                    pool.wait_ge(part1, 2 * n + 1 + side)
                    nc.gpsimd.tensor_tensor(r[:, :], f[:, :], parts[:, 0, :, :].rearrange("p c t -> p (c t)"),
                                            ALU.subtract).then_inc(rest1, 1)
                for side, (r, parts) in enumerate(((rq, pq), (rk, pk))):
                    pool.wait_ge(part2, 2 * n + 1 + side)
                    nc.gpsimd.tensor_tensor(parts[:, 2, :, :].rearrange("p c t -> p (c t)"), r[:, :],
                                            parts[:, 1, :, :].rearrange("p c t -> p (c t)"), ALU.subtract).then_inc(part3, 1)

            def body(n, p, k, project_next, load):
                if project_next:
                    split(n + 1)

            steps(pool, body, lambda: split(0))

        @block.vector
        def _(dve):
            def queries(n):
                dve.wait_ge(q_ready, n + 1)
                if not (isinstance(n, int) and n == 0):
                    dve.wait_ge(rest1, 2 * n - 1)
                for cc in range(NC):
                    cols = slice(cc * SEQ, (cc + 1) * SEQ)
                    ins = nc.vector.scalar_tensor_tensor(fq[:, cols], bankA[:, cols], bq[:, cc:cc + 1],
                                                         cosq[:, :] if rope else mask[2][:, :], ALU.add, ALU.mult)
                ins.then_inc(q_out, 1)
                if rope:
                    for src_, b_, tab, dst, rdy, out in ((bankB, bqs, sinq, tq, qr_ready, qr_out),
                                                         (bankA, bk, cosk, fk, k_ready, k_out),
                                                         (bankB, bks, sink, tk, kr_ready, kr_out)):
                        dve.wait_ge(rdy, n + 1)
                        if dst is fk and not (isinstance(n, int) and n == 0):
                            dve.wait_ge(rest1, 2 * n)
                        for cc in range(NC):
                            cols = slice(cc * SEQ, (cc + 1) * SEQ)
                            ins = nc.vector.scalar_tensor_tensor(dst[:, cols], src_[:, cols], b_[:, cc:cc + 1],
                                                                 tab[:, :], ALU.add, ALU.mult)
                        ins.then_inc(out, 1)

            def value_rows(n, p, k):
                if rope:
                    dve.wait_ge(mc_loaded[p], 16 * (k + 1))
                    nc.vector.tensor_copy(mcf[:, p, :], mcu[:, p, :]).then_inc(mc_step, 1)
                    dve.wait_ge(mc_step, 2 * n + 1)
                dve.wait_ge(v_ready, n + 1)
                if not (isinstance(n, int) and n < 2):
                    dve.wait_ge(pv_done, H * n - 12)
                heads = [V[:, p, u, 0:H * VW].rearrange("p (h e) -> p h e", e=VW) for u in range(NU)]
                for u in range(NU):
                    ins = nc.vector.tensor_tensor(heads[u][:, :, 0:DK], bankA[:, u * D:(u + 1) * D].rearrange("p (h e) -> p h e", e=DK),
                                                  bv[:, :].rearrange("p (h e) -> p h e", e=DK), ALU.add)
                if rope:
                    ins.then_inc(mc_step, 1)
                    dve.wait_ge(mc_step, 2 * n + 2)
                    for u in range(NU):
                        nc.vector.tensor_copy(heads[u][:, :, DK], mcf[:, p, u:u + 1].broadcast_to([P, H]))
                        ins = nc.vector.tensor_scalar(heads[u][:, :, 0:DK], heads[u][:, :, 0:DK], mcf[:, p, u:u + 1],
                                                      None, ALU.mult)
                ins.then_inc(v_out, 1)

            def maxima(n, h):
                dve.wait_ge(s_ready, H * n + h + 1)
                if h == 0 and not (isinstance(n, int) and n == 0):
                    dve.wait_ge(m_step, 2 * n)
                nc.vector.tensor_reduce(mx[:, :, h:h + 1], bankS[h % 2][:, :].rearrange("p (u k) -> p u k", u=NU),
                                        AXX, ALU.max).then_inc(max_done, 1)

            def minus_maxima(n):
                dve.wait_ge(max_done, H * n + H + 2)
                nc.vector.tensor_scalar(MQ[:, :, 0:H], mx[:, :, :], -1.0, None, ALU.mult).then_inc(m_step, 1)
                dve.wait_ge(m_step, 2 * n + 1)
                nc.vector.scalar_tensor_tensor(MQ[:, :, H:2 * H], mx[:, :, :], -1.0, MQ[:, :, 0:H],
                                               ALU.mult, ALU.subtract).then_inc(m_step, 1)

            def max_columns(n):
                dve.wait_ge(mt_ready, n + 1)
                nc.vector.tensor_copy(MT[:, :], bankB16[0:2 * H, 0:SEQ]).then_inc(mt_out, 1)

            def normalise(n, p, k, g):
                dve.wait_ge(ot_turned, QUADS * n + g + 3)
                if g == 0:
                    dve.wait_ge(ao_stored[p], 16 * (k + 1))
                o = (bankA, bankB)[g % 2][:, 0:NU * P].rearrange("p (g e) -> p g e", e=32)
                dve.wait_ge(head_norm, QUADS * n + g + 4)
                nc.vector.reciprocal(rec[:, :, :].rearrange("p u h -> p (u h)"), o[:, :, DK]).then_inc(rec_done, 1)
                dve.wait_ge(rec_done, QUADS * n + g + 1)
                for u in range(NU):
                    dst = AO[:, p, u, g * 4 * DK:(g + 1) * 4 * DK].rearrange("p (h e) -> p h e", e=DK)
                    ins = nc.vector.tensor_tensor(dst, o[:, 4 * u:4 * u + 4, 0:DK],
                                                  rec[:, u, :].unsqueeze(2).broadcast_to([P, 4, DK]), ALU.mult)
                ins.then_inc(head_norm, 1)

            def first():
                dve.sem_inc(max_done, 2)
                dve.sem_inc(head_norm, QUADS)
                dve.sem_inc(ot_turned, 2)
                dve.sem_inc(pv_done, 4)
                for p in range(2):
                    dve.sem_inc(ao_stored[p], 16)
                nc.vector.memset(V[:, :, :, :], 1.0)
                nc.vector.memset(QS[ROW_KEY:ROWS_ALL, :, :, :], 1.0 if rope else 0.0)
                nc.vector.memset(KS[ROW_KEY:ROWS_ALL, :, :, :], 1.0).then_inc(ready0, 1)
                dve.wait_ge(w_loaded, 16 * N_W)
                queries(0)
                value_rows(0, 0, 0)
                for h in range(H):
                    maxima(0, h)
                minus_maxima(0)

            def body(n, p, k, project_next, load):
                max_columns(n)
                if project_next:
                    queries(n + 1)
                    value_rows(n + 1, 1 - p, k + p)
                for h in range(6, H):
                    if h in (6, 10, 14):
                        normalise(n, p, k, (h - 6) // 4)
                    if project_next and h < 14:
                        maxima(n + 1, 2 * (h - 6))
                        maxima(n + 1, 2 * (h - 6) + 1)
                        if h == 13:
                            minus_maxima(n + 1)
                normalise(n, p, k, QUADS - 1)

            steps(dve, body, first)


def by_sequence(eng, first, body):
    first()
    with eng.Fori(0, B // 2 - 1) as j:
        body(2 * j, 0, j, True, True)
        body(2 * j + 1, 1, j, True, True)
    body(B - 2, 0, B // 2 - 1, True, False)
    body(B - 1, 1, B // 2 - 1, False, False)


def token_block(nc, tag, c, X, Y, AO, w, affine, gate, ffn):
    with ExitStack() as ctx:
        sb = lambda n, s, d=F32: ctx.enter_context(nc.sbuf_tensor(f"{tag}_{n}", s, d))
        sem = ctx.enter_context(stage_semaphores(nc, tag))
        pair = lambda n: [sem(n + "0"), sem(n + "1")]
        bank = lambda n: ctx.enter_context(nc.psum_tensor(f"{tag}_{n}", [P, 512], F32))
        ident = c["ident"]

        ab = sb("ab", [P, 2, NU, D])
        yb = ab if ffn else (sb("yb", [P, 2, NU, D]) if affine else None)
        xb = sb("xb", [P, 2, NU, D]) if gate is not None else None
        aT = sb("aT", [P, 2, NC, SEQ])
        if ffn:
            w1, w2 = sb("w1", [P, NC, FF]), sb("w2", [P, NF, D])
            b1 = sb("b1", [P, NF])
            hT = sb("hT", [P, 2, NF, SEQ])
            bankH = [bank(f"H{j}") for j in range(NF // 2)]
        else:
            wo = sb("wo", [P, NC, D])
        bias = sb("bias", [P, D])
        yb_bias = sb("ybb", [P, NU, D])
        z = sb("z", [P, NU, D])
        if affine:
            gain, shift = sb("gain", [P, D]), sb("shift", [P, D])
            zn, zg = sb("zn", [P, NU, D]), sb("zg", [P, NU, D])
            t1 = norm_tiles(lambda n, s: sb("a" + n, s))
        if gate is not None:
            t2 = norm_tiles(lambda n, s: sb("g" + n, s))
            xo = sb("xo", [P, 2, NU, D])
            wb = sb("wb", [P, NU, D])
        ob = sb("ob", [P, 2, NU, D])
        bankT = [bank("T0"), bank("T1")]
        bankZ = [bank("Z0"), bank("Z1")]
        flat = lambda a: a.rearrange("p u d -> p (u d)")
        rows = lambda a: a[:, :].unsqueeze(1).broadcast_to([P, NU, D])

        w_loaded = sem("w_loaded")
        a_loaded, y_loaded, x_loaded = pair("a_loaded"), pair("y_loaded"), pair("x_loaded")
        y_stored, x_stored = pair("y_stored"), pair("x_stored")
        waited, waited_dve = sem("waited"), sem("waited_dve")
        turned, t_out, h_ready, h_out = sem("turned"), sem("t_out"), sem("h_ready"), sem("h_out")
        z_ready, z_done, ybb_done, bias_added = sem("z_ready"), sem("z_done"), sem("ybb_done"), sem("bias_added")
        step1, root1, normed1, gained, shifted = sem("step1"), sem("root1"), sem("normed1"), sem("gained"), sem("shifted")
        step2, root2, x_new, finished = sem("step2"), sem("root2"), sem("x_new"), sem("finished")
        n_w = 16 * (4 if ffn else 2) + 16 * 2 * affine

        block = ctx.enter_context(nc.Block())

        @block.sync
        def _(sp):
            def wait(semaphore, value):
                sp.wait_ge(semaphore, value)
                if not isinstance(value, int):
                    sp.sem_inc(waited, 1)

            def load(n, p):
                sp.dma_start(ab[:, p, :, :], sequence_rows(Y if ffn else AO, n)).then_inc(a_loaded[p], 16)
                if affine and not ffn:
                    sp.dma_start(yb[:, p, :, :], sequence_rows(Y, n)).then_inc(y_loaded[p], 16)
                if gate is not None:
                    sp.dma_start(xb[:, p, :, :], sequence_rows(X, n)).then_inc(x_loaded[p], 16)

            def first():
                if ffn:
                    sp.dma_start(w1[:, :, :], w["w1"].rearrange("(c p) n -> p c n", p=P)).then_inc(w_loaded, 16)
                    sp.dma_start(w2[:, :, :], w["w2"].rearrange("(c p) n -> p c n", p=P)).then_inc(w_loaded, 16)
                    sp.dma_start(b1[:, :], w["b1"].rearrange("(c p) -> p c", p=P), allow_slow_non_contiguous=True).then_inc(w_loaded, 16)
                else:
                    sp.dma_start(wo[:, :, :], w["wo"].rearrange("(c p) n -> p c n", p=P)).then_inc(w_loaded, 16)
                sp.dma_start(bias[:, :], w["b"].partition_broadcast(P)).then_inc(w_loaded, 16)
                if affine:
                    sp.dma_start(gain[:, :], w["g"].partition_broadcast(P)).then_inc(w_loaded, 16)
                    sp.dma_start(shift[:, :], w["beta"].partition_broadcast(P)).then_inc(w_loaded, 16)
                for n in range(2):
                    load(n, n)

            def body(n, p, k, more, more2):
                wait(finished, n + 1)
                sp.dma_start(sequence_rows(Y, n), ob[:, p, :, :]).then_inc(y_stored[p], 16)
                if gate is not None:
                    sp.dma_start(sequence_rows(X, n), xo[:, p, :, :]).then_inc(x_stored[p], 16)
                if more2:
                    load(n + 2, p)

            by_sequence(sp, first, body)
            for p in range(2):
                sp.wait_ge(y_stored[p], 16 + 16 * (B // 2))
                if gate is not None:
                    sp.wait_ge(x_stored[p], 16 + 16 * (B // 2))

        @block.tensor
        def _(pe):
            def turn(n, p, k):
                pe.wait_ge(a_loaded[p], 16 * (k + 1))
                pe.wait_ge(t_out, n + 1)
                for cc in range(NC):
                    for u in range(NU):
                        ins = nc.tensor.transpose(bankT[p][:, cc * SEQ + u * P:cc * SEQ + (u + 1) * P],
                                                  ab[:, p, u, cc * P:(cc + 1) * P], ident[:, :])
                ins.then_inc(turned, 1)

            def project(n, p):
                pe.wait_ge(t_out, n + 3)
                pe.wait_ge(z_done, n + 1)
                for u in range(NU):
                    for kc in range(NC):
                        ins = nc.tensor.matmul(bankZ[p][:, u * D:(u + 1) * D], aT[:, p, kc, u * P:(u + 1) * P],
                                               wo[:, kc, :], start=(kc == 0), stop=(kc == NC - 1))
                ins.then_inc(z_ready, 1)

            def up(n, p):
                pe.wait_ge(t_out, n + 3)
                for j in range(NF // 2):
                    pe.wait_ge(h_out, NF // 2 * n + j + 1)
                    for f in (2 * j, 2 * j + 1):
                        for kc in range(NC):
                            ins = nc.tensor.matmul(bankH[j][:, (f % 2) * SEQ:(f % 2 + 1) * SEQ],
                                                   w1[:, kc, f * P:(f + 1) * P], aT[:, p, kc, :],
                                                   start=(kc == 0), stop=(kc == NC - 1))
                    ins.then_inc(h_ready, 1)

            def down(n, p):
                pe.wait_ge(h_out, NF // 2 * (n + 2))
                pe.wait_ge(z_done, n + 1)
                for u in range(NU):
                    for f in range(NF):
                        ins = nc.tensor.matmul(bankZ[p][:, u * D:(u + 1) * D], hT[:, p, f, u * P:(u + 1) * P],
                                               w2[:, f, :], start=(f == 0), stop=(f == NF - 1))
                ins.then_inc(z_ready, 1)

            def first():
                pe.wait_ge(w_loaded, n_w)
                turn(0, 0, 0)

            def body(n, p, k, more, more2):
                if ffn:
                    up(n, p)
                if more:
                    turn(n + 1, 1 - p, k + p)
                if ffn:
                    down(n, p)
                else:
                    project(n, p)

            by_sequence(pe, first, body)

        @block.scalar
        def _(act):
            def bring(n, p):
                act.wait_ge(turned, n + 1)
                act.wait_ge(z_ready, n + 1)
                nc.scalar.activation(flat(aT[:, p, :, :]), bankT[p][:, :], ACT.Copy).then_inc(t_out, 1)

            def hidden(n, p):
                for j in range(NF // 2):
                    act.wait_ge(h_ready, NF // 2 * n + j + 1)
                    for f in (2 * j, 2 * j + 1):
                        ins = nc.scalar.activation(hT[:, p, f, :], bankH[j][:, (f % 2) * SEQ:(f % 2 + 1) * SEQ],
                                                   ACT.Relu, bias=b1[:, f:f + 1])
                    ins.then_inc(h_out, 1)

            def first():
                act.sem_inc(t_out, 2)
                act.sem_inc(z_ready, 2)
                if ffn:
                    act.sem_inc(h_out, NF // 2)
                    act.wait_ge(w_loaded, n_w)
                bring(0, 0)

            def body(n, p, k, more, more2):
                if ffn:
                    hidden(n, p)
                if more:
                    bring(n + 1, 1 - p)
                if affine:
                    norm_root(nc, act, t1, step1, root1, n)
                if gate is not None:
                    norm_root(nc, act, t2, step2, root2, n)

            by_sequence(act, first, body)

        @block.gpsimd
        def _(pool):
            def first():
                pool.wait_ge(w_loaded, n_w)

            def body(n, p, k, more, more2):
                pool.wait_ge((a_loaded if ffn else y_loaded)[p], 16 * (k + 1))
                pool.wait_ge(z_done, n + 2)
                nc.gpsimd.tensor_tensor(yb_bias[:, :, :], yb[:, p, :, :], rows(bias), ALU.add).then_inc(ybb_done, 1)
                pool.wait_ge(normed1, n + 1)
                nc.gpsimd.tensor_tensor(zg[:, :, :], zn[:, :, :], rows(gain), ALU.mult).then_inc(gained, 1)
                pool.wait_ge(gained, n + 1)
                if gate is None:
                    pool.wait_ge(y_stored[p], 16 * (k + 1))
                    nc.gpsimd.tensor_tensor(ob[:, p, :, :], zg[:, :, :], rows(shift), ALU.add).then_inc(finished, 1)
                else:
                    pool.wait_ge(x_new, n + 1)
                    nc.gpsimd.tensor_tensor(wb[:, :, :], zg[:, :, :], rows(shift), ALU.add).then_inc(shifted, 1)

            if affine:
                by_sequence(pool, first, body)

        @block.vector
        def _(dve):
            def first():
                dve.sem_inc(z_done, 2)
                for p in range(2):
                    dve.sem_inc(y_stored[p], 16)
                    if gate is not None:
                        dve.sem_inc(x_stored[p], 16)
                if gate is not None:
                    dve.sem_inc(x_new, 1)
                dve.wait_ge(w_loaded, n_w)

            def body(n, p, k, more, more2):
                zb = bankZ[p][:, :].rearrange("p (u d) -> p u d", u=NU)
                dve.wait_ge(z_ready, n + 3)
                if affine:
                    dve.wait_ge(ybb_done, n + 1)
                    nc.vector.tensor_tensor(z[:, :, :], zb, yb_bias[:, :, :], ALU.add).then_inc(z_done, 1)
                    dve.wait_ge(z_done, n + 3)
                    norm_rows(nc, dve, z, zn, t1, step1, root1, n, waited_dve).then_inc(normed1, 1)
                    w_rows = wb if gate is not None else None
                else:
                    nc.vector.tensor_tensor(z[:, :, :], zb, rows(bias), ALU.add).then_inc(z_done, 1)
                    w_rows = z
                if gate is None:
                    return
                dve.wait_ge(x_loaded[p], 16 * (k + 1))
                dve.wait_ge(x_stored[p], 16 * (k + 1))
                if affine:
                    dve.wait_ge(shifted, n + 1)
                else:
                    dve.wait_ge(z_done, n + 3)
                nc.vector.scalar_tensor_tensor(flat(xo[:, p, :, :]), flat(w_rows[:, :, :]), gate, flat(xb[:, p, :, :]),
                                               ALU.mult, ALU.add).then_inc(x_new, 1)
                dve.wait_ge(x_new, n + 2)
                dve.wait_ge(y_stored[p], 16 * (k + 1))
                norm_rows(nc, dve, xo[:, p], ob[:, p], t2, step2, root2, n, waited_dve).then_inc(finished, 1)

            by_sequence(dve, first, body)


def router(nc, tag, c, Y, wg, bg, L):
    with ExitStack() as ctx:
        sb = lambda n, s, d=F32: ctx.enter_context(nc.sbuf_tensor(f"{tag}_{n}", s, d))
        sem = ctx.enter_context(stage_semaphores(nc, tag))
        pair = lambda n: [sem(n + "0"), sem(n + "1")]
        bank = lambda n: ctx.enter_context(nc.psum_tensor(f"{tag}_{n}", [P, 512], F32))
        yb, yT = sb("yb", [P, 2, NU, D]), sb("yT", [P, 2, NC, SEQ])
        w, b = sb("w", [P, NC, NE]), sb("b", [P, NE])
        lb = sb("lb", [P, 2, NU, NE])
        bankT, bankL = [bank("T0"), bank("T1")], [bank("L0"), bank("L1")]
        w_loaded, loaded, stored = sem("w_loaded"), pair("loaded"), pair("stored")
        turned, t_out, l_ready, l_out, waited = sem("turned"), sem("t_out"), sem("l_ready"), sem("l_out"), sem("waited")
        block = ctx.enter_context(nc.Block())

        @block.sync
        def _(sp):
            def wait(semaphore, value):
                sp.wait_ge(semaphore, value)
                if not isinstance(value, int):
                    sp.sem_inc(waited, 1)

            def load(n, p):
                sp.dma_start(yb[:, p, :, :], sequence_rows(Y, n)).then_inc(loaded[p], 16)

            def first():
                sp.dma_start(w[:, :, :], wg.rearrange("(c p) e -> p c e", p=P)).then_inc(w_loaded, 16)
                sp.dma_start(b[:, :], bg.partition_broadcast(P)).then_inc(w_loaded, 16)
                load(0, 0)
                load(1, 1)

            def body(n, p, k, more, more2):
                if more2:
                    wait(turned, n + 1)
                    load(n + 2, p)
                wait(l_out, n + 3)
                sp.dma_start(sequence_rows(L, n), lb[:, p, :, :]).then_inc(stored[p], 16)

            by_sequence(sp, first, body)
            for p in range(2):
                sp.wait_ge(stored[p], 16 + 16 * (B // 2))

        @block.tensor
        def _(pe):
            def turn(n, p, k):
                pe.wait_ge(loaded[p], 16 * (k + 1))
                pe.wait_ge(t_out, n + 1)
                for cc in range(NC):
                    for u in range(NU):
                        ins = nc.tensor.transpose(bankT[p][:, cc * SEQ + u * P:cc * SEQ + (u + 1) * P],
                                                  yb[:, p, u, cc * P:(cc + 1) * P], c["ident"][:, :])
                ins.then_inc(turned, 1)

            def body(n, p, k, more, more2):
                if more:
                    turn(n + 1, 1 - p, k + p)
                pe.wait_ge(t_out, n + 3)
                pe.wait_ge(l_out, n + 1)
                for u in range(NU):
                    for kc in range(NC):
                        ins = nc.tensor.matmul(bankL[p][:, u * NE:(u + 1) * NE], yT[:, p, kc, u * P:(u + 1) * P],
                                               w[:, kc, :], start=(kc == 0), stop=(kc == NC - 1))
                ins.then_inc(l_ready, 1)

            def first():
                pe.wait_ge(w_loaded, 32)
                turn(0, 0, 0)

            by_sequence(pe, first, body)

        @block.scalar
        def _(act):
            def body(n, p, k, more, more2):
                act.wait_ge(turned, n + 1)
                act.wait_ge(l_ready, n + 1)
                nc.scalar.activation(yT[:, p, :, :].rearrange("p c t -> p (c t)"), bankT[p][:, :], ACT.Copy).then_inc(t_out, 1)

            def first():
                act.sem_inc(t_out, 2)
                act.sem_inc(l_ready, 2)

            by_sequence(act, first, body)

        @block.vector
        def _(dve):
            def body(n, p, k, more, more2):
                dve.wait_ge(l_ready, n + 3)
                dve.wait_ge(stored[p], 16 * (k + 1))
                nc.vector.tensor_tensor(lb[:, p, :, :], bankL[p][:, 0:NU * NE].rearrange("p (u e) -> p u e", u=NU),
                                        b[:, :].unsqueeze(1).broadcast_to([P, NU, NE]), ALU.add).then_inc(l_out, 1)

            def first():
                dve.sem_inc(l_out, 2)
                for p in range(2):
                    dve.sem_inc(stored[p], 16)
                dve.wait_ge(w_loaded, 32)

            by_sequence(dve, first, body)


def bias_parts(nc, tag, b1, b2, parts):
    with ExitStack() as ctx:
        sb = lambda n, s, d=F32: ctx.enter_context(nc.sbuf_tensor(f"{tag}_{n}", s, d))
        bf, r1, r2, q = sb("bf", [NE, FF + D]), sb("r1", [NE, FF + D]), sb("r2", [NE, FF + D]), sb("q", [NE, 3, FF + D], BF16)
        sem = ctx.enter_context(stage_semaphores(nc, tag))
        loaded, step, stored = sem("loaded"), sem("step"), sem("stored")
        block = ctx.enter_context(nc.Block())

        @block.sync
        def _(sp):
            sp.dma_start(bf[:, 0:FF], b1).then_inc(loaded, 16)
            sp.dma_start(bf[:, FF:FF + D], b2).then_inc(loaded, 16)
            sp.wait_ge(step, 5)
            sp.dma_start(parts.rearrange("s e n -> e s n"), q[:, :, :]).then_inc(stored, 16)
            sp.wait_ge(stored, 16)

        @block.vector
        def _(dve):
            dve.wait_ge(loaded, 32)
            nc.vector.tensor_copy(q[:, 0, :], bf[:, :]).then_inc(step, 1)
            dve.wait_ge(step, 1)
            nc.vector.tensor_tensor(r1[:, :], bf[:, :], q[:, 0, :], ALU.subtract).then_inc(step, 1)
            dve.wait_ge(step, 2)
            nc.vector.tensor_copy(q[:, 1, :], r1[:, :]).then_inc(step, 1)
            dve.wait_ge(step, 3)
            nc.vector.tensor_tensor(r2[:, :], r1[:, :], q[:, 1, :], ALU.subtract).then_inc(step, 1)
            dve.wait_ge(step, 4)
            nc.vector.tensor_copy(q[:, 2, :], r2[:, :]).then_inc(step, 1)


def route(nc, tag, c, L, Y, top, slots, xd, dest, weight, slot_expert, gate):
    with ExitStack() as ctx:
        sb = lambda n, s, d=F32: ctx.enter_context(nc.sbuf_tensor(f"{tag}_{n}", s, d))
        sem = ctx.enter_context(stage_semaphores(nc, tag))
        full = [P, NT, NE]
        left, eq, rev, expd = sb("left", full), sb("eq", full), sb("rev", full), sb("expd", full)
        hot = [sb(f"hot{i}", full) for i in range(top)]
        m = [sb(f"m{i}", [P, NT]) for i in range(top)]
        rm, total, inv = sb("rm", [P, NT]), sb("total", [P, NT]), sb("inv", [P, NT])
        prob = [sb(f"prob{i}", [P, NT]) for i in range(top)]
        psum_, pinv = sb("psum", [P, NT]), sb("pinv", [P, NT])
        padded = sb("padded", [P, 2 * NT * NE], BF16)
        chosen = padded[:, NT * NE:2 * NT * NE]
        pos = sb("pos", full)
        count_i, tiles_i = sb("count_i", [P, NE], I32), sb("tiles_i", [P, NE], I32)
        tiles, last, start, zero8 = sb("tiles", [P, NE]), sb("last", [P, NE]), sb("start", [P, NE]), sb("zero8", [P, NE])
        destf = [sb(f"destf{i}", [P, NT]) for i in range(top)]
        slot_no, passed, slot_f = sb("slot_no", [1, slots]), sb("passed", [1, slots, NE]), sb("slot_f", [1, slots])
        rank = ctx.enter_context(nc.psum_tensor(f"{tag}_rank", [P, 512], F32))
        count = ctx.enter_context(nc.psum_tensor(f"{tag}_count", [P, 512], F32))
        ranked, step, exp_done, scattered, iota_done = sem("ranked"), sem("step"), sem("exp_done"), sem("scattered"), sem("iota_done")
        block = ctx.enter_context(nc.Block())
        per_expert = lambda a: a[:, :].unsqueeze(2).broadcast_to(full)

        marks = {}

        @block.vector
        def _(dve):
            n = [0]

            def then(ins):
                n[0] += 1
                ins.then_inc(step, 1)
                dve.wait_ge(step, n[0])

            for e in range(NE):
                ins = nc.vector.memset(rev[:, :, e:e + 1], float(NE - e))
            nc.vector.memset(padded[:, 0:NT * NE], 0.0)
            then(nc.vector.memset(zero8[:, :], 0.0))
            for i in range(top):
                lg = L if i == 0 else left
                then(nc.vector.tensor_reduce(m[i][:, :], lg[:, :, :], AXX, ALU.max))
                then(nc.vector.tensor_tensor(eq[:, :, :], lg[:, :, :], per_expert(m[i]), ALU.is_equal))
                then(nc.vector.tensor_tensor(hot[i][:, :, :], eq[:, :, :], rev[:, :, :], ALU.mult))
                then(nc.vector.tensor_reduce(rm[:, :], hot[i][:, :, :], AXX, ALU.max))
                then(nc.vector.tensor_tensor(hot[i][:, :, :], rev[:, :, :], per_expert(rm), ALU.is_equal))
                if i + 1 < top:
                    then(nc.vector.scalar_tensor_tensor(left[:, :, :], hot[i][:, :, :], OFF, lg[:, :, :], ALU.mult, ALU.add))
            if top == 2:
                then(nc.vector.tensor_tensor(chosen[:, :].rearrange("p (t e) -> p t e", e=NE), hot[0][:, :, :], hot[1][:, :, :], ALU.add))
            else:
                then(nc.vector.tensor_copy(chosen[:, :].rearrange("p (t e) -> p t e", e=NE), hot[0][:, :, :]))
            marks["chosen"] = n[0]
            then(nc.vector.tensor_tensor(eq[:, :, :], L[:, :, :], per_expert(m[0]), ALU.subtract))
            marks["centred"] = n[0]

            dve.wait_ge(ranked, 1)
            then(nc.vector.tensor_scalar(count_i[:, :], count[:, 0:NE], float(P - 1), None, ALU.add))
            then(nc.vector.tensor_scalar(tiles_i[:, :], count_i[:, :], 7, None, ALU.arith_shift_right))
            then(nc.vector.tensor_copy(tiles[:, :], tiles_i[:, :]))
            then(nc.vector.tensor_tensor_scan(last[:, :], tiles[:, :], zero8[:, :], 0.0, ALU.add, ALU.add))
            then(nc.vector.tensor_tensor(start[:, :], last[:, :], tiles[:, :], ALU.subtract))
            then(nc.vector.scalar_tensor_tensor(pos[:, :, :], start[:, :].unsqueeze(1).broadcast_to(full), float(P),
                                                rank[:, 0:NT * NE].rearrange("p (t e) -> p t e", e=NE), ALU.mult, ALU.add))
            for i in range(top):
                then(nc.vector.tensor_tensor(left[:, :, :], hot[i][:, :, :], pos[:, :, :], ALU.mult))
                then(nc.vector.tensor_reduce(destf[i][:, :], left[:, :, :], AXX, ALU.add))
                then(nc.vector.tensor_copy(dest[i][:, :], destf[i][:, :]))
            marks["dest"] = n[0]
            dve.wait_ge(iota_done, 1)
            then(nc.vector.tensor_tensor(passed[:, :, :], last[0:1, :].unsqueeze(1).broadcast_to([1, slots, NE]),
                                         slot_no[:, :].unsqueeze(2).broadcast_to([1, slots, NE]), ALU.is_le))
            then(nc.vector.tensor_reduce(slot_f[:, :], passed[:, :, :], AXX, ALU.add))
            then(nc.vector.tensor_scalar(slot_expert[:, 0:slots], slot_f[:, :], float(NE - 1), None, ALU.min))

            dve.wait_ge(exp_done, 1)
            then(nc.vector.tensor_reduce(total[:, :], expd[:, :, :], AXX, ALU.add))
            then(nc.vector.reciprocal(inv[:, :], total[:, :]))
            for i in range(top):
                then(nc.vector.tensor_tensor(left[:, :, :], hot[i][:, :, :], expd[:, :, :], ALU.mult))
                then(nc.vector.tensor_reduce(m[i][:, :], left[:, :, :], AXX, ALU.add))
                then(nc.vector.tensor_tensor(prob[i][:, :], m[i][:, :], inv[:, :], ALU.mult))
            if top == 2:
                then(nc.vector.tensor_tensor(psum_[:, :], prob[0][:, :], prob[1][:, :], ALU.add))
                then(nc.vector.reciprocal(pinv[:, :], psum_[:, :]))
                for i in range(top):
                    then(nc.vector.tensor_tensor(prob[i][:, :], prob[i][:, :], pinv[:, :], ALU.mult))
            for i in range(top):
                then(nc.vector.tensor_scalar(weight[i][:, :], prob[i][:, :], gate, None, ALU.mult))

        @block.scalar
        def _(act):
            act.wait_ge(step, marks["centred"])
            nc.scalar.activation(expd[:, :, :], eq[:, :, :], ACT.Exp).then_inc(exp_done, 1)

        @block.tensor
        def _(pe):
            pe.wait_ge(step, marks["chosen"])
            nc.tensor.matmul(rank[:, 0:NT * NE], c["before"][:, :], chosen[:, :], start=True, stop=False)
            for j in range(1, NT):
                nc.tensor.matmul(rank[:, 0:NT * NE], c["ones"][:, :], padded[:, (NT - j) * NE:(2 * NT - j) * NE],
                                 start=False, stop=(j == NT - 1))
            for j in range(NT):
                ins = nc.tensor.matmul(count[:, 0:NE], c["ones"][:, :], chosen[:, j * NE:(j + 1) * NE],
                                       start=(j == 0), stop=(j == NT - 1))
            ins.then_inc(ranked, 1)

        @block.gpsimd
        def _(pool):
            pool.iota(slot_no[:, :], pattern=[[1, slots]], base=0, channel_multiplier=0,
                      allow_small_or_imprecise_dtypes=True).then_inc(iota_done, 1)
            pool.wait_ge(step, marks["dest"])
            for t in range(NT):
                for i in range(top):
                    pool.indirect_dma_start(out=xd, out_offset=bass.IndirectOffsetOnAxis(ap=dest[i][:, t:t + 1], axis=0),
                                            in_=Y[:, t, :], in_offset=None).then_inc(scattered, 16)
            pool.wait_ge(scattered, 16 * NT * top)


def experts(nc, tag, c, slots, xd, yd, slot_expert, w1_in, w2_in, parts):
    with ExitStack() as ctx:
        sb = lambda n, s, d=F32: ctx.enter_context(nc.sbuf_tensor(f"{tag}_{n}", s, d))
        sem = ctx.enter_context(stage_semaphores(nc, tag))
        pair = lambda n: [sem(n + "0"), sem(n + "1")]
        bank = lambda n, w=512: ctx.enter_context(nc.psum_tensor(f"{tag}_{n}", [P, w], F32))
        W1 = sb("W1", [P, NE, NC, FF])
        W2 = sb("W2", [P, NE, NF, D])
        bp = sb("bp", [3, NE * (FF + D)], BF16)
        xs, xT, hs, hT, ys = sb("xs", [P, 2, D]), sb("xT", [P, 2, D]), sb("hs", [P, FF]), sb("hT", [P, FF]), sb("ys", [P, 2, D])
        bankX, bankY = bank("X"), bank("Y")
        bankH, bankHT = bank("H", FF), bank("HT", FF)
        b_loaded, e_loaded, w_ready = sem("b_loaded"), [sem(f"e_loaded{e}") for e in range(NE)], sem("w_ready")
        x_loaded, y_stored, waited = pair("x_loaded"), pair("y_stored"), sem("waited")
        x_turned, x_out, h_ready, h_out = sem("x_turned"), sem("x_out"), sem("h_ready"), sem("h_out")
        h_turned, ht_out, y_ready, y_out = sem("h_turned"), sem("ht_out"), sem("y_ready"), sem("y_out")
        block = ctx.enter_context(nc.Block())
        ident = c["ident"]
        odd = slots % 2
        assert odd

        def by_slot(eng, first, body, lastly):
            first()
            with eng.Fori(0, (slots - 3) // 2) as j:
                body(2 * j + 1, 1, j, True)
                body(2 * j + 2, 0, j + 1, True)
            body(slots - 2, 1, (slots - 3) // 2, True)
            body(slots - 1, 0, (slots - 1) // 2, False)
            lastly()

        @block.sync
        def _(sp):
            def wait(semaphore, value):
                sp.wait_ge(semaphore, value)
                if not isinstance(value, int):
                    sp.sem_inc(waited, 1)

            def load(s, p):
                sp.dma_start(xs[:, p, :], xd[bass.ds(s * P, P), :]).then_inc(x_loaded[p], 16)

            def store(s, p):
                sp.dma_start(yd[bass.ds(s * P, P), :], ys[:, p, :]).then_inc(y_stored[p], 16)

            load(0, 0)
            load(1, 1)

            def first():
                sp.wait_ge(x_turned, 1)
                load(2, 0)

            def body(s, p, k, more):
                wait(y_out, s + 1)
                store(s - 1, 1 - p)
                if more and not (isinstance(s, int) and s + 2 >= slots):
                    wait(x_turned, s + 1)
                    load(s + 2, p)

            def lastly():
                sp.wait_ge(y_out, slots + 1)
                store(slots - 1, 0)

            by_slot(sp, first, body, lastly)
            sp.wait_ge(y_stored[0], 16 + 16 * ((slots + 1) // 2))
            sp.wait_ge(y_stored[1], 16 + 16 * (slots // 2))

        @block.gpsimd
        def _(pool):
            pool.dma_start(bp[:, :], parts.rearrange("s e n -> s (e n)")).then_inc(b_loaded, 16)
            for e in range(NE):
                pool.dma_start(W1[:, e, :, :], w1_in[e].rearrange("(c p) n -> p c n", p=P)).then_inc(e_loaded[e], 16)
                pool.dma_start(W2[:, e, :, :], w2_in[e].rearrange("(c p) n -> p c n", p=P)).then_inc(e_loaded[e], 16)
            for e in range(NE):
                pool.wait_ge(e_loaded[e], 32)
                pool.sem_inc(w_ready, 1)

        @block.tensor
        def _(pe):
            def turn_x(s, p, k):
                pe.wait_ge(x_loaded[p], 16 * (k + 1))
                pe.wait_ge(x_out, s + 1)
                for cc in range(NC):
                    ins = nc.tensor.transpose(bankX[:, cc * P:(cc + 1) * P], xs[:, p, cc * P:(cc + 1) * P], ident[:, :])
                ins.then_inc(x_turned, 1)

            def expert_of(s):
                return nc.tensor.value_load(slot_expert[0:1, bass.ds(s, 1)], min_val=0, max_val=NE - 1)

            def up(s, p, e):
                pe.wait_ge(w_ready, e + 1)
                pe.wait_ge(x_out, s + 2)
                pe.wait_ge(h_out, s + 1)
                w1e = W1[:, bass.ds(e, 1), :, :].rearrange("p o c n -> p (o c) n")
                for half in range(2):
                    cols = slice(half * 512, (half + 1) * 512)
                    nc.tensor.matmul(bankH[:, cols], c["ones"][0:3, :], bp[:, bass.ds(e * (FF + D) + half * 512, 512)],
                                     start=True, stop=False)
                    for cc in range(NC):
                        ins = nc.tensor.matmul(bankH[:, cols], xT[:, p, cc * P:(cc + 1) * P], w1e[:, cc, cols],
                                               start=False, stop=(cc == NC - 1))
                ins.then_inc(h_ready, 1)

            def turn_h(s):
                pe.wait_ge(h_out, s + 2)
                pe.wait_ge(ht_out, s + 1)
                for f in range(NF):
                    ins = nc.tensor.transpose(bankHT[:, f * P:(f + 1) * P], hs[:, f * P:(f + 1) * P], ident[:, :])
                ins.then_inc(h_turned, 1)

            def down(s, e):
                pe.wait_ge(ht_out, s + 2)
                pe.wait_ge(y_out, s + 1)
                w2e = W2[:, bass.ds(e, 1), :, :].rearrange("p o c n -> p (o c) n")
                nc.tensor.matmul(bankY[:, 0:D], c["ones"][0:3, :], bp[:, bass.ds(e * (FF + D) + FF, D)], start=True, stop=False)
                for f in range(NF):
                    ins = nc.tensor.matmul(bankY[:, 0:D], hT[:, f * P:(f + 1) * P], w2e[:, f, :],
                                           start=False, stop=(f == NF - 1))
                ins.then_inc(y_ready, 1)

            def first():
                pe.wait_ge(b_loaded, 16)
                turn_x(0, 0, 0)
                up(0, 0, expert_of(0))
                turn_x(1, 1, 0)
                turn_h(0)

            def body(s, p, k, more):
                up(s, p, expert_of(s))
                down(s - 1, expert_of(s - 1))
                if more:
                    turn_x(s + 1, 1 - p, k + p)
                turn_h(s)

            by_slot(pe, first, body, lambda: down(slots - 1, expert_of(slots - 1)))

        @block.scalar
        def _(act):
            def bring_x(s, p):
                act.wait_ge(x_turned, s + 1)
                if not (isinstance(s, int) and s < 2):
                    act.wait_ge(h_ready, s - 1)
                nc.scalar.activation(xT[:, p, :], bankX[:, 0:D], ACT.Copy).then_inc(x_out, 1)

            def bring_h(s):
                act.wait_ge(h_turned, s + 2)
                act.wait_ge(y_ready, s + 1)
                nc.scalar.activation(hT[:, :], bankHT[:, :], ACT.Copy).then_inc(ht_out, 1)

            def first():
                act.sem_inc(x_out, 1)
                act.sem_inc(ht_out, 1)
                act.sem_inc(y_ready, 1)
                bring_x(0, 0)
                bring_x(1, 1)
                bring_h(0)

            def body(s, p, k, more):
                if more:
                    bring_x(s + 1, 1 - p)
                bring_h(s)

            by_slot(act, first, body, lambda: None)

        @block.vector
        def _(dve):
            def relu(s):
                dve.wait_ge(h_ready, s + 1)
                dve.wait_ge(h_turned, s + 1)
                nc.vector.tensor_scalar(hs[:, :], bankH[:, :], 0.0, None, ALU.max).then_inc(h_out, 1)

            def out_rows(s, p, k):
                dve.wait_ge(y_ready, s + 2)
                dve.wait_ge(y_stored[p], 16 * (k + 1))
                nc.vector.tensor_copy(ys[:, p, :], bankY[:, 0:D]).then_inc(y_out, 1)

            def first():
                dve.sem_inc(h_out, 1)
                dve.sem_inc(h_turned, 1)
                dve.sem_inc(y_out, 1)
                for p in range(2):
                    dve.sem_inc(y_stored[p], 16)
                relu(0)

            def body(s, p, k, more):
                relu(s)
                out_rows(s - 1, 1 - p, k - 1 + p)

            by_slot(dve, first, body, lambda: out_rows(slots - 1, 0, (slots - 1) // 2))


def combine(nc, tag, X, Y, top, yd, dest, weight, out=None):
    with ExitStack() as ctx:
        sb = lambda n, s, d=F32: ctx.enter_context(nc.sbuf_tensor(f"{tag}_{n}", s, d))
        sem = ctx.enter_context(stage_semaphores(nc, tag))
        RING = 8
        g = sb("g", [P, RING, D])
        t = norm_tiles(sb)
        gathered = [sem(f"gathered{r}") for r in range(RING)]
        added, step, root, waited, stored, normed = sem("added"), sem("step"), sem("root"), sem("waited"), sem("stored"), sem("normed")
        block = ctx.enter_context(nc.Block())

        @block.gpsimd
        def _(pool):
            for q in range(NT * top):
                i, t_ = q // NU % top, q // (NU * top) * NU + q % NU
                if q >= RING:
                    pool.wait_ge(added, q - RING + 1)
                pool.indirect_dma_start(out=g[:, q % RING, :], out_offset=None, in_=yd,
                                        in_offset=bass.IndirectOffsetOnAxis(ap=dest[i][:, t_:t_ + 1], axis=0)
                                        ).then_inc(gathered[q % RING], 16)

        @block.vector
        def _(dve):
            for n in range(B):
                for i in range(top):
                    for u in range(NU):
                        tt = n * NU + u
                        q = (n * top + i) * NU + u
                        dve.wait_ge(gathered[q % RING], 16 * (q // RING + 1))
                        if i:
                            dve.wait_ge(added, q - NU + 1)
                        nc.vector.scalar_tensor_tensor(X[:, tt, :], g[:, q % RING, :], weight[i][:, tt:tt + 1], X[:, tt, :],
                                                       ALU.mult, ALU.add).then_inc(added, 1)
                if out is None:
                    dve.wait_ge(added, (n + 1) * NU * top)
                    norm_rows(nc, dve, X[:, n * NU:(n + 1) * NU, :], Y[:, n * NU:(n + 1) * NU, :], t, step, root, n, waited).then_inc(normed, 1)
                    dve.wait_ge(normed, n + 1)

        @block.scalar
        def _(act):
            if out is None:
                for n in range(B):
                    norm_root(nc, act, t, step, root, n)

        @block.sync
        def _(sp):
            if out is not None:
                for n in range(B):
                    sp.wait_ge(added, (n + 1) * NU * top)
                    sp.dma_start(sequence_rows(out, n), X[:, n * NU:(n + 1) * NU, :]).then_inc(stored, 16)
                sp.wait_ge(stored, 16 * B)


SLOTS0 = (2 * T + (P - 1) * NE) // P
SLOTS1 = (T + (P - 1) * NE) // P


def flamingo(nc, a, out):
    dram = lambda n, s, d=F32: nc.dram_tensor(n, s, d, kind="Internal").ap()
    xd0, yd0 = dram("xd0", (SLOTS0 * P, D)), dram("yd0", (SLOTS0 * P, D))
    xd1, yd1 = dram("xd1", (SLOTS1 * P, D)), dram("yd1", (SLOTS1 * P, D))
    parts0, parts1 = dram("parts0", (3, NE, FF + D), BF16), dram("parts1", (3, NE, FF + D), BF16)
    key_off = dram("key_off", (B, SEQ), BF16)
    ctx_in = a["ctx_1024"]

    with ExitStack() as ctx:
        sb = lambda n, s, d=F32: ctx.enter_context(nc.sbuf_tensor(n, s, d))
        ident, identb = sb("ident", [P, P]), sb("identb", [P, P], BF16)
        before, ones = sb("before", [P, P], BF16), sb("ones", [P, P], BF16)
        gates = sb("gates", [P, 4])
        L = sb("L", [P, NT, NE])
        dest = [sb(f"dest{i}", [P, NT], U32) for i in range(2)]
        weight = [sb(f"weight{i}", [P, NT]) for i in range(2)]
        slot_expert = sb("slot_expert", [1, SLOTS0], I32)
        X, Y = sb("X", [P, NT, D]), sb("Y", [P, NT, D])
        c = {"ident": ident, "identb": identb, "before": before, "ones": ones}
        gate_x0, gate_x1, gate_f0, gate_f1 = (gates[:, i:i + 1] for i in range(4))

        with ExitStack() as s:
            sbs = lambda n, sh, d=F32: s.enter_context(nc.sbuf_tensor(n, sh, d))
            raw, zero, before_f = sbs("raw", [P, 4]), sbs("zero", [P, D]), sbs("before_f", [P, P])
            keys_u, off = sbs("keys_u", [B, SEQ], U8), sbs("off", [B, SEQ], BF16)
            sem = s.enter_context(stage_semaphores(nc, "setup"))
            loaded, done, zeroed, made = sem("loaded"), sem("done"), sem("zeroed"), sem("made")
            block = s.enter_context(nc.Block())

            @block.sync
            def _(sp):
                sp.dma_start(ident[:, :], a["c_ident"]).then_inc(loaded, 16)
                sp.dma_start(before_f[:, :], a["c_before"]).then_inc(loaded, 16)
                sp.dma_start(raw[:, 0:2], a["g_xattn"].partition_broadcast(P)).then_inc(loaded, 16)
                sp.dma_start(raw[:, 2:4], a["g_ffn"].partition_broadcast(P)).then_inc(loaded, 16)
                sp.dma_start(keys_u[:, :], a["mask_BxS2_bf1"]).then_inc(loaded, 16)
                sp.wait_ge(zeroed, 1)
                for xd, slots in ((xd0, SLOTS0), (xd1, SLOTS1)):
                    sp.dma_start(xd.rearrange("(s p) d -> p s d", p=P),
                                 zero[:, :].unsqueeze(1).broadcast_to([P, slots, D])).then_inc(done, 16)
                sp.wait_ge(made, 2)
                sp.dma_start(key_off, off[:, :]).then_inc(done, 16)
                sp.wait_ge(done, 16 * 3)

            @block.vector
            def _(dve):
                nc.vector.memset(zero[:, :], 0.0).then_inc(zeroed, 1)
                dve.wait_ge(loaded, 16 * 5)
                nc.vector.tensor_copy(identb[:, :], ident[:, :])
                nc.vector.tensor_copy(before[:, :], before_f[:, :])
                nc.vector.memset(ones[:, :], 1.0)
                nc.vector.tensor_scalar(off[:, :], keys_u[:, :], 1.0, -OFF, ALU.subtract, ALU.mult).then_inc(made, 1)

            @block.scalar
            def _(act):
                act.wait_ge(loaded, 16 * 5)
                nc.scalar.activation(gates[:, :], raw[:, :], ACT.Tanh).then_inc(made, 1)

        bias_parts(nc, "bp0", a["L0_ffn_b1"], a["L0_ffn_b2"], parts0)
        bias_parts(nc, "bp1", a["L1_ffn_b1"], a["L1_ffn_b2"], parts1)
        first_norm(nc, a["x"], X, Y)

        def xattn_weights(pre):
            return {k: a[pre + k] for k in ("wq", "bq", "wk", "bk", "wv", "bv")}

        with nc.sbuf_tensor("AO0", [P, NT, D], F32) as AO:
            for i, mask in ((1, "mask_1x1xSxS2_ik0"), (2, "mask_1x1xSxS2_if1")):
                pre = f"L0_xattn_m{i}_"
                with nc.sbuf_tensor(f"Bm{i}", [P, NU * SEQ], BF16) as Bm, nc.sbuf_tensor(f"BmT{i}", [P, NU * SEQ], BF16) as BmT, \
                        nc.sbuf_tensor(f"R{i}", [P, SEQ], F32) as R:
                    mask_setup(nc, a[mask], ident, Bm, BmT, R, f"mask{i}")
                    attention(nc, f"att{i}", c, Y, ctx_in if i == 2 else None, xattn_weights(pre), AO, mask=(Bm, BmT, R))
                token_block(nc, f"mid{i}", c, X, Y, AO, {"wo": a[pre + "wo"], "b": a[pre + "bo"], "g": a[f"L0_xattn_ln{i}_g"],
                                                          "beta": a[f"L0_xattn_ln{i}_b"]}, affine=True, gate=None, ffn=False)
        token_block(nc, "ffn", c, X, Y, None, {"w1": a["L0_xattn_ff_w1"], "b1": a["L0_xattn_ff_b1"], "w2": a["L0_xattn_ff_w2"],
                                               "b": a["L0_xattn_ff_b2"], "g": a["L0_xattn_ln3_g"], "beta": a["L0_xattn_ln3_b"]},
                    affine=True, gate=gate_x0, ffn=True)
        router(nc, "router0", c, Y, a["L0_ffn_Wg"], a["L0_ffn_bg"], L)
        route(nc, "route0", c, L, Y, 2, SLOTS0, xd0, dest, weight, slot_expert, gate_f0)
        experts(nc, "exp0", c, SLOTS0, xd0, yd0, slot_expert, a["L0_ffn_W1"], a["L0_ffn_W2"], parts0)
        combine(nc, "comb0", X, Y, 2, yd0, dest, weight)
        with nc.sbuf_tensor("AO1", [P, NT, D], F32) as AO:
            wkv, bkv = a["L1_xattn_Wkv"], a["L1_xattn_bkv"]
            w = {"wq": a["L1_xattn_Wq"], "bq": a["L1_xattn_bq"], "wk": wkv[:, 0:D], "bk": bkv[0:D], "wv": wkv[:, D:2 * D],
                 "bv": bkv[D:2 * D], "wqs": a["c_wq_pairs"], "bqs": a["c_bq_pairs"], "wks": a["c_wk_pairs"], "bks": a["c_bk_pairs"]}
            attention(nc, "att3", c, Y, ctx_in, w, AO, rope={"keys": a["mask_BxS2_bf1"], "key_off": key_off, **{
                k: a["c_" + k] for k in ("cosq", "sinq", "cosk", "sink")}})
            token_block(nc, "out", c, X, Y, AO, {"wo": a["L1_xattn_Wo"], "b": a["L1_xattn_bo"]}, affine=False, gate=gate_x1, ffn=False)
        router(nc, "router1", c, Y, a["L1_ffn_router_W"], a["L1_ffn_router_b"], L)
        route(nc, "route1", c, L, Y, 1, SLOTS1, xd1, dest, weight, slot_expert, gate_f1)
        experts(nc, "exp1", c, SLOTS1, xd1, yd1, slot_expert, a["L1_ffn_W1"], a["L1_ffn_W2"], parts1)
        combine(nc, "comb1", X, Y, 1, yd1, dest, weight, out=out)


def constants():
    import numpy as np
    f = np.float32
    inv = (f(1.0) / f(10000.0) ** (np.arange(0, DK, 2, dtype=f) / f(DK))).astype(f)
    pos = (f(10.0) * (np.arange(SEQ, dtype=f) / f(SEQ))).astype(f)
    angle = (pos[:, None] * inv).astype(f)
    pair = (np.arange(P) % DK) // 2
    cos, sin = np.cos(angle).T[pair].astype(f), np.sin(angle).T[pair].astype(f)
    sign = np.where(np.arange(P) % 2 == 0, f(-1), f(1))[:, None]
    return {"c_ident": np.eye(P, dtype=f), "c_before": np.triu(np.ones((P, P), f), 1),
            "c_cosk": cos, "c_sink": sin * sign, "c_cosq": cos * f(0.125), "c_sinq": sin * sign * f(0.125)}


def kernel(**inputs):
    import numpy as np
    import concourse.bacc as bacc
    from concourse.bass_utils import run_bass_kernel_spmd

    def pairs(w):
        return w.reshape(w.shape[:-1] + (-1, 2))[..., ::-1].reshape(w.shape)

    given = {k: np.asarray(v) for k, v in inputs.items()}
    given["mask_BxS2_bf1"] = given["mask_BxS2_bf1"].view(np.uint8)
    given["c_wq_pairs"], given["c_bq_pairs"] = pairs(given["L1_xattn_Wq"]), pairs(given["L1_xattn_bq"])
    given["c_wk_pairs"] = pairs(np.ascontiguousarray(given["L1_xattn_Wkv"][:, :D]))
    given["c_bk_pairs"] = pairs(given["L1_xattn_bkv"][:D])
    given.update(constants())
    nc = bacc.Bacc("TRN2", target_bir_lowering=False, num_devices=1)
    arrays, aps = {}, {}
    for name, v in given.items():
        v = np.ascontiguousarray(v)
        arrays[f"in_{name}"] = v
        aps[name] = nc.dram_tensor(f"in_{name}", v.shape, mybir.dt.from_np(v.dtype), kind="ExternalInput").ap()
    out = nc.dram_tensor("out_0", (B, SEQ, D), F32, kind="ExternalOutput").ap()
    flamingo(nc, aps, out)
    return run_bass_kernel_spmd(nc, [arrays], core_ids=[0]).results[0]["out_0"]
```

```python
import concourse.bass as bass
from concourse import mybir
from contextlib import ExitStack, contextmanager

F32 = mybir.dt.float32
BF16 = mybir.dt.bfloat16
I32 = mybir.dt.int32
U32 = mybir.dt.uint32
U8 = mybir.dt.uint8
ACT = mybir.ActivationFunctionType
ALU = mybir.AluOpType
AXX = mybir.AxisListType.X

P = 128
B, SEQ, D = 8, 256, 256
H = 16
DK = D // H
NU = SEQ // P
NC = D // P
T = B * SEQ
NT = T // P
FF = 1024
NF = FF // P
NE = 8
EPS = 1e-5
NEG = -1.0e9
LOWEST = -3.0e38
OFF = -1.0e30

STACKS = ((0, (0, 3), (0, 3)), (3 * DK, (0, 2), (1, 3)), (5 * DK, (0, 1), (2, 3)))
ROWS = 6 * DK
ROW_KEY = ROWS
ROW_MAX = ROWS + 1
ROWS_ALL = ROWS + 3
VW = DK + 1
QUADS = H // 4
SCORES_AT = ((), (), (0,), (1, 2), (3,), (4,), (5, 6), (7,), (8,), (9, 10), (11,), (12,), (13, 14), (15,), (), ())


@contextmanager
def stage_semaphores(nc, tag):
    taken = []

    def sem(n):
        taken.append(nc.alloc_semaphore(f"{tag}_{n}"))
        return taken[-1]

    yield sem
    nc.clear_and_free_semaphores(taken)
    nc.all_engine_barrier()


NORM_STEPS = 8


def norm_tiles(sb):
    return {"stats": sb("stats", [P, NU, 6]), "mv": sb("mv", [P, NU, 2]), "ve": sb("ve", [P, NU]), "std": sb("std", [P, NU]),
            "r0": sb("r0", [P, NU]), "r1": sb("r1", [P, NU]), "r2": sb("r2", [P, NU]), "r3": sb("r3", [P, NU]), "rstd": sb("rstd", [P, NU])}


def norm_rows(nc, dve, x, y, t, step, std_done, n, waited):
    base = NORM_STEPS * n

    def after(i, ins):
        ins.then_inc(step, 1)
        dve.wait_ge(step, base + i)

    for u in range(NU):
        ins = nc.vector.bn_stats(t["stats"][:, u, :], x[:, u, :])
    after(1, ins)
    dve.sem_inc(waited, 1)
    for u in range(NU):
        ins = nc.vector.bn_aggr(t["mv"][:, u, :], t["stats"][:, u, :])
    after(2, ins)
    nc.vector.tensor_scalar(t["ve"][:, :], t["mv"][:, :, 1], EPS, None, ALU.add).then_inc(step, 1)
    dve.wait_ge(std_done, n + 1)
    after(4, nc.vector.reciprocal(t["r0"][:, :], t["std"][:, :]))
    after(5, nc.vector.tensor_tensor(t["r1"][:, :], t["r0"][:, :], t["ve"][:, :], ALU.mult))
    after(6, nc.vector.tensor_tensor(t["r2"][:, :], t["r1"][:, :], t["r0"][:, :], ALU.mult))
    after(7, nc.vector.tensor_scalar(t["r3"][:, :], t["r2"][:, :], -0.5, 1.5, ALU.mult, ALU.add))
    after(8, nc.vector.tensor_tensor(t["rstd"][:, :], t["r0"][:, :], t["r3"][:, :], ALU.mult))
    for u in range(NU):
        ins = nc.vector.tensor_scalar(y[:, u, :], x[:, u, :], t["mv"][:, u, 0:1], t["rstd"][:, u:u + 1],
                                      ALU.subtract, ALU.mult)
    return ins


def norm_root(nc, act, t, step, std_done, n):
    act.wait_ge(step, NORM_STEPS * n + 3)
    nc.scalar.activation(t["std"][:, :], t["ve"][:, :], ACT.Sqrt).then_inc(std_done, 1)


def sequence_rows(a, n):
    if len(a.shape) == 3 and a.shape[0] == B:
        return a[n].rearrange("(u p) d -> p u d", p=P)
    return a[:, bass.ds(n * NU, NU), :]


def first_norm(nc, x, X, Y):
    with ExitStack() as ctx:
        sb = lambda n, s, d=F32: ctx.enter_context(nc.sbuf_tensor(f"ln_{n}", s, d))
        sem = ctx.enter_context(stage_semaphores(nc, "ln"))
        yb = sb("yb", [P, 2, NU, D])
        xb = sb("xb", [P, 2, NU, D])
        t = norm_tiles(sb)
        loaded, x_kept, stored = ([sem(f"{n}{p}") for p in range(2)] for n in ("loaded", "x_kept", "stored"))
        step, std_done, normed, waited, waited_sp = sem("step"), sem("std_done"), sem("normed"), sem("waited"), sem("waited_sp")
        block = ctx.enter_context(nc.Block())

        @block.sync
        def _(sp):
            def load(n, p):
                sp.dma_start(xb[:, p, :, :], sequence_rows(x, n)).then_inc(loaded[p], 16)

            load(0, 0)
            load(1, 1)
            with sp.Fori(0, B // 2 - 1) as j:
                for p in range(2):
                    n = 2 * j + p
                    sp.wait_ge(normed, n + 1)
                    sp.sem_inc(waited_sp, 1)
                    sp.dma_start(sequence_rows(Y, n), yb[:, p, :, :]).then_inc(stored[p], 16)
                    sp.dma_start(sequence_rows(X, n), xb[:, p, :, :]).then_inc(x_kept[p], 16)
                    sp.wait_ge(x_kept[p], 16 * (j + 1))
                    sp.sem_inc(waited_sp, 1)
                    load(n + 2, p)
            for p in range(2):
                n = B - 2 + p
                sp.wait_ge(normed, n + 1)
                sp.dma_start(sequence_rows(Y, n), yb[:, p, :, :]).then_inc(stored[p], 16)
                sp.dma_start(sequence_rows(X, n), xb[:, p, :, :]).then_inc(x_kept[p], 16)
            for p in range(2):
                sp.wait_ge(stored[p], 16 * (B // 2))
                sp.wait_ge(x_kept[p], 16 * (B // 2))

        @block.scalar
        def _(act):
            with act.Fori(0, B) as n:
                norm_root(nc, act, t, step, std_done, n)

        @block.vector
        def _(dve):
            def norm(n, p, k):
                dve.wait_ge(loaded[p], 16 * (k + 1))
                norm_rows(nc, dve, xb[:, p], yb[:, p], t, step, std_done, n, waited).then_inc(normed, 1)

            norm(0, 0, 0)
            norm(1, 1, 0)
            with dve.Fori(1, B // 2) as j:
                for p in range(2):
                    dve.wait_ge(stored[p], 16 * j)
                    norm(2 * j + p, p, j)


def mask_setup(nc, mask, ident, Bm, BmT, R, tag):
    with ExitStack() as ctx:
        sb = lambda n, s, d: ctx.enter_context(nc.sbuf_tensor(f"{tag}_{n}", s, d))
        sem = ctx.enter_context(stage_semaphores(nc, tag))
        mi = sb("mi", [P, NU, SEQ], I32)
        keep = sb("keep", [P, NU, SEQ], F32)
        rowkeep = sb("rowkeep", [P, NU], F32)
        bias = sb("bias", [P, NU, SEQ], F32)
        rowtile = sb("rowtile", [P, NU, P], F32)
        pT = [ctx.enter_context(nc.psum_tensor(f"{tag}_pT{k}", [P, 512], F32)) for k in range(2)]
        loaded, step, turned = sem("loaded"), sem("step"), sem("turned")
        block = ctx.enter_context(nc.Block())

        @block.sync
        def _(sp):
            sp.dma_start(mi[:, :, :], mask[0, 0].rearrange("(u p) k -> p u k", p=P)).then_inc(loaded, 16)

        @block.vector
        def _(dve):
            dve.wait_ge(loaded, 16)
            nc.vector.tensor_scalar(keep[:, :, :], mi[:, :, :], 0.0, None, ALU.not_equal).then_inc(step, 1)
            dve.wait_ge(step, 1)
            nc.vector.tensor_reduce(rowkeep[:, :], keep[:, :, :], AXX, ALU.max).then_inc(step, 1)
            dve.wait_ge(step, 2)
            nc.vector.tensor_scalar(bias[:, :, :], keep[:, :, :], 1.0, -NEG, ALU.subtract, ALU.mult).then_inc(step, 1)
            dve.wait_ge(step, 3)
            for u in range(NU):
                nc.vector.tensor_scalar(Bm[:, u * SEQ:(u + 1) * SEQ], bias[:, u, :], rowkeep[:, u:u + 1], None, ALU.mult)
                nc.vector.tensor_scalar(keep[:, u, :], bias[:, u, :], rowkeep[:, u:u + 1], None, ALU.mult)
                ins = nc.vector.tensor_scalar(rowtile[:, u, :], bias[:, u, 0:P], 0.0, rowkeep[:, u:u + 1], ALU.mult, ALU.add)
            ins.then_inc(step, 1)
            dve.wait_ge(turned, 1)
            nc.vector.tensor_copy(BmT[:, :], pT[0][:, :])
            nc.vector.tensor_copy(R[:, :], pT[1][:, 0:SEQ])

        @block.tensor
        def _(pe):
            pe.wait_ge(step, 4)
            for kt in range(NU):
                for u in range(NU):
                    nc.tensor.transpose(pT[0][:, kt * SEQ + u * P:kt * SEQ + (u + 1) * P],
                                        keep[:, u, kt * P:(kt + 1) * P], ident[:, :])
            for u in range(NU):
                ins = nc.tensor.transpose(pT[1][:, u * P:(u + 1) * P], rowtile[:, u, :], ident[:, :])
            ins.then_inc(turned, 1)


def attention(nc, tag, c, src, ctx_in, w, out_ao, mask=None, rope=None):
    cross = ctx_in is not None
    masked = mask is not None
    with ExitStack() as ctx:
        sb = lambda n, s, d=F32: ctx.enter_context(nc.sbuf_tensor(f"{tag}_{n}", s, d))
        sem = ctx.enter_context(stage_semaphores(nc, tag))
        pair = lambda n: [sem(n + "0"), sem(n + "1")]
        bank = lambda n: ctx.enter_context(nc.psum_tensor(f"{tag}_{n}", [P, 512], F32))

        yb = sb("yb", [P, 2, NU, D])
        yT = sb("yT", [P, 2, NC, SEQ])
        cin = sb("cin", [P, 2, NU, D]) if cross else None
        cT = sb("cT", [P, 2, NC, SEQ]) if cross else yT
        wq, wk, wv = sb("wq", [P, NC, D]), sb("wk", [P, NC, D]), sb("wv", [P, NC, D])
        bq, bk, bv = sb("bq", [P, NC]), sb("bk", [P, NC]), sb("bv", [P, D])
        fq, fk = sb("fq", [P, NC * SEQ]), sb("fk", [P, NC * SEQ])
        rq, rk = sb("rq", [P, NC * SEQ]), sb("rk", [P, NC * SEQ])
        pq, pk = sb("pq", [P, 3, NC, SEQ], BF16), sb("pk", [P, 3, NC, SEQ], BF16)
        q_place, k_place = (0, 1, 2), (2, 1, 0)
        QS, KS = sb("QS", [P, 2, H, SEQ], BF16), sb("KS", [P, 2, H, SEQ], BF16)
        V = sb("V", [P, 2, NU, H * VW + 32])
        PT = sb("PT", [P, 4, NU * SEQ])
        OTS = sb("OTS", [P, 2, SEQ])
        rec = sb("rec", [P, NU, 4])
        mx = sb("mx", [P, NU, H])
        MQ = sb("MQ", [P, NU, 2 * H], BF16)
        MT = sb("MT", [2 * H, SEQ], BF16)
        if masked:
            masked_scores = sb("masked_scores", [P, 2, NU, SEQ], BF16)
        if rope:
            wqs, wks = sb("wqs", [P, NC, D]), sb("wks", [P, NC, D])
            bqs, bks = sb("bqs", [P, NC]), sb("bks", [P, NC])
            tq, tk = sb("tq", [P, NC * SEQ]), sb("tk", [P, NC * SEQ])
            mcu, mcf = sb("mcu", [P, 2, NU], U8), sb("mcf", [P, 2, NU])
            cosq, sinq, cosk, sink = (sb(n, [P, NC, SEQ]) for n in ("cosq", "sinq", "cosk", "sink"))
        bankS = [bank("S0"), bank("S1")]
        bankT = [bank("T0"), bank("T1")]
        bankO = [bank("O0"), bank("O1")]
        bankA, bankB = bank("A"), bank("B")
        max_bank = bankS[0][:, 0:P].bitcast(BF16)

        dram = lambda n, s: nc.dram_tensor(f"{tag}_{n}", s, BF16, kind="Internal").ap()
        q_dram, k_dram = dram("q_dram", (2, 3, D, SEQ)), dram("k_dram", (2, 3, D, SEQ))
        m_dram = dram("m_dram", (2, H, SEQ))

        w_loaded, ready0, waited, waited_dve = sem("w_loaded"), sem("ready0"), sem("waited"), sem("waited_dve")
        x_loaded, c_loaded, stacked, max_rows = pair("x_loaded"), pair("c_loaded"), pair("stacked"), pair("max_rows")
        mc_loaded = pair("mc_loaded")
        spread, m_spread = pair("spread"), sem("m_spread")
        t_ready, tc_ready, t_out, tc_out = sem("t_ready"), sem("tc_ready"), sem("t_out"), sem("tc_out")
        q_ready, k_ready, v_ready = sem("q_ready"), sem("k_ready"), sem("v_ready")
        q_out, k_out, v_out = sem("q_out"), sem("k_out"), sem("v_out")
        qr_ready, kr_ready, qr_out, kr_out = sem("qr_ready"), sem("kr_ready"), sem("qr_out"), sem("kr_out")
        f_sum = sem("f_sum")
        part1, part2, part3, rest1 = sem("part1"), sem("part2"), sem("part3"), sem("rest1")
        s_ready, max_done, m_step, mt_ready, mt_out = sem("s_ready"), sem("max_done"), sem("m_step"), sem("mt_ready"), sem("mt_out")
        st_ready, exp_done, pv_done = sem("st_ready"), sem("exp_done"), sem("pv_done")
        ot_out, ot_turned, rec_done, head_norm = sem("ot_out"), sem("ot_turned"), sem("rec_done"), sem("head_norm")
        mc_step = sem("mc_step")
        N_W = 6 + 4 * bool(rope) + 4 * bool(rope)
        N_STACK = 2 * len(STACKS) + bool(rope)
        later = lambda n, first: not (isinstance(n, int) and n < first)

        def steps(eng, body, first):
            first()
            with eng.Fori(0, B // 2 - 1) as j:
                body(2 * j, 0, j, True, True)
                body(2 * j + 1, 1, j, True, True)
            body(B - 2, 0, B // 2 - 1, True, False)
            body(B - 1, 1, B // 2 - 1, False, False)

        block = ctx.enter_context(nc.Block())

        @block.sync
        def _(sp):
            def wait(semaphore, value):
                sp.wait_ge(semaphore, value)
                if not isinstance(value, int):
                    sp.sem_inc(waited, 1)

            def load_rows(n, p):
                if later(n, 2):
                    wait(t_ready, n - 1)
                sp.dma_start(yb[:, p, :, :], sequence_rows(src, n)).then_inc(x_loaded[p], 16)
                if cross:
                    if later(n, 2):
                        wait(tc_ready, n - 1)
                    sp.dma_start(cin[:, p, :, :], sequence_rows(ctx_in, n)).then_inc(c_loaded[p], 16)
                if rope:
                    if later(n, 2):
                        wait(mc_step, 2 * n - 3)
                    sp.dma_start(mcu[:, p, :], rope["keys"][bass.ds(n, 1), :].rearrange("o (u p) -> p (o u)", p=P),
                                 allow_slow_non_contiguous=True).then_inc(mc_loaded[p], 16)

            def spread_parts(n, p, k):
                if later(n, 2):
                    wait(stacked[p], 16 * N_STACK * k)
                for side, (parts, dram) in enumerate(((pq, q_dram), (pk, k_dram))):
                    wait(part3, 2 * n + 1 + side)
                    sp.dma_start(dram[p].rearrange("s (c r) t -> r s c t", r=P), parts[:, :, :, :]).then_inc(spread[side], 16)

            def stack(n, p, k):
                wait(pv_done, H * n + 4 - H if later(n, 1) else 4)
                for side, (dram, dst) in enumerate(((q_dram, QS), (k_dram, KS))):
                    wait(spread[side], 16 * (n + 1))
                    for row, q_run, k_run in STACKS:
                        a, b = (q_run, k_run)[side]
                        sp.dma_start(dst[row:row + (b - a) * DK, p, :, :],
                                     dram[p, a:b].rearrange("s (d h) t -> (s d) h t", d=DK)).then_inc(stacked[p], 16)
                if rope:
                    sp.dma_start(KS[ROW_KEY:ROW_KEY + 1, p, :, :],
                                 rope["key_off"][bass.ds(n, 1), :].unsqueeze(1).broadcast_to([1, H, SEQ])).then_inc(stacked[p], 16)

            def first():
                for n in range(2):
                    load_rows(n, n)
                for a, d in ((wq, w["wq"]), (wk, w["wk"]), (wv, w["wv"])):
                    sp.dma_start(a[:, :, :], d.rearrange("(c p) n -> p c n", p=P)).then_inc(w_loaded, 16)
                for a, d in ((bq, w["bq"]), (bk, w["bk"])):
                    sp.dma_start(a[:, :], d.rearrange("(c p) -> p c", p=P), allow_slow_non_contiguous=True).then_inc(w_loaded, 16)
                sp.dma_start(bv[:, :], w["bv"].partition_broadcast(P)).then_inc(w_loaded, 16)
                if rope:
                    for a, d in ((wqs, w["wqs"]), (wks, w["wks"])):
                        sp.dma_start(a[:, :, :], d.rearrange("(c p) n -> p c n", p=P)).then_inc(w_loaded, 16)
                    for a, d in ((bqs, w["bqs"]), (bks, w["bks"])):
                        sp.dma_start(a[:, :], d.rearrange("(c p) -> p c", p=P), allow_slow_non_contiguous=True).then_inc(w_loaded, 16)
                    for a, d in ((cosq, "cosq"), (sinq, "sinq"), (cosk, "cosk"), (sink, "sink")):
                        sp.dma_start(a[:, :, :], rope[d].rearrange("(c p) t -> p c t", p=P)).then_inc(w_loaded, 16)
                spread_parts(0, 0, 0)
                wait(ready0, 2)
                stack(0, 0, 0)
                spread_parts(1, 1, 0)

            def body(n, p, k, more, more2):
                if more2:
                    load_rows(n + 2, p)
                wait(mt_out, n + 1)
                sp.dma_start(m_dram.rearrange("j h t -> (j h) t"), MT[:, :]).then_inc(m_spread, 16)
                wait(m_spread, 16 * (n + 1))
                sp.dma_start(QS[ROW_MAX:ROW_MAX + 2, p, :, :], m_dram).then_inc(max_rows[p], 16)
                if more:
                    stack(n + 1, 1 - p, k + p)
                if more2:
                    spread_parts(n + 2, p, k + 1)

            steps(sp, body, first)

        @block.tensor
        def _(pe):
            ident = c["ident"]
            identb = c["identb"]
            last_a, last_b = (kr_out, k_out) if rope else (k_out, q_out)

            def turn(n, p, k):
                pe.wait_ge(x_loaded[p], 16 * (k + 1))
                if later(n, 2):
                    pe.wait_ge(exp_done, H * n - 31)
                if later(n, 1):
                    pe.wait_ge(t_out, n)
                for cc in range(NC):
                    for u in range(NU):
                        ins = nc.tensor.transpose(bankT[0][:, cc * SEQ + u * P:cc * SEQ + (u + 1) * P],
                                                  yb[:, p, u, cc * P:(cc + 1) * P], ident[:, :])
                ins.then_inc(t_ready, 1)
                if cross:
                    if later(n, 2):
                        pe.wait_ge(exp_done, H * n - 30)
                    if later(n, 1):
                        pe.wait_ge(tc_out, n)
                    pe.wait_ge(c_loaded[p], 16 * (k + 1))
                    for cc in range(NC):
                        for u in range(NU):
                            ins = nc.tensor.transpose(bankT[1][:, cc * SEQ + u * P:cc * SEQ + (u + 1) * P],
                                                      cin[:, p, u, cc * P:(cc + 1) * P], ident[:, :])
                    ins.then_inc(tc_ready, 1)

            def product(dst, wt, rhs, done):
                for cc in range(NC):
                    for kc in range(NC):
                        ins = nc.tensor.matmul(dst[:, cc * SEQ:(cc + 1) * SEQ], wt[:, kc, cc * P:(cc + 1) * P],
                                               rhs[:, kc, :], start=(kc == 0), stop=(kc == NC - 1))
                ins.then_inc(done, 1)

            def queries_and_keys(n, p):
                pe.wait_ge(t_out, n + 1)
                if later(n, 2):
                    pe.wait_ge(head_norm, QUADS * (n - 1))
                if later(n, 1):
                    pe.wait_ge(last_b, n)
                product(bankB, wq, yT[:, p], q_ready)
                if later(n, 1):
                    pe.wait_ge(v_out, n)
                if cross:
                    pe.wait_ge(tc_out, n + 1)
                if rope:
                    product(bankA, wqs, yT[:, p], qr_ready)
                    pe.wait_ge(q_out, n + 1)
                    product(bankB, wk, cT[:, p], k_ready)
                    pe.wait_ge(qr_out, n + 1)
                    product(bankA, wks, cT[:, p], kr_ready)
                else:
                    product(bankA, wk, cT[:, p], k_ready)

            def project_values(n, p):
                pe.wait_ge(last_a, n + 1)
                if later(n, 1):
                    pe.wait_ge(head_norm, QUADS * n - 1)
                for u in range(NU):
                    for kc in range(NC):
                        ins = nc.tensor.matmul(bankA[:, u * D:(u + 1) * D], cT[:, p, kc, u * P:(u + 1) * P], wv[:, kc, :],
                                               start=(kc == 0), stop=(kc == NC - 1))
                ins.then_inc(v_ready, 1)

            rows = ROW_KEY + 1 if rope else ROWS

            def scores(n, p, k, h):
                if h == 0:
                    pe.wait_ge(stacked[p], 16 * N_STACK * (k + 1))
                    if later(n, 1):
                        pe.wait_ge(mt_out, n)
                pe.wait_ge(max_done, H * n + h + 1)
                for u in range(NU):
                    ins = nc.tensor.matmul(bankS[h % 2][:, u * SEQ:(u + 1) * SEQ], QS[0:rows, p, h, u * P:(u + 1) * P],
                                           KS[0:rows, p, h, :], start=True, stop=True)
                ins.then_inc(s_ready, 1)

            def turn_max(n):
                pe.wait_ge(m_step, 2 * n + 2)
                for u in range(NU):
                    ins = nc.tensor.transpose(max_bank[0:2 * H, u * P:(u + 1) * P], MQ[:, u, :], identb[:, :])
                ins.then_inc(mt_ready, 1)

            def scores_T(n, p, k, h):
                if h == 0:
                    pe.wait_ge(max_rows[p], 16 * (k + 1))
                pe.wait_ge(exp_done, H * n + h + 1)
                bk_ = bankT[h % 2]
                if masked:
                    nc.tensor.matmul(bk_[:, :], identb[:, :], mask[1][:, :], start=True, stop=False)
                for u in range(NU):
                    ins = nc.tensor.matmul(bk_[:, u * SEQ:(u + 1) * SEQ], KS[0:ROWS_ALL, p, h, u * P:(u + 1) * P],
                                           QS[0:ROWS_ALL, p, h, :], start=not masked, stop=(not masked or u == NU - 1))
                ins.then_inc(st_ready, 1)

            def values(n, p, k, h):
                pe.wait_ge(exp_done, H * n + h + 3)
                if h == 0:
                    pe.wait_ge(v_out, n + 1)
                if h % 4 == 0:
                    pe.wait_ge(ot_out, QUADS * n + h // 4 + 1)
                o = bankO[(h // 4) % 2][32 * (h % 4):32 * (h % 4) + 32, 0:SEQ]
                for u in range(NU):
                    ins = nc.tensor.matmul(o, V[:, p, u, h * VW:h * VW + 32], PT[:, h % 4, u * SEQ:(u + 1) * SEQ],
                                           start=(u == 0), stop=(u == NU - 1))
                ins.then_inc(pv_done, 1)

            def turn_out(n, g, more, more2):
                pe.wait_ge(ot_out, QUADS * n + g + 3)
                pe.wait_ge(head_norm, QUADS * (n + 1) + g - 1)
                if g < 2 and more2:
                    pe.wait_ge((last_a, last_b)[g], n + 3)
                elif g == 0 and more:
                    pe.wait_ge(v_out, n + 2)
                bk_ = (bankA, bankB)[g % 2]
                for u in range(NU):
                    ins = nc.tensor.transpose(bk_[:, u * P:(u + 1) * P], OTS[:, g % 2, u * P:(u + 1) * P], ident[:, :])
                ins.then_inc(ot_turned, 1)

            def first():
                turn(0, 0, 0)
                pe.wait_ge(w_loaded, 16 * N_W)
                queries_and_keys(0, 0)
                project_values(0, 0)
                turn(1, 1, 0)
                queries_and_keys(1, 1)
                for h in range(H):
                    scores(0, 0, 0, h)
                turn_max(0)

            def body(n, p, k, more, more2):
                if more2:
                    turn(n + 2, p, k + 1)
                if more:
                    project_values(n + 1, 1 - p)
                if more2:
                    queries_and_keys(n + 2, p)
                for h in range(H):
                    scores_T(n, p, k, h)
                    if h >= 1:
                        values(n, p, k, h - 1)
                    if h in (6, 10, 14):
                        turn_out(n, (h - 6) // 4, more, more2)
                    if more:
                        for h1 in SCORES_AT[h]:
                            scores(n + 1, 1 - p, k + p, h1)
                    if more and h == 15:
                        turn_max(n + 1)
                values(n, p, k, H - 1)
                turn_out(n, QUADS - 1, more, more2)

            steps(pe, body, first)

        @block.scalar
        def _(act):
            def bring(n, p):
                act.wait_ge(t_ready, n + 1)
                if later(n, 2):
                    act.wait_ge(v_ready, n - 1)
                    act.wait_ge((kr_ready if rope else k_ready), n - 1)
                nc.scalar.activation(yT[:, p, :, :].rearrange("p c t -> p (c t)"), bankT[0][:, :], ACT.Copy).then_inc(t_out, 1)
                if cross:
                    act.wait_ge(tc_ready, n + 1)
                    nc.scalar.activation(cT[:, p, :, :].rearrange("p c t -> p (c t)"), bankT[1][:, :], ACT.Copy).then_inc(tc_out, 1)

            def first_part(n, side, f, parts, place):
                if rope:
                    act.wait_ge(f_sum, 2 * n + 1 + side)
                else:
                    act.wait_ge((q_out, k_out)[side], n + 1)
                if later(n, 1):
                    act.wait_ge(spread[side], 16 * n)
                nc.scalar.activation(parts[:, place[0], :, :].rearrange("p c t -> p (c t)"), f[:, :], ACT.Copy).then_inc(part1, 1)

            def second_part(n, side, r, parts, place):
                act.wait_ge(rest1, 2 * n + 1 + side)
                nc.scalar.activation(parts[:, place[1], :, :].rearrange("p c t -> p (c t)"), r[:, :], ACT.Copy).then_inc(part2, 1)

            def keys(n):
                if rope:
                    return
                act.wait_ge(k_ready, n + 1)
                if later(n, 1):
                    act.wait_ge(rest1, 2 * n)
                for cc in range(NC):
                    ins = nc.scalar.activation(fk[:, cc * SEQ:(cc + 1) * SEQ], bankA[:, cc * SEQ:(cc + 1) * SEQ],
                                               ACT.Identity, bias=bk[:, cc:cc + 1])
                ins.then_inc(k_out, 1)

            def exps(n, h):
                act.wait_ge(st_ready, H * n + h + 1)
                act.wait_ge(pv_done, H * n + h + 1)
                nc.scalar.activation(PT[:, h % 4, :], bankT[h % 2][:, :], ACT.Exp).then_inc(exp_done, 1)

            def outputs(n, g):
                act.wait_ge(pv_done, H * n + 4 * g + 8)
                act.wait_ge(ot_turned, QUADS * n + g + 1)
                nc.scalar.activation(OTS[:, g % 2, :], bankO[g % 2][:, 0:SEQ], ACT.Copy).then_inc(ot_out, 1)

            def parts_of(n, p):
                bring(n, p)
                first_part(n, 0, fq, pq, q_place)
                keys(n)
                first_part(n, 1, fk, pk, k_place)

            def first():
                act.sem_inc(exp_done, 2)
                act.sem_inc(ot_out, 2)
                act.wait_ge(w_loaded, 16 * N_W)
                for n in range(2):
                    parts_of(n, n)
                    second_part(n, 0, rq, pq, q_place)
                    second_part(n, 1, rk, pk, k_place)

            def body(n, p, k, more, more2):
                if more2:
                    parts_of(n + 2, p)
                for h in range(H):
                    exps(n, h)
                    if h < 2 and more2:
                        second_part(n + 2, h, (rq, rk)[h], (pq, pk)[h], (q_place, k_place)[h])
                    if h in (5, 9, 13):
                        outputs(n, (h - 5) // 4)
                outputs(n, QUADS - 1)

            steps(act, body, first)

        @block.gpsimd
        def _(pool):
            def split(n):
                if rope:
                    for side, (f, t) in enumerate(((fq, tq), (fk, tk))):
                        pool.wait_ge((qr_out, kr_out)[side], n + 1)
                        nc.gpsimd.tensor_tensor(f[:, :], f[:, :], t[:, :], ALU.add).then_inc(f_sum, 1)
                for side, (f, r, parts, place) in enumerate(((fq, rq, pq, q_place), (fk, rk, pk, k_place))):
                    pool.wait_ge(part1, 2 * n + 1 + side)
                    nc.gpsimd.tensor_tensor(r[:, :], f[:, :], parts[:, place[0], :, :].rearrange("p c t -> p (c t)"),
                                            ALU.subtract).then_inc(rest1, 1)
                for side, (r, parts, place) in enumerate(((rq, pq, q_place), (rk, pk, k_place))):
                    pool.wait_ge(part2, 2 * n + 1 + side)
                    nc.gpsimd.tensor_tensor(parts[:, place[2], :, :].rearrange("p c t -> p (c t)"), r[:, :],
                                            parts[:, place[1], :, :].rearrange("p c t -> p (c t)"), ALU.subtract).then_inc(part3, 1)

            def first():
                nc.gpsimd.memset(V[:, :, :, :], 1.0).then_inc(ready0, 1)
                split(0)
                split(1)

            def body(n, p, k, more, more2):
                if more2:
                    split(n + 2)

            steps(pool, body, first)

        @block.vector
        def _(dve):
            def queries(n):
                dve.wait_ge(q_ready, n + 1)
                if later(n, 1):
                    dve.wait_ge(rest1, 2 * n - 1)
                for cc in range(NC):
                    cols = slice(cc * SEQ, (cc + 1) * SEQ)
                    ins = nc.vector.scalar_tensor_tensor(fq[:, cols], bankB[:, cols], bq[:, cc:cc + 1],
                                                         cosq[:, cc, :] if rope else mask[2][:, :], ALU.add, ALU.mult)
                ins.then_inc(q_out, 1)
                if rope:
                    for src_, b_, tab, dst, rdy, out in ((bankA, bqs, sinq, tq, qr_ready, qr_out),
                                                         (bankB, bk, cosk, fk, k_ready, k_out),
                                                         (bankA, bks, sink, tk, kr_ready, kr_out)):
                        dve.wait_ge(rdy, n + 1)
                        if dst is fk and later(n, 1):
                            dve.wait_ge(rest1, 2 * n)
                        for cc in range(NC):
                            cols = slice(cc * SEQ, (cc + 1) * SEQ)
                            ins = nc.vector.scalar_tensor_tensor(dst[:, cols], src_[:, cols], b_[:, cc:cc + 1],
                                                                 tab[:, cc, :], ALU.add, ALU.mult)
                        ins.then_inc(out, 1)

            def value_rows(n, p, k):
                if rope:
                    dve.wait_ge(mc_loaded[p], 16 * (k + 1))
                    nc.vector.tensor_copy(mcf[:, p, :], mcu[:, p, :]).then_inc(mc_step, 1)
                    dve.wait_ge(mc_step, 2 * n + 1)
                dve.wait_ge(v_ready, n + 1)
                if later(n, 2):
                    dve.wait_ge(pv_done, H * n - 12)
                heads = [V[:, p, u, 0:H * VW].rearrange("p (h e) -> p h e", e=VW) for u in range(NU)]
                for u in range(NU):
                    ins = nc.vector.tensor_tensor(heads[u][:, :, 0:DK], bankA[:, u * D:(u + 1) * D].rearrange("p (h e) -> p h e", e=DK),
                                                  bv[:, :].rearrange("p (h e) -> p h e", e=DK), ALU.add)
                if rope:
                    ins.then_inc(mc_step, 1)
                    dve.wait_ge(mc_step, 2 * n + 2)
                    for u in range(NU):
                        nc.vector.tensor_copy(heads[u][:, :, DK], mcf[:, p, u:u + 1].broadcast_to([P, H]))
                        ins = nc.vector.tensor_scalar(heads[u][:, :, 0:DK], heads[u][:, :, 0:DK], mcf[:, p, u:u + 1],
                                                      None, ALU.mult)
                ins.then_inc(v_out, 1)

            def maxima(n, h):
                dve.wait_ge(s_ready, H * n + h + 1)
                if h == 0 and later(n, 1):
                    dve.wait_ge(m_step, 2 * n)
                if not masked:
                    nc.vector.tensor_reduce(mx[:, :, h:h + 1], bankS[h % 2][:, :].rearrange("p (u k) -> p u k", u=NU),
                                            AXX, ALU.max).then_inc(max_done, 1)
                    return
                dve.wait_ge(max_done, H * n + h + 1)
                dve.sem_inc(waited_dve, 1)
                for u in range(NU):
                    ins = nc.vector.tensor_tensor_reduce(masked_scores[:, h % 2, u, :], bankS[h % 2][:, u * SEQ:(u + 1) * SEQ],
                                                         mask[0][:, u * SEQ:(u + 1) * SEQ], 1.0, LOWEST, ALU.add, ALU.max,
                                                         accum_out=mx[:, u, h:h + 1])
                ins.then_inc(max_done, 1)

            def minus_maxima(n):
                dve.wait_ge(max_done, H * n + H + 2)
                nc.vector.tensor_scalar(MQ[:, :, 0:H], mx[:, :, :], -1.0, None, ALU.mult).then_inc(m_step, 1)
                dve.wait_ge(m_step, 2 * n + 1)
                nc.vector.scalar_tensor_tensor(MQ[:, :, H:2 * H], mx[:, :, :], -1.0, MQ[:, :, 0:H],
                                               ALU.mult, ALU.subtract).then_inc(m_step, 1)

            def max_columns(n):
                dve.wait_ge(mt_ready, n + 1)
                if later(n, 1):
                    dve.wait_ge(m_spread, 16 * n)
                nc.vector.tensor_copy(MT[:, :], max_bank[0:2 * H, 0:SEQ]).then_inc(mt_out, 1)

            def normalise(n, p, k, g):
                dve.wait_ge(ot_turned, QUADS * n + g + 3)
                o = (bankA, bankB)[g % 2][:, 0:NU * P].rearrange("p (g e) -> p g e", e=32)
                dve.wait_ge(head_norm, QUADS * n + g + 4)
                nc.vector.reciprocal(rec[:, :, :].rearrange("p u h -> p (u h)"), o[:, :, DK]).then_inc(rec_done, 1)
                dve.wait_ge(rec_done, QUADS * n + g + 1)
                for u in range(NU):
                    dst = out_ao[:, bass.ds(n * NU + u, 1), g * 4 * DK:(g + 1) * 4 * DK].rearrange("p o (h e) -> p (o h) e", e=DK)
                    ins = nc.vector.tensor_tensor(dst, o[:, 4 * u:4 * u + 4, 0:DK],
                                                  rec[:, u, :].unsqueeze(2).broadcast_to([P, 4, DK]), ALU.mult)
                ins.then_inc(head_norm, 1)

            def first():
                dve.sem_inc(max_done, 2)
                dve.sem_inc(head_norm, QUADS)
                dve.sem_inc(ot_turned, 2)
                dve.sem_inc(pv_done, 4)
                nc.vector.memset(QS[ROW_KEY:ROWS_ALL, :, :, :], 1.0 if rope else 0.0)
                nc.vector.memset(KS[ROW_KEY:ROWS_ALL, :, :, :], 1.0).then_inc(ready0, 1)
                dve.wait_ge(w_loaded, 16 * N_W)
                queries(0)
                dve.wait_ge(ready0, 2)
                value_rows(0, 0, 0)
                queries(1)
                for h in range(H):
                    maxima(0, h)
                minus_maxima(0)
                max_columns(0)

            def body(n, p, k, more, more2):
                if more:
                    value_rows(n + 1, 1 - p, k + p)
                if more2:
                    queries(n + 2)
                for h in range(H):
                    if h in (6, 10, 14):
                        normalise(n, p, k, (h - 6) // 4)
                    if more:
                        for h1 in SCORES_AT[h]:
                            maxima(n + 1, h1)
                        if h == 13:
                            minus_maxima(n + 1)
                    if more and h == 15:
                        max_columns(n + 1)
                normalise(n, p, k, QUADS - 1)

            steps(dve, body, first)


def by_sequence(eng, first, body):
    first()
    with eng.Fori(0, B // 2 - 1) as j:
        body(2 * j, 0, j, True, True)
        body(2 * j + 1, 1, j, True, True)
    body(B - 2, 0, B // 2 - 1, True, False)
    body(B - 1, 1, B // 2 - 1, False, False)


def token_block(nc, tag, c, X, Y, AO, w, affine, gate, ffn):
    with ExitStack() as ctx:
        sb = lambda n, s, d=F32: ctx.enter_context(nc.sbuf_tensor(f"{tag}_{n}", s, d))
        sem = ctx.enter_context(stage_semaphores(nc, tag))
        pair = lambda n: [sem(n + "0"), sem(n + "1")]
        bank = lambda n: ctx.enter_context(nc.psum_tensor(f"{tag}_{n}", [P, 512], F32))
        ident = c["ident"]

        ab = sb("ab", [P, 2, NU, D])
        aT = sb("aT", [P, 2, NC, SEQ])
        if ffn:
            w1, w2 = sb("w1", [P, NC, FF]), sb("w2", [P, NF, D])
            b1 = sb("b1", [P, NF])
            hT = sb("hT", [P, 2, NF, SEQ])
            bankH = [bank(f"H{j}") for j in range(NF // 2)]
        else:
            wo = sb("wo", [P, NC, D])
        bias = sb("bias", [P, D])
        z = sb("z", [P, 2, NU, D])
        if affine:
            yb_bias = sb("ybb", [P, 2, NU, D])
            gain, shift = sb("gain", [P, D]), sb("shift", [P, D])
            zn, zg = sb("zn", [P, 2, NU, D]), sb("zg", [P, 2, NU, D])
            t1 = norm_tiles(lambda n, s: sb("a" + n, s))
        if gate is not None:
            t2 = norm_tiles(lambda n, s: sb("g" + n, s))
            xo = sb("xo", [P, 2, NU, D])
            wb = sb("wb", [P, 2, NU, D])
        bankT = [bank("T0"), bank("T1")]
        bankZ = [bank("Z0"), bank("Z1")]
        flat = lambda a: a.rearrange("p u d -> p (u d)")
        rows = lambda a: a[:, :].unsqueeze(1).broadcast_to([P, NU, D])
        here = lambda a, n: a[:, bass.ds(n * NU, NU), :]

        w_loaded = sem("w_loaded")
        a_loaded, x_stored = pair("a_loaded"), pair("x_stored")
        waited, waited_dve, waited_pool = sem("waited"), sem("waited_dve"), sem("waited_pool")
        turned, t_out, h_ready, h_out = sem("turned"), sem("t_out"), sem("h_ready"), sem("h_out")
        z_ready, z_done, ybb_done = sem("z_ready"), sem("z_done"), sem("ybb_done")
        step1, root1, normed1, gained, shifted = sem("step1"), sem("root1"), sem("normed1"), sem("gained"), sem("shifted")
        step2, root2, x_new, finished = sem("step2"), sem("root2"), sem("x_new"), sem("finished")
        n_w = 16 * (4 if ffn else 2) + 16 * 2 * affine

        block = ctx.enter_context(nc.Block())

        @block.sync
        def _(sp):
            def wait(semaphore, value):
                sp.wait_ge(semaphore, value)
                if not isinstance(value, int):
                    sp.sem_inc(waited, 1)

            def load(n, p):
                sp.dma_start(ab[:, p, :, :], here(Y if ffn else AO, n)).then_inc(a_loaded[p], 16)

            def first():
                for n in range(2):
                    load(n, n)
                if ffn:
                    sp.dma_start(w1[:, :, :], w["w1"].rearrange("(c p) n -> p c n", p=P)).then_inc(w_loaded, 16)
                    sp.dma_start(w2[:, :, :], w["w2"].rearrange("(c p) n -> p c n", p=P)).then_inc(w_loaded, 16)
                    sp.dma_start(b1[:, :], w["b1"].rearrange("(c p) -> p c", p=P), allow_slow_non_contiguous=True).then_inc(w_loaded, 16)
                else:
                    sp.dma_start(wo[:, :, :], w["wo"].rearrange("(c p) n -> p c n", p=P)).then_inc(w_loaded, 16)
                sp.dma_start(bias[:, :], w["b"].partition_broadcast(P)).then_inc(w_loaded, 16)
                if affine:
                    sp.dma_start(gain[:, :], w["g"].partition_broadcast(P)).then_inc(w_loaded, 16)
                    sp.dma_start(shift[:, :], w["beta"].partition_broadcast(P)).then_inc(w_loaded, 16)

            def body(n, p, k, more, more2):
                if more2:
                    wait(turned, n + 1)
                    load(n + 2, p)
                if gate is not None:
                    wait(x_new, n + 1)
                    sp.dma_start(here(X, n), xo[:, p, :, :]).then_inc(x_stored[p], 16)

            by_sequence(sp, first, body)
            if gate is not None:
                for p in range(2):
                    sp.wait_ge(x_stored[p], 16 + 16 * (B // 2))

        @block.tensor
        def _(pe):
            def turn(n, p, k):
                pe.wait_ge(a_loaded[p], 16 * (k + 1))
                pe.wait_ge(t_out, n + 1)
                for cc in range(NC):
                    for u in range(NU):
                        ins = nc.tensor.transpose(bankT[p][:, cc * SEQ + u * P:cc * SEQ + (u + 1) * P],
                                                  ab[:, p, u, cc * P:(cc + 1) * P], ident[:, :])
                ins.then_inc(turned, 1)

            def project(n, p):
                pe.wait_ge(t_out, n + 3)
                pe.wait_ge(z_done, n + 1)
                for u in range(NU):
                    for kc in range(NC):
                        ins = nc.tensor.matmul(bankZ[p][:, u * D:(u + 1) * D], aT[:, p, kc, u * P:(u + 1) * P],
                                               wo[:, kc, :], start=(kc == 0), stop=(kc == NC - 1))
                ins.then_inc(z_ready, 1)

            def up(n, p):
                pe.wait_ge(t_out, n + 3)
                for j in range(NF // 2):
                    pe.wait_ge(h_out, NF // 2 * n + j + 1)
                    for f in (2 * j, 2 * j + 1):
                        for kc in range(NC):
                            ins = nc.tensor.matmul(bankH[j][:, (f % 2) * SEQ:(f % 2 + 1) * SEQ],
                                                   w1[:, kc, f * P:(f + 1) * P], aT[:, p, kc, :],
                                                   start=(kc == 0), stop=(kc == NC - 1))
                    ins.then_inc(h_ready, 1)

            def down(n, p):
                pe.wait_ge(h_out, NF // 2 * (n + 2))
                pe.wait_ge(z_done, n + 1)
                for u in range(NU):
                    for f in range(NF):
                        ins = nc.tensor.matmul(bankZ[p][:, u * D:(u + 1) * D], hT[:, p, f, u * P:(u + 1) * P],
                                               w2[:, f, :], start=(f == 0), stop=(f == NF - 1))
                ins.then_inc(z_ready, 1)

            def first():
                turn(0, 0, 0)
                turn(1, 1, 0)
                pe.wait_ge(w_loaded, n_w)
                if ffn:
                    up(0, 0)

            def body(n, p, k, more, more2):
                if not ffn:
                    project(n, p)
                else:
                    if more:
                        up(n + 1, 1 - p)
                    down(n, p)
                if more2:
                    turn(n + 2, p, k + 1)

            by_sequence(pe, first, body)

        @block.scalar
        def _(act):
            def bring(n, p):
                act.wait_ge(turned, n + 1)
                act.wait_ge(z_ready, n + 1)
                nc.scalar.activation(flat(aT[:, p, :, :]), bankT[p][:, :], ACT.Copy).then_inc(t_out, 1)

            def hidden(n, p):
                act.wait_ge(z_ready, n + 1)
                for j in range(NF // 2):
                    act.wait_ge(h_ready, NF // 2 * n + j + 1)
                    for f in (2 * j, 2 * j + 1):
                        ins = nc.scalar.activation(hT[:, p, f, :], bankH[j][:, (f % 2) * SEQ:(f % 2 + 1) * SEQ],
                                                   ACT.Relu, bias=b1[:, f:f + 1])
                    ins.then_inc(h_out, 1)

            def first():
                act.sem_inc(t_out, 2)
                act.sem_inc(z_ready, 2)
                if ffn:
                    act.sem_inc(h_out, NF // 2)
                bring(0, 0)
                bring(1, 1)
                if ffn:
                    act.wait_ge(w_loaded, n_w)
                    hidden(0, 0)

            def body(n, p, k, more, more2):
                if ffn and more:
                    hidden(n + 1, 1 - p)
                if more2:
                    bring(n + 2, p)
                if affine:
                    norm_root(nc, act, t1, step1, root1, n)
                if gate is not None:
                    norm_root(nc, act, t2, step2, root2, n)

            by_sequence(act, first, body)

        @block.gpsimd
        def _(pool):
            def add_bias(n, p):
                pool.wait_ge(z_done, n + 1)
                pool.sem_inc(waited_pool, 1)
                nc.gpsimd.tensor_tensor(yb_bias[:, p, :, :], here(Y, n), rows(bias), ALU.add).then_inc(ybb_done, 1)

            def first():
                pool.wait_ge(w_loaded, n_w)
                add_bias(0, 0)

            def body(n, p, k, more, more2):
                if more:
                    add_bias(n + 1, 1 - p)
                pool.wait_ge(normed1, n + 1)
                nc.gpsimd.tensor_tensor(zg[:, p, :, :], zn[:, p, :, :], rows(gain), ALU.mult).then_inc(gained, 1)
                pool.wait_ge(gained, n + 3)
                pool.sem_inc(waited_pool, 1)
                if gate is None:
                    nc.gpsimd.tensor_tensor(here(Y, n), zg[:, p, :, :], rows(shift), ALU.add).then_inc(finished, 1)
                else:
                    nc.gpsimd.tensor_tensor(wb[:, p, :, :], zg[:, p, :, :], rows(shift), ALU.add).then_inc(shifted, 1)

            if affine:
                by_sequence(pool, first, body)

        @block.vector
        def _(dve):
            def first():
                dve.sem_inc(z_done, 2)
                dve.sem_inc(gained, 2)
                if gate is not None:
                    for p in range(2):
                        dve.sem_inc(x_stored[p], 16)
                dve.wait_ge(w_loaded, n_w)

            def body(n, p, k, more, more2):
                zb = bankZ[p][:, :].rearrange("p (u d) -> p u d", u=NU)
                dve.wait_ge(z_ready, n + 3)
                if affine:
                    dve.wait_ge(ybb_done, n + 1)
                    nc.vector.tensor_tensor(z[:, p, :, :], zb, yb_bias[:, p, :, :], ALU.add).then_inc(z_done, 1)
                    dve.wait_ge(z_done, n + 3)
                    dve.wait_ge(gained, n + 1)
                    norm_rows(nc, dve, z[:, p], zn[:, p], t1, step1, root1, n, waited_dve).then_inc(normed1, 1)
                    w_rows = wb[:, p, :, :] if gate is not None else None
                else:
                    nc.vector.tensor_tensor(z[:, p, :, :], zb, rows(bias), ALU.add).then_inc(z_done, 1)
                    w_rows = z[:, p, :, :]
                if gate is None:
                    return
                dve.wait_ge(x_stored[p], 16 * (k + 1))
                if affine:
                    dve.wait_ge(shifted, n + 1)
                else:
                    dve.wait_ge(z_done, n + 3)
                nc.vector.scalar_tensor_tensor(xo[:, p, :, :], w_rows, gate, here(X, n), ALU.mult, ALU.add).then_inc(x_new, 1)
                dve.wait_ge(x_new, n + 1)
                norm_rows(nc, dve, xo[:, p], here(Y, n), t2, step2, root2, n, waited_dve).then_inc(finished, 1)

            by_sequence(dve, first, body)


def router(nc, tag, c, Y, wg, bg, L):
    with ExitStack() as ctx:
        sb = lambda n, s, d=F32: ctx.enter_context(nc.sbuf_tensor(f"{tag}_{n}", s, d))
        sem = ctx.enter_context(stage_semaphores(nc, tag))
        pair = lambda n: [sem(n + "0"), sem(n + "1")]
        bank = lambda n: ctx.enter_context(nc.psum_tensor(f"{tag}_{n}", [P, 512], F32))
        yb, yT = sb("yb", [P, 2, NU, D]), sb("yT", [P, 2, NC, SEQ])
        w, b = sb("w", [P, NC, NE]), sb("b", [P, NE])
        lb = sb("lb", [P, 2, NU, NE])
        bankT, bankL = [bank("T0"), bank("T1")], [bank("L0"), bank("L1")]
        w_loaded, loaded, stored = sem("w_loaded"), pair("loaded"), pair("stored")
        turned, t_out, l_ready, l_out, waited = sem("turned"), sem("t_out"), sem("l_ready"), sem("l_out"), sem("waited")
        block = ctx.enter_context(nc.Block())

        @block.sync
        def _(sp):
            def wait(semaphore, value):
                sp.wait_ge(semaphore, value)
                if not isinstance(value, int):
                    sp.sem_inc(waited, 1)

            def load(n, p):
                sp.dma_start(yb[:, p, :, :], sequence_rows(Y, n)).then_inc(loaded[p], 16)

            def first():
                sp.dma_start(w[:, :, :], wg.rearrange("(c p) e -> p c e", p=P)).then_inc(w_loaded, 16)
                sp.dma_start(b[:, :], bg.partition_broadcast(P)).then_inc(w_loaded, 16)
                load(0, 0)
                load(1, 1)

            def body(n, p, k, more, more2):
                if more2:
                    wait(turned, n + 1)
                    load(n + 2, p)
                wait(l_out, n + 3)
                sp.dma_start(sequence_rows(L, n), lb[:, p, :, :]).then_inc(stored[p], 16)

            by_sequence(sp, first, body)
            for p in range(2):
                sp.wait_ge(stored[p], 16 + 16 * (B // 2))

        @block.tensor
        def _(pe):
            def turn(n, p, k):
                pe.wait_ge(loaded[p], 16 * (k + 1))
                pe.wait_ge(t_out, n + 1)
                for cc in range(NC):
                    for u in range(NU):
                        ins = nc.tensor.transpose(bankT[p][:, cc * SEQ + u * P:cc * SEQ + (u + 1) * P],
                                                  yb[:, p, u, cc * P:(cc + 1) * P], c["ident"][:, :])
                ins.then_inc(turned, 1)

            def body(n, p, k, more, more2):
                if more:
                    turn(n + 1, 1 - p, k + p)
                pe.wait_ge(t_out, n + 3)
                pe.wait_ge(l_out, n + 1)
                for u in range(NU):
                    for kc in range(NC):
                        ins = nc.tensor.matmul(bankL[p][:, u * NE:(u + 1) * NE], yT[:, p, kc, u * P:(u + 1) * P],
                                               w[:, kc, :], start=(kc == 0), stop=(kc == NC - 1))
                ins.then_inc(l_ready, 1)

            def first():
                pe.wait_ge(w_loaded, 32)
                turn(0, 0, 0)

            by_sequence(pe, first, body)

        @block.scalar
        def _(act):
            def body(n, p, k, more, more2):
                act.wait_ge(turned, n + 1)
                act.wait_ge(l_ready, n + 1)
                nc.scalar.activation(yT[:, p, :, :].rearrange("p c t -> p (c t)"), bankT[p][:, :], ACT.Copy).then_inc(t_out, 1)

            def first():
                act.sem_inc(t_out, 2)
                act.sem_inc(l_ready, 2)

            by_sequence(act, first, body)

        @block.vector
        def _(dve):
            def body(n, p, k, more, more2):
                dve.wait_ge(l_ready, n + 3)
                dve.wait_ge(stored[p], 16 * (k + 1))
                nc.vector.tensor_tensor(lb[:, p, :, :], bankL[p][:, 0:NU * NE].rearrange("p (u e) -> p u e", u=NU),
                                        b[:, :].unsqueeze(1).broadcast_to([P, NU, NE]), ALU.add).then_inc(l_out, 1)

            def first():
                dve.sem_inc(l_out, 2)
                for p in range(2):
                    dve.sem_inc(stored[p], 16)
                dve.wait_ge(w_loaded, 32)

            by_sequence(dve, first, body)


def bias_parts(nc, tag, b1, b2, parts):
    with ExitStack() as ctx:
        sb = lambda n, s, d=F32: ctx.enter_context(nc.sbuf_tensor(f"{tag}_{n}", s, d))
        bf, r1, r2, q = sb("bf", [NE, FF + D]), sb("r1", [NE, FF + D]), sb("r2", [NE, FF + D]), sb("q", [NE, 3, FF + D], BF16)
        sem = ctx.enter_context(stage_semaphores(nc, tag))
        loaded, step, stored = sem("loaded"), sem("step"), sem("stored")
        block = ctx.enter_context(nc.Block())

        @block.sync
        def _(sp):
            sp.dma_start(bf[:, 0:FF], b1).then_inc(loaded, 16)
            sp.dma_start(bf[:, FF:FF + D], b2).then_inc(loaded, 16)
            sp.wait_ge(step, 5)
            sp.dma_start(parts.rearrange("s e n -> e s n"), q[:, :, :]).then_inc(stored, 16)
            sp.wait_ge(stored, 16)

        @block.vector
        def _(dve):
            dve.wait_ge(loaded, 32)
            nc.vector.tensor_copy(q[:, 0, :], bf[:, :]).then_inc(step, 1)
            dve.wait_ge(step, 1)
            nc.vector.tensor_tensor(r1[:, :], bf[:, :], q[:, 0, :], ALU.subtract).then_inc(step, 1)
            dve.wait_ge(step, 2)
            nc.vector.tensor_copy(q[:, 1, :], r1[:, :]).then_inc(step, 1)
            dve.wait_ge(step, 3)
            nc.vector.tensor_tensor(r2[:, :], r1[:, :], q[:, 1, :], ALU.subtract).then_inc(step, 1)
            dve.wait_ge(step, 4)
            nc.vector.tensor_copy(q[:, 2, :], r2[:, :]).then_inc(step, 1)


def route(nc, tag, c, L, Y, top, slots, xd, dest, weight, slot_expert, gate):
    with ExitStack() as ctx:
        sb = lambda n, s, d=F32: ctx.enter_context(nc.sbuf_tensor(f"{tag}_{n}", s, d))
        sem = ctx.enter_context(stage_semaphores(nc, tag))
        full = [P, NT, NE]
        left, eq, rev, expd = sb("left", full), sb("eq", full), sb("rev", full), sb("expd", full)
        hot = [sb(f"hot{i}", full) for i in range(top)]
        m = [sb(f"m{i}", [P, NT]) for i in range(top)]
        rm, total, inv = sb("rm", [P, NT]), sb("total", [P, NT]), sb("inv", [P, NT])
        prob = [sb(f"prob{i}", [P, NT]) for i in range(top)]
        psum_, pinv = sb("psum", [P, NT]), sb("pinv", [P, NT])
        padded = sb("padded", [P, 2 * NT * NE], BF16)
        chosen = padded[:, NT * NE:2 * NT * NE]
        pos = sb("pos", full)
        count_i, tiles_i = sb("count_i", [P, NE], I32), sb("tiles_i", [P, NE], I32)
        tiles, last, start, zero8 = sb("tiles", [P, NE]), sb("last", [P, NE]), sb("start", [P, NE]), sb("zero8", [P, NE])
        destf = [sb(f"destf{i}", [P, NT]) for i in range(top)]
        slot_no, passed, slot_f = sb("slot_no", [1, slots]), sb("passed", [1, slots, NE]), sb("slot_f", [1, slots])
        rank = ctx.enter_context(nc.psum_tensor(f"{tag}_rank", [P, 512], F32))
        count = ctx.enter_context(nc.psum_tensor(f"{tag}_count", [P, 512], F32))
        ranked, step, exp_done, scattered, iota_done = sem("ranked"), sem("step"), sem("exp_done"), sem("scattered"), sem("iota_done")
        block = ctx.enter_context(nc.Block())
        per_expert = lambda a: a[:, :].unsqueeze(2).broadcast_to(full)

        marks = {}

        @block.vector
        def _(dve):
            n = [0]

            def then(ins):
                n[0] += 1
                ins.then_inc(step, 1)
                dve.wait_ge(step, n[0])

            for e in range(NE):
                ins = nc.vector.memset(rev[:, :, e:e + 1], float(NE - e))
            nc.vector.memset(padded[:, 0:NT * NE], 0.0)
            then(nc.vector.memset(zero8[:, :], 0.0))
            for i in range(top):
                lg = L if i == 0 else left
                then(nc.vector.tensor_reduce(m[i][:, :], lg[:, :, :], AXX, ALU.max))
                then(nc.vector.tensor_tensor(eq[:, :, :], lg[:, :, :], per_expert(m[i]), ALU.is_equal))
                then(nc.vector.tensor_tensor(hot[i][:, :, :], eq[:, :, :], rev[:, :, :], ALU.mult))
                then(nc.vector.tensor_reduce(rm[:, :], hot[i][:, :, :], AXX, ALU.max))
                then(nc.vector.tensor_tensor(hot[i][:, :, :], rev[:, :, :], per_expert(rm), ALU.is_equal))
                if i + 1 < top:
                    then(nc.vector.scalar_tensor_tensor(left[:, :, :], hot[i][:, :, :], OFF, lg[:, :, :], ALU.mult, ALU.add))
            if top == 2:
                then(nc.vector.tensor_tensor(chosen[:, :].rearrange("p (t e) -> p t e", e=NE), hot[0][:, :, :], hot[1][:, :, :], ALU.add))
            else:
                then(nc.vector.tensor_copy(chosen[:, :].rearrange("p (t e) -> p t e", e=NE), hot[0][:, :, :]))
            marks["chosen"] = n[0]
            then(nc.vector.tensor_tensor(eq[:, :, :], L[:, :, :], per_expert(m[0]), ALU.subtract))
            marks["centred"] = n[0]

            dve.wait_ge(ranked, 1)
            then(nc.vector.tensor_scalar(count_i[:, :], count[:, 0:NE], float(P - 1), None, ALU.add))
            then(nc.vector.tensor_scalar(tiles_i[:, :], count_i[:, :], 7, None, ALU.arith_shift_right))
            then(nc.vector.tensor_copy(tiles[:, :], tiles_i[:, :]))
            then(nc.vector.tensor_tensor_scan(last[:, :], tiles[:, :], zero8[:, :], 0.0, ALU.add, ALU.add))
            then(nc.vector.tensor_tensor(start[:, :], last[:, :], tiles[:, :], ALU.subtract))
            then(nc.vector.scalar_tensor_tensor(pos[:, :, :], start[:, :].unsqueeze(1).broadcast_to(full), float(P),
                                                rank[:, 0:NT * NE].rearrange("p (t e) -> p t e", e=NE), ALU.mult, ALU.add))
            for i in range(top):
                then(nc.vector.tensor_tensor(left[:, :, :], hot[i][:, :, :], pos[:, :, :], ALU.mult))
                then(nc.vector.tensor_reduce(destf[i][:, :], left[:, :, :], AXX, ALU.add))
                then(nc.vector.tensor_copy(dest[i][:, :], destf[i][:, :]))
            marks["dest"] = n[0]
            dve.wait_ge(iota_done, 1)
            then(nc.vector.tensor_tensor(passed[:, :, :], last[0:1, :].unsqueeze(1).broadcast_to([1, slots, NE]),
                                         slot_no[:, :].unsqueeze(2).broadcast_to([1, slots, NE]), ALU.is_le))
            then(nc.vector.tensor_reduce(slot_f[:, :], passed[:, :, :], AXX, ALU.add))
            then(nc.vector.tensor_scalar(slot_expert[:, 0:slots], slot_f[:, :], float(NE - 1), None, ALU.min))

            dve.wait_ge(exp_done, 1)
            then(nc.vector.tensor_reduce(total[:, :], expd[:, :, :], AXX, ALU.add))
            then(nc.vector.reciprocal(inv[:, :], total[:, :]))
            for i in range(top):
                then(nc.vector.tensor_tensor(left[:, :, :], hot[i][:, :, :], expd[:, :, :], ALU.mult))
                then(nc.vector.tensor_reduce(m[i][:, :], left[:, :, :], AXX, ALU.add))
                then(nc.vector.tensor_tensor(prob[i][:, :], m[i][:, :], inv[:, :], ALU.mult))
            if top == 2:
                then(nc.vector.tensor_tensor(psum_[:, :], prob[0][:, :], prob[1][:, :], ALU.add))
                then(nc.vector.reciprocal(pinv[:, :], psum_[:, :]))
                for i in range(top):
                    then(nc.vector.tensor_tensor(prob[i][:, :], prob[i][:, :], pinv[:, :], ALU.mult))
            for i in range(top):
                then(nc.vector.tensor_scalar(weight[i][:, :], prob[i][:, :], gate, None, ALU.mult))

        @block.scalar
        def _(act):
            act.wait_ge(step, marks["centred"])
            nc.scalar.activation(expd[:, :, :], eq[:, :, :], ACT.Exp).then_inc(exp_done, 1)

        @block.tensor
        def _(pe):
            pe.wait_ge(step, marks["chosen"])
            nc.tensor.matmul(rank[:, 0:NT * NE], c["before"][:, :], chosen[:, :], start=True, stop=False)
            for j in range(1, NT):
                nc.tensor.matmul(rank[:, 0:NT * NE], c["ones"][:, :], padded[:, (NT - j) * NE:(2 * NT - j) * NE],
                                 start=False, stop=(j == NT - 1))
            for j in range(NT):
                ins = nc.tensor.matmul(count[:, 0:NE], c["ones"][:, :], chosen[:, j * NE:(j + 1) * NE],
                                       start=(j == 0), stop=(j == NT - 1))
            ins.then_inc(ranked, 1)

        @block.gpsimd
        def _(pool):
            pool.iota(slot_no[:, :], pattern=[[1, slots]], base=0, channel_multiplier=0,
                      allow_small_or_imprecise_dtypes=True).then_inc(iota_done, 1)
            pool.wait_ge(step, marks["dest"])
            for t in range(NT):
                for i in range(top):
                    pool.indirect_dma_start(out=xd, out_offset=bass.IndirectOffsetOnAxis(ap=dest[i][:, t:t + 1], axis=0),
                                            in_=Y[:, t, :], in_offset=None).then_inc(scattered, 16)
            pool.wait_ge(scattered, 16 * NT * top)


def experts(nc, tag, c, slots, xd, yd, slot_expert, w1_in, w2_in, parts):
    with ExitStack() as ctx:
        sb = lambda n, s, d=F32: ctx.enter_context(nc.sbuf_tensor(f"{tag}_{n}", s, d))
        sem = ctx.enter_context(stage_semaphores(nc, tag))
        pair = lambda n: [sem(n + "0"), sem(n + "1")]
        bank = lambda n, w=512: ctx.enter_context(nc.psum_tensor(f"{tag}_{n}", [P, w], F32))
        W1 = sb("W1", [P, NE, NC, FF])
        W2 = sb("W2", [P, NE, NF, D])
        bp = sb("bp", [3, NE * (FF + D)], BF16)
        xs, xT, hs, hT, ys = sb("xs", [P, 2, D]), sb("xT", [P, 2, D]), sb("hs", [P, FF]), sb("hT", [P, FF]), sb("ys", [P, 2, D])
        bankX, bankY = bank("X"), bank("Y")
        bankH, bankHT = bank("H", FF), bank("HT", FF)
        b_loaded, e_loaded, w_ready = sem("b_loaded"), [sem(f"e_loaded{e}") for e in range(NE)], sem("w_ready")
        x_loaded, y_stored, waited = pair("x_loaded"), pair("y_stored"), sem("waited")
        x_turned, x_out, h_ready, h_out = sem("x_turned"), sem("x_out"), sem("h_ready"), sem("h_out")
        h_turned, ht_out, y_ready, y_out = sem("h_turned"), sem("ht_out"), sem("y_ready"), sem("y_out")
        block = ctx.enter_context(nc.Block())
        ident = c["ident"]
        odd = slots % 2
        assert odd

        def by_slot(eng, first, body, lastly):
            first()
            with eng.Fori(0, (slots - 3) // 2) as j:
                body(2 * j + 1, 1, j, True)
                body(2 * j + 2, 0, j + 1, True)
            body(slots - 2, 1, (slots - 3) // 2, True)
            body(slots - 1, 0, (slots - 1) // 2, False)
            lastly()

        @block.sync
        def _(sp):
            def wait(semaphore, value):
                sp.wait_ge(semaphore, value)
                if not isinstance(value, int):
                    sp.sem_inc(waited, 1)

            def load(s, p):
                sp.dma_start(xs[:, p, :], xd[bass.ds(s * P, P), :]).then_inc(x_loaded[p], 16)

            def store(s, p):
                sp.dma_start(yd[bass.ds(s * P, P), :], ys[:, p, :]).then_inc(y_stored[p], 16)

            load(0, 0)
            load(1, 1)

            def first():
                sp.wait_ge(x_turned, 1)
                load(2, 0)

            def body(s, p, k, more):
                wait(y_out, s + 1)
                store(s - 1, 1 - p)
                if more and not (isinstance(s, int) and s + 2 >= slots):
                    wait(x_turned, s + 1)
                    load(s + 2, p)

            def lastly():
                sp.wait_ge(y_out, slots + 1)
                store(slots - 1, 0)

            by_slot(sp, first, body, lastly)
            sp.wait_ge(y_stored[0], 16 + 16 * ((slots + 1) // 2))
            sp.wait_ge(y_stored[1], 16 + 16 * (slots // 2))

        @block.gpsimd
        def _(pool):
            pool.dma_start(bp[:, :], parts.rearrange("s e n -> s (e n)")).then_inc(b_loaded, 16)
            for e in range(NE):
                pool.dma_start(W1[:, e, :, :], w1_in[e].rearrange("(c p) n -> p c n", p=P)).then_inc(e_loaded[e], 16)
                pool.dma_start(W2[:, e, :, :], w2_in[e].rearrange("(c p) n -> p c n", p=P)).then_inc(e_loaded[e], 16)
            for e in range(NE):
                pool.wait_ge(e_loaded[e], 32)
                pool.sem_inc(w_ready, 1)

        @block.tensor
        def _(pe):
            def turn_x(s, p, k):
                pe.wait_ge(x_loaded[p], 16 * (k + 1))
                pe.wait_ge(x_out, s + 1)
                for cc in range(NC):
                    ins = nc.tensor.transpose(bankX[:, cc * P:(cc + 1) * P], xs[:, p, cc * P:(cc + 1) * P], ident[:, :])
                ins.then_inc(x_turned, 1)

            def expert_of(s):
                return nc.tensor.value_load(slot_expert[0:1, bass.ds(s, 1)], min_val=0, max_val=NE - 1)

            def up(s, p, e):
                pe.wait_ge(w_ready, e + 1)
                pe.wait_ge(x_out, s + 2)
                pe.wait_ge(h_out, s + 1)
                w1e = W1[:, bass.ds(e, 1), :, :].rearrange("p o c n -> p (o c) n")
                for half in range(2):
                    cols = slice(half * 512, (half + 1) * 512)
                    nc.tensor.matmul(bankH[:, cols], c["ones"][0:3, :], bp[:, bass.ds(e * (FF + D) + half * 512, 512)],
                                     start=True, stop=False)
                    for cc in range(NC):
                        ins = nc.tensor.matmul(bankH[:, cols], xT[:, p, cc * P:(cc + 1) * P], w1e[:, cc, cols],
                                               start=False, stop=(cc == NC - 1))
                ins.then_inc(h_ready, 1)

            def turn_h(s):
                pe.wait_ge(h_out, s + 2)
                pe.wait_ge(ht_out, s + 1)
                for f in range(NF):
                    ins = nc.tensor.transpose(bankHT[:, f * P:(f + 1) * P], hs[:, f * P:(f + 1) * P], ident[:, :])
                ins.then_inc(h_turned, 1)

            def down(s, e):
                pe.wait_ge(ht_out, s + 2)
                pe.wait_ge(y_out, s + 1)
                w2e = W2[:, bass.ds(e, 1), :, :].rearrange("p o c n -> p (o c) n")
                nc.tensor.matmul(bankY[:, 0:D], c["ones"][0:3, :], bp[:, bass.ds(e * (FF + D) + FF, D)], start=True, stop=False)
                for f in range(NF):
                    ins = nc.tensor.matmul(bankY[:, 0:D], hT[:, f * P:(f + 1) * P], w2e[:, f, :],
                                           start=False, stop=(f == NF - 1))
                ins.then_inc(y_ready, 1)

            def first():
                pe.wait_ge(b_loaded, 16)
                turn_x(0, 0, 0)
                up(0, 0, expert_of(0))
                turn_x(1, 1, 0)
                turn_h(0)

            def body(s, p, k, more):
                up(s, p, expert_of(s))
                down(s - 1, expert_of(s - 1))
                if more:
                    turn_x(s + 1, 1 - p, k + p)
                turn_h(s)

            by_slot(pe, first, body, lambda: down(slots - 1, expert_of(slots - 1)))

        @block.scalar
        def _(act):
            def bring_x(s, p):
                act.wait_ge(x_turned, s + 1)
                if not (isinstance(s, int) and s < 2):
                    act.wait_ge(h_ready, s - 1)
                nc.scalar.activation(xT[:, p, :], bankX[:, 0:D], ACT.Copy).then_inc(x_out, 1)

            def bring_h(s):
                act.wait_ge(h_turned, s + 2)
                act.wait_ge(y_ready, s + 1)
                nc.scalar.activation(hT[:, :], bankHT[:, :], ACT.Copy).then_inc(ht_out, 1)

            def first():
                act.sem_inc(x_out, 1)
                act.sem_inc(ht_out, 1)
                act.sem_inc(y_ready, 1)
                bring_x(0, 0)
                bring_x(1, 1)
                bring_h(0)

            def body(s, p, k, more):
                if more:
                    bring_x(s + 1, 1 - p)
                bring_h(s)

            by_slot(act, first, body, lambda: None)

        @block.vector
        def _(dve):
            def relu(s):
                dve.wait_ge(h_ready, s + 1)
                dve.wait_ge(h_turned, s + 1)
                nc.vector.tensor_scalar(hs[:, :], bankH[:, :], 0.0, None, ALU.max).then_inc(h_out, 1)

            def out_rows(s, p, k):
                dve.wait_ge(y_ready, s + 2)
                dve.wait_ge(y_stored[p], 16 * (k + 1))
                nc.vector.tensor_copy(ys[:, p, :], bankY[:, 0:D]).then_inc(y_out, 1)

            def first():
                dve.sem_inc(h_out, 1)
                dve.sem_inc(h_turned, 1)
                dve.sem_inc(y_out, 1)
                for p in range(2):
                    dve.sem_inc(y_stored[p], 16)
                relu(0)

            def body(s, p, k, more):
                relu(s)
                out_rows(s - 1, 1 - p, k - 1 + p)

            by_slot(dve, first, body, lambda: out_rows(slots - 1, 0, (slots - 1) // 2))


def combine(nc, tag, X, Y, top, yd, dest, weight, out=None):
    with ExitStack() as ctx:
        sb = lambda n, s, d=F32: ctx.enter_context(nc.sbuf_tensor(f"{tag}_{n}", s, d))
        sem = ctx.enter_context(stage_semaphores(nc, tag))
        RING = 8
        g = sb("g", [P, RING, D])
        t = norm_tiles(sb)
        gathered = [sem(f"gathered{r}") for r in range(RING)]
        added, step, root, waited, stored, normed = sem("added"), sem("step"), sem("root"), sem("waited"), sem("stored"), sem("normed")
        block = ctx.enter_context(nc.Block())

        @block.gpsimd
        def _(pool):
            for q in range(NT * top):
                i, t_ = q // NU % top, q // (NU * top) * NU + q % NU
                if q >= RING:
                    pool.wait_ge(added, q - RING + 1)
                pool.indirect_dma_start(out=g[:, q % RING, :], out_offset=None, in_=yd,
                                        in_offset=bass.IndirectOffsetOnAxis(ap=dest[i][:, t_:t_ + 1], axis=0)
                                        ).then_inc(gathered[q % RING], 16)

        @block.vector
        def _(dve):
            for n in range(B):
                for i in range(top):
                    for u in range(NU):
                        tt = n * NU + u
                        q = (n * top + i) * NU + u
                        dve.wait_ge(gathered[q % RING], 16 * (q // RING + 1))
                        if i:
                            dve.wait_ge(added, q - NU + 1)
                        nc.vector.scalar_tensor_tensor(X[:, tt, :], g[:, q % RING, :], weight[i][:, tt:tt + 1], X[:, tt, :],
                                                       ALU.mult, ALU.add).then_inc(added, 1)
                if out is None:
                    dve.wait_ge(added, (n + 1) * NU * top)
                    norm_rows(nc, dve, X[:, n * NU:(n + 1) * NU, :], Y[:, n * NU:(n + 1) * NU, :], t, step, root, n, waited).then_inc(normed, 1)
                    dve.wait_ge(normed, n + 1)

        @block.scalar
        def _(act):
            if out is None:
                for n in range(B):
                    norm_root(nc, act, t, step, root, n)

        @block.sync
        def _(sp):
            if out is not None:
                for n in range(B):
                    sp.wait_ge(added, (n + 1) * NU * top)
                    sp.dma_start(sequence_rows(out, n), X[:, n * NU:(n + 1) * NU, :]).then_inc(stored, 16)
                sp.wait_ge(stored, 16 * B)


SLOTS0 = (2 * T + (P - 1) * NE) // P
SLOTS1 = (T + (P - 1) * NE) // P


def flamingo(nc, a, out):
    dram = lambda n, s, d=F32: nc.dram_tensor(n, s, d, kind="Internal").ap()
    xd0, yd0 = dram("xd0", (SLOTS0 * P, D)), dram("yd0", (SLOTS0 * P, D))
    xd1, yd1 = dram("xd1", (SLOTS1 * P, D)), dram("yd1", (SLOTS1 * P, D))
    parts0, parts1 = dram("parts0", (3, NE, FF + D), BF16), dram("parts1", (3, NE, FF + D), BF16)
    key_off = dram("key_off", (B, SEQ), BF16)
    ctx_in = a["ctx_1024"]

    with ExitStack() as ctx:
        sb = lambda n, s, d=F32: ctx.enter_context(nc.sbuf_tensor(n, s, d))
        ident, identb = sb("ident", [P, P]), sb("identb", [P, P], BF16)
        before, ones = sb("before", [P, P], BF16), sb("ones", [P, P], BF16)
        gates = sb("gates", [P, 4])
        L = sb("L", [P, NT, NE])
        dest = [sb(f"dest{i}", [P, NT], U32) for i in range(2)]
        weight = [sb(f"weight{i}", [P, NT]) for i in range(2)]
        slot_expert = sb("slot_expert", [1, SLOTS0], I32)
        X, Y = sb("X", [P, NT, D]), sb("Y", [P, NT, D])
        c = {"ident": ident, "identb": identb, "before": before, "ones": ones}
        gate_x0, gate_x1, gate_f0, gate_f1 = (gates[:, i:i + 1] for i in range(4))

        with ExitStack() as s:
            sbs = lambda n, sh, d=F32: s.enter_context(nc.sbuf_tensor(n, sh, d))
            raw, zero, before_f = sbs("raw", [P, 4]), sbs("zero", [P, D]), sbs("before_f", [P, P])
            keys_u, off = sbs("keys_u", [B, SEQ], U8), sbs("off", [B, SEQ], BF16)
            sem = s.enter_context(stage_semaphores(nc, "setup"))
            loaded, done, zeroed, made = sem("loaded"), sem("done"), sem("zeroed"), sem("made")
            block = s.enter_context(nc.Block())

            @block.sync
            def _(sp):
                sp.dma_start(ident[:, :], a["c_ident"]).then_inc(loaded, 16)
                sp.dma_start(before_f[:, :], a["c_before"]).then_inc(loaded, 16)
                sp.dma_start(raw[:, 0:2], a["g_xattn"].partition_broadcast(P)).then_inc(loaded, 16)
                sp.dma_start(raw[:, 2:4], a["g_ffn"].partition_broadcast(P)).then_inc(loaded, 16)
                sp.dma_start(keys_u[:, :], a["mask_BxS2_bf1"]).then_inc(loaded, 16)
                sp.wait_ge(zeroed, 1)
                for xd, slots in ((xd0, SLOTS0), (xd1, SLOTS1)):
                    sp.dma_start(xd.rearrange("(s p) d -> p s d", p=P),
                                 zero[:, :].unsqueeze(1).broadcast_to([P, slots, D])).then_inc(done, 16)
                sp.wait_ge(made, 2)
                sp.dma_start(key_off, off[:, :]).then_inc(done, 16)
                sp.wait_ge(done, 16 * 3)

            @block.vector
            def _(dve):
                nc.vector.memset(zero[:, :], 0.0).then_inc(zeroed, 1)
                dve.wait_ge(loaded, 16 * 5)
                nc.vector.tensor_copy(identb[:, :], ident[:, :])
                nc.vector.tensor_copy(before[:, :], before_f[:, :])
                nc.vector.memset(ones[:, :], 1.0)
                nc.vector.tensor_scalar(off[:, :], keys_u[:, :], 1.0, -OFF, ALU.subtract, ALU.mult).then_inc(made, 1)

            @block.scalar
            def _(act):
                act.wait_ge(loaded, 16 * 5)
                nc.scalar.activation(gates[:, :], raw[:, :], ACT.Tanh).then_inc(made, 1)

        bias_parts(nc, "bp0", a["L0_ffn_b1"], a["L0_ffn_b2"], parts0)
        bias_parts(nc, "bp1", a["L1_ffn_b1"], a["L1_ffn_b2"], parts1)
        first_norm(nc, a["x"], X, Y)

        def xattn_weights(pre):
            return {"wq": a[f"c_{pre}wq"], "bq": a[f"c_{pre}bq"], "wk": a[f"c_{pre}wk"], "bk": a[f"c_{pre}bk"],
                    "wv": a[pre + "wv"], "bv": a[pre + "bv"]}

        with nc.sbuf_tensor("AO0", [P, NT, D], F32) as AO:
            for i, mask in ((1, "mask_1x1xSxS2_ik0"), (2, "mask_1x1xSxS2_if1")):
                pre = f"L0_xattn_m{i}_"
                with nc.sbuf_tensor(f"Bm{i}", [P, NU * SEQ], BF16) as Bm, nc.sbuf_tensor(f"BmT{i}", [P, NU * SEQ], BF16) as BmT, \
                        nc.sbuf_tensor(f"R{i}", [P, SEQ], F32) as R:
                    mask_setup(nc, a[mask], ident, Bm, BmT, R, f"mask{i}")
                    attention(nc, f"att{i}", c, Y, ctx_in if i == 2 else None, xattn_weights(pre), AO, mask=(Bm, BmT, R))
                token_block(nc, f"mid{i}", c, X, Y, AO, {"wo": a[pre + "wo"], "b": a[pre + "bo"], "g": a[f"L0_xattn_ln{i}_g"],
                                                          "beta": a[f"L0_xattn_ln{i}_b"]}, affine=True, gate=None, ffn=False)
        token_block(nc, "ffn", c, X, Y, None, {"w1": a["L0_xattn_ff_w1"], "b1": a["L0_xattn_ff_b1"], "w2": a["L0_xattn_ff_w2"],
                                               "b": a["L0_xattn_ff_b2"], "g": a["L0_xattn_ln3_g"], "beta": a["L0_xattn_ln3_b"]},
                    affine=True, gate=gate_x0, ffn=True)
        router(nc, "router0", c, Y, a["L0_ffn_Wg"], a["L0_ffn_bg"], L)
        route(nc, "route0", c, L, Y, 2, SLOTS0, xd0, dest, weight, slot_expert, gate_f0)
        experts(nc, "exp0", c, SLOTS0, xd0, yd0, slot_expert, a["L0_ffn_W1"], a["L0_ffn_W2"], parts0)
        combine(nc, "comb0", X, Y, 2, yd0, dest, weight)
        with nc.sbuf_tensor("AO1", [P, NT, D], F32) as AO:
            wkv, bkv = a["L1_xattn_Wkv"], a["L1_xattn_bkv"]
            w = {"wv": wkv[:, D:2 * D], "bv": bkv[D:2 * D], **{k: a["c_L1_" + k] for k in ("wq", "bq", "wk", "bk")},
                 "wqs": a["c_wq_pairs"], "bqs": a["c_bq_pairs"], "wks": a["c_wk_pairs"], "bks": a["c_bk_pairs"]}
            attention(nc, "att3", c, Y, ctx_in, w, AO, rope={"keys": a["mask_BxS2_bf1"], "key_off": key_off, **{
                k: a["c_" + k] for k in ("cosq", "sinq", "cosk", "sink")}})
            token_block(nc, "out", c, X, Y, AO, {"wo": a["L1_xattn_Wo"], "b": a["L1_xattn_bo"]}, affine=False, gate=gate_x1, ffn=False)
        router(nc, "router1", c, Y, a["L1_ffn_router_W"], a["L1_ffn_router_b"], L)
        route(nc, "route1", c, L, Y, 1, SLOTS1, xd1, dest, weight, slot_expert, gate_f1)
        experts(nc, "exp1", c, SLOTS1, xd1, yd1, slot_expert, a["L1_ffn_W1"], a["L1_ffn_W2"], parts1)
        combine(nc, "comb1", X, Y, 1, yd1, dest, weight, out=out)


def constants():
    import numpy as np
    f = np.float32
    inv = (f(1.0) / f(10000.0) ** (np.arange(0, DK, 2, dtype=f) / f(DK))).astype(f)
    pos = (f(10.0) * (np.arange(SEQ, dtype=f) / f(SEQ))).astype(f)
    angle = (pos[:, None] * inv).astype(f)
    feature = np.arange(D) // H
    cos, sin = np.cos(angle).T[feature // 2].astype(f), np.sin(angle).T[feature // 2].astype(f)
    sign = np.where(feature % 2 == 0, f(-1), f(1))[:, None]
    return {"c_ident": np.eye(P, dtype=f), "c_before": np.triu(np.ones((P, P), f), 1),
            "c_cosk": cos, "c_sink": sin * sign, "c_cosq": cos * f(0.125), "c_sinq": sin * sign * f(0.125)}


def kernel(**inputs):
    import numpy as np
    import concourse.bacc as bacc
    from concourse.bass_utils import run_bass_kernel_spmd

    def by_feature(w):
        return np.swapaxes(w.reshape(w.shape[:-1] + (H, DK)), -1, -2).reshape(w.shape)

    def pairs(w):
        return w.reshape(w.shape[:-1] + (-1, 2))[..., ::-1].reshape(w.shape)

    given = {k: np.asarray(v) for k, v in inputs.items()}
    given["mask_BxS2_bf1"] = given["mask_BxS2_bf1"].view(np.uint8)
    for pre in ("L0_xattn_m1_", "L0_xattn_m2_"):
        for k in ("wq", "bq", "wk", "bk"):
            given[f"c_{pre}{k}"] = by_feature(given.pop(pre + k))
    wkv, bkv = given["L1_xattn_Wkv"], given["L1_xattn_bkv"]
    for k, v in (("q", given.pop("L1_xattn_Wq")), ("k", np.ascontiguousarray(wkv[:, :D]))):
        given[f"c_L1_w{k}"], given[f"c_w{k}_pairs"] = by_feature(v), by_feature(pairs(v))
    for k, v in (("q", given.pop("L1_xattn_bq")), ("k", bkv[:D])):
        given[f"c_L1_b{k}"], given[f"c_b{k}_pairs"] = by_feature(v), by_feature(pairs(v))
    given.update(constants())
    nc = bacc.Bacc("TRN2", target_bir_lowering=False, num_devices=1)
    arrays, aps = {}, {}
    for name, v in given.items():
        v = np.ascontiguousarray(v)
        arrays[f"in_{name}"] = v
        aps[name] = nc.dram_tensor(f"in_{name}", v.shape, mybir.dt.from_np(v.dtype), kind="ExternalInput").ap()
    out = nc.dram_tensor("out_0", (B, SEQ, D), F32, kind="ExternalOutput").ap()
    flamingo(nc, aps, out)
    return run_bass_kernel_spmd(nc, [arrays], core_ids=[0]).results[0]["out_0"]
```

```python
import concourse.bass as bass
from concourse import mybir
from contextlib import ExitStack, contextmanager

F32 = mybir.dt.float32
BF16 = mybir.dt.bfloat16
I32 = mybir.dt.int32
U32 = mybir.dt.uint32
U8 = mybir.dt.uint8
ACT = mybir.ActivationFunctionType
ALU = mybir.AluOpType
AXX = mybir.AxisListType.X

P = 128
B, SEQ, D = 8, 256, 256
H = 16
DK = D // H
NU = SEQ // P
NC = D // P
T = B * SEQ
NT = T // P
FF = 1024
NF = FF // P
NE = 8
EPS = 1e-5
NEG = -1.0e9
LOWEST = -3.0e38
OFF = -1.0e30

STACKS = ((0, (0, 3), (0, 3)), (3 * DK, (0, 2), (1, 3)), (5 * DK, (0, 1), (2, 3)))
ROWS = 6 * DK
ROW_KEY = ROWS
ROW_MAX = ROWS + 1
ROWS_ALL = ROWS + 3
VW = DK + 1
QUADS = H // 4
SCORES_AT = ((), (), (0,), (1,), (2, 3), (4,), (5,), (6, 7), (8,), (9, 10), (11,), (12,), (13, 14), (15,), (), ())
SCORES_AT_ROPE = ((0,), (1,), (2,), (3,), (4, 5), (6,), (7,), (8,), (9,), (10, 11), (12,), (13,), (14,), (15,), (), ())


@contextmanager
def stage_semaphores(nc, tag):
    taken = []

    def sem(n):
        taken.append(nc.alloc_semaphore(f"{tag}_{n}"))
        return taken[-1]

    yield sem
    nc.clear_and_free_semaphores(taken)
    nc.all_engine_barrier()


NORM_STEPS = 8


def norm_tiles(sb):
    return {"stats": sb("stats", [P, NU, 6]), "mv": sb("mv", [P, NU, 2]), "ve": sb("ve", [P, NU]), "std": sb("std", [P, NU]),
            "r0": sb("r0", [P, NU]), "r1": sb("r1", [P, NU]), "r2": sb("r2", [P, NU]), "r3": sb("r3", [P, NU]), "rstd": sb("rstd", [P, NU])}


def norm_rows(nc, dve, x, y, t, step, std_done, n, waited):
    base = NORM_STEPS * n

    def after(i, ins):
        ins.then_inc(step, 1)
        dve.wait_ge(step, base + i)

    for u in range(NU):
        ins = nc.vector.bn_stats(t["stats"][:, u, :], x[:, u, :])
    after(1, ins)
    dve.sem_inc(waited, 1)
    for u in range(NU):
        ins = nc.vector.bn_aggr(t["mv"][:, u, :], t["stats"][:, u, :])
    after(2, ins)
    nc.vector.tensor_scalar(t["ve"][:, :], t["mv"][:, :, 1], EPS, None, ALU.add).then_inc(step, 1)
    dve.wait_ge(std_done, n + 1)
    after(4, nc.vector.reciprocal(t["r0"][:, :], t["std"][:, :]))
    after(5, nc.vector.tensor_tensor(t["r1"][:, :], t["r0"][:, :], t["ve"][:, :], ALU.mult))
    after(6, nc.vector.tensor_tensor(t["r2"][:, :], t["r1"][:, :], t["r0"][:, :], ALU.mult))
    after(7, nc.vector.tensor_scalar(t["r3"][:, :], t["r2"][:, :], -0.5, 1.5, ALU.mult, ALU.add))
    after(8, nc.vector.tensor_tensor(t["rstd"][:, :], t["r0"][:, :], t["r3"][:, :], ALU.mult))
    for u in range(NU):
        ins = nc.vector.tensor_scalar(y[:, u, :], x[:, u, :], t["mv"][:, u, 0:1], t["rstd"][:, u:u + 1],
                                      ALU.subtract, ALU.mult)
    return ins


def norm_root(nc, act, t, step, std_done, n):
    act.wait_ge(step, NORM_STEPS * n + 3)
    nc.scalar.activation(t["std"][:, :], t["ve"][:, :], ACT.Sqrt).then_inc(std_done, 1)


def sequence_rows(a, n):
    if len(a.shape) == 3 and a.shape[0] == B:
        return a[n].rearrange("(u p) d -> p u d", p=P)
    return a[:, bass.ds(n * NU, NU), :]


def prepare(nc, a, const, masks, X, Y, key_off, parts, xd):
    with ExitStack() as ctx:
        sb = lambda n, s, d=F32: ctx.enter_context(nc.sbuf_tensor(f"pre_{n}", s, d))
        sem = ctx.enter_context(stage_semaphores(nc, "pre"))
        M, LAYERS = len(masks), len(parts)
        raw, zero, before_f = sb("raw", [P, 4]), sb("zero", [P, D]), sb("before_f", [P, P])
        keys_u, off = sb("keys_u", [B, SEQ], U8), sb("off", [B, SEQ], BF16)
        mi = sb("mi", [P, M, NU, SEQ], I32)
        keep, term = sb("keep", [P, M, NU, SEQ]), sb("term", [P, M, NU, SEQ])
        rowkeep, rowtile = sb("rowkeep", [P, M, NU]), sb("rowtile", [P, M, NU, P])
        bf = sb("bf", [NE, LAYERS, FF + D])
        r1, r2 = sb("rest1", [NE, LAYERS, FF + D]), sb("rest2", [NE, LAYERS, FF + D])
        q = sb("q", [NE, LAYERS, 3, FF + D], BF16)
        t = norm_tiles(sb)
        pT = [ctx.enter_context(nc.psum_tensor(f"pre_pT{i}", [P, 512], F32)) for i in range(M)]
        pR = [ctx.enter_context(nc.psum_tensor(f"pre_pR{i}", [P, 512], F32)) for i in range(M)]
        loaded, masks_in, biases_in, x_in = sem("loaded"), sem("masks_in"), sem("biases_in"), [sem("x_in0"), sem("x_in1")]
        zeroed, off_made, stored, gates_made = sem("zeroed"), sem("off_made"), sem("stored"), sem("gates_made")
        mask_step, turned, split = sem("mask_step"), sem("turned"), sem("split")
        step, std_done, normed, waited = sem("step"), sem("std_done"), sem("normed"), sem("waited")
        N_LOADED = 5
        block = ctx.enter_context(nc.Block())

        @block.sync
        def _(sp):
            for i, (mask, _, _, _) in enumerate(masks):
                sp.dma_start(mi[:, i, :, :], mask[0, 0].rearrange("(u p) k -> p u k", p=P)).then_inc(masks_in, 16)
            sp.dma_start(const["ident"][:, :], a["c_ident"]).then_inc(loaded, 16)
            sp.dma_start(before_f[:, :], a["c_before"]).then_inc(loaded, 16)
            sp.dma_start(raw[:, 0:2], a["g_xattn"].partition_broadcast(P)).then_inc(loaded, 16)
            sp.dma_start(raw[:, 2:4], a["g_ffn"].partition_broadcast(P)).then_inc(loaded, 16)
            sp.dma_start(keys_u[:, :], a["mask_BxS2_bf1"]).then_inc(loaded, 16)
            rows = a["x"].rearrange("b (u p) d -> p (b u) d", p=P)
            for half in range(2):
                tiles = slice(half * NT // 2, (half + 1) * NT // 2)
                sp.dma_start(X[:, tiles, :], rows[:, tiles, :]).then_inc(x_in[half], 16)
            for i, (b1, b2, _) in enumerate(parts):
                sp.dma_start(bf[:, i, 0:FF], b1).then_inc(biases_in, 16)
                sp.dma_start(bf[:, i, FF:FF + D], b2).then_inc(biases_in, 16)
            sp.wait_ge(zeroed, 1)
            for rows_ in xd:
                slots = rows_.shape[0] // P
                sp.dma_start(rows_.rearrange("(s p) d -> p s d", p=P),
                             zero[:, :].unsqueeze(1).broadcast_to([P, slots, D])).then_inc(stored, 16)
            sp.wait_ge(off_made, 1)
            sp.dma_start(key_off, off[:, :]).then_inc(stored, 16)
            sp.wait_ge(split, 5)
            for i, (_, _, out) in enumerate(parts):
                sp.dma_start(out.rearrange("s e n -> e s n"), q[:, i, :, :]).then_inc(stored, 16)
            sp.wait_ge(stored, 16 * (len(xd) + 1 + LAYERS))

        @block.gpsimd
        def _(pool):
            pool.wait_ge(biases_in, 32 * LAYERS)
            nc.gpsimd.tensor_copy(q[:, :, 0, :], bf[:, :, :]).then_inc(split, 1)
            pool.wait_ge(split, 1)
            nc.gpsimd.tensor_tensor(r1[:, :, :], bf[:, :, :], q[:, :, 0, :], ALU.subtract).then_inc(split, 1)
            pool.wait_ge(split, 2)
            nc.gpsimd.tensor_copy(q[:, :, 1, :], r1[:, :, :]).then_inc(split, 1)
            pool.wait_ge(split, 3)
            nc.gpsimd.tensor_tensor(r2[:, :, :], r1[:, :, :], q[:, :, 1, :], ALU.subtract).then_inc(split, 1)
            pool.wait_ge(split, 4)
            nc.gpsimd.tensor_copy(q[:, :, 2, :], r2[:, :, :]).then_inc(split, 1)

        @block.scalar
        def _(act):
            act.wait_ge(loaded, 16 * N_LOADED)
            nc.scalar.activation(const["gates"][:, :], raw[:, :], ACT.Tanh).then_inc(gates_made, 1)
            with act.Fori(0, B) as n:
                norm_root(nc, act, t, step, std_done, n)

        @block.tensor
        def _(pe):
            pe.wait_ge(loaded, 16 * N_LOADED)
            pe.wait_ge(mask_step, 4)
            for i in range(M):
                for kt in range(NU):
                    for u in range(NU):
                        nc.tensor.transpose(pT[i][:, kt * SEQ + u * P:kt * SEQ + (u + 1) * P],
                                            keep[:, i, u, kt * P:(kt + 1) * P], const["ident"][:, :])
                for u in range(NU):
                    ins = nc.tensor.transpose(pR[i][:, u * P:(u + 1) * P], rowtile[:, i, u, :], const["ident"][:, :])
            ins.then_inc(turned, 1)

        @block.vector
        def _(dve):
            nc.vector.memset(zero[:, :], 0.0).then_inc(zeroed, 1)
            nc.vector.memset(const["ones"][:, :], 1.0)
            dve.wait_ge(masks_in, 16 * M)
            nc.vector.tensor_scalar(keep[:, :, :, :], mi[:, :, :, :], 0.0, None, ALU.not_equal).then_inc(mask_step, 1)
            dve.wait_ge(mask_step, 1)
            nc.vector.tensor_reduce(rowkeep[:, :, :], keep[:, :, :, :], AXX, ALU.max).then_inc(mask_step, 1)
            dve.wait_ge(mask_step, 2)
            nc.vector.tensor_scalar(term[:, :, :, :], keep[:, :, :, :], 1.0, -NEG, ALU.subtract, ALU.mult).then_inc(mask_step, 1)
            dve.wait_ge(mask_step, 3)
            for i, (_, Bm, _, _) in enumerate(masks):
                for u in range(NU):
                    kept = rowkeep[:, i, u:u + 1]
                    nc.vector.tensor_scalar(Bm[:, u * SEQ:(u + 1) * SEQ], term[:, i, u, :], kept, None, ALU.mult)
                    nc.vector.tensor_scalar(keep[:, i, u, :], term[:, i, u, :], kept, None, ALU.mult)
                    ins = nc.vector.tensor_scalar(rowtile[:, i, u, :], term[:, i, u, 0:P], 0.0, kept, ALU.mult, ALU.add)
            ins.then_inc(mask_step, 1)
            dve.wait_ge(loaded, 16 * N_LOADED)
            nc.vector.tensor_copy(const["identb"][:, :], const["ident"][:, :])
            nc.vector.tensor_copy(const["before"][:, :], before_f[:, :])
            nc.vector.tensor_scalar(off[:, :], keys_u[:, :], 1.0, -OFF, ALU.subtract, ALU.mult).then_inc(off_made, 1)
            for half in range(2):
                dve.wait_ge(x_in[half], 16)
            with dve.Fori(0, B) as n:
                norm_rows(nc, dve, X[:, bass.ds(n * NU, NU), :], Y[:, bass.ds(n * NU, NU), :], t, step, std_done, n,
                          waited).then_inc(normed, 1)
                dve.wait_ge(normed, n + 1)
                dve.sem_inc(waited, 1)
            dve.wait_ge(turned, 1)
            for i, (_, _, BmT, R) in enumerate(masks):
                nc.vector.tensor_copy(BmT[:, :], pT[i][:, :])
                nc.vector.tensor_copy(R[:, :], pR[i][:, 0:SEQ])


def attention(nc, tag, c, src, ctx_in, w, out_ao, mask=None, rope=None):
    cross = ctx_in is not None
    masked = mask is not None
    with ExitStack() as ctx:
        sb = lambda n, s, d=F32: ctx.enter_context(nc.sbuf_tensor(f"{tag}_{n}", s, d))
        sem = ctx.enter_context(stage_semaphores(nc, tag))
        pair = lambda n: [sem(n + "0"), sem(n + "1")]
        bank = lambda n: ctx.enter_context(nc.psum_tensor(f"{tag}_{n}", [P, 512], F32))

        yb = sb("yb", [P, 2, NU, D])
        yT = sb("yT", [P, 2, NC, SEQ])
        cin = sb("cin", [P, 2, NU, D]) if cross else None
        cT = sb("cT", [P, 2, NC, SEQ]) if cross else yT
        wq, wk, wv = sb("wq", [P, NC, D]), sb("wk", [P, NC, D]), sb("wv", [P, NC, D])
        bq, bk, bv = sb("bq", [P, NC]), sb("bk", [P, NC]), sb("bv", [P, D])
        fq, fk = sb("fq", [P, NC * SEQ]), sb("fk", [P, NC * SEQ])
        rq, rk = sb("rq", [P, NC * SEQ]), sb("rk", [P, NC * SEQ])
        pq, pk = sb("pq", [P, 3, NC, SEQ], BF16), sb("pk", [P, 3, NC, SEQ], BF16)
        q_place, k_place = (0, 1, 2), (2, 1, 0)
        QS, KS = sb("QS", [P, 2, H, SEQ], BF16), sb("KS", [P, 2, H, SEQ], BF16)
        V = sb("V", [P, 2, NU, H * VW + 32])
        PT = sb("PT", [P, 4, NU * SEQ])
        OTS = sb("OTS", [P, 2, SEQ])
        rec = sb("rec", [P, NU, 4])
        mx = sb("mx", [P, NU, H])
        MQ = sb("MQ", [P, NU, 2 * H], BF16)
        MT = sb("MT", [2 * H, SEQ], BF16)
        if masked:
            masked_scores = sb("masked_scores", [P, 2, NU, SEQ], BF16)
        if rope:
            wqs, wks = sb("wqs", [P, NC, D]), sb("wks", [P, NC, D])
            bqs, bks = sb("bqs", [P, NC]), sb("bks", [P, NC])
            tq, tk = sb("tq", [P, NC * SEQ]), sb("tk", [P, NC * SEQ])
            mcu, mcf = sb("mcu", [P, 2, NU], U8), sb("mcf", [P, 2, NU])
            cosq, sinq, cosk, sink = (sb(n, [P, NC, SEQ]) for n in ("cosq", "sinq", "cosk", "sink"))
        bankS = [bank("S0"), bank("S1")]
        bankT = [bank("T0"), bank("T1")]
        bankO = [bank("O0"), bank("O1")]
        bankA, bankB = bank("A"), bank("B")
        max_bank = bankS[0][:, 0:P].bitcast(BF16)

        dram = lambda n, s: nc.dram_tensor(f"{tag}_{n}", s, BF16, kind="Internal").ap()
        q_dram, k_dram = dram("q_dram", (2, 3, D, SEQ)), dram("k_dram", (2, 3, D, SEQ))
        m_dram = dram("m_dram", (2, H, SEQ))

        w_loaded, ready0, waited, waited_dve = sem("w_loaded"), sem("ready0"), sem("waited"), sem("waited_dve")
        x_loaded, c_loaded, stacked, max_rows = pair("x_loaded"), pair("c_loaded"), pair("stacked"), pair("max_rows")
        mc_loaded = pair("mc_loaded")
        spread, m_spread = pair("spread"), sem("m_spread")
        t_ready, tc_ready, t_out, tc_out = sem("t_ready"), sem("tc_ready"), sem("t_out"), sem("tc_out")
        q_ready, k_ready, v_ready = sem("q_ready"), sem("k_ready"), sem("v_ready")
        q_out, k_out, v_out = sem("q_out"), sem("k_out"), sem("v_out")
        qr_ready, kr_ready, qr_out, kr_out = sem("qr_ready"), sem("kr_ready"), sem("qr_out"), sem("kr_out")
        f_sum = sem("f_sum")
        part1, part2, part3, rest1 = sem("part1"), sem("part2"), sem("part3"), sem("rest1")
        s_ready, max_done, m_step, mt_ready, mt_out = sem("s_ready"), sem("max_done"), sem("m_step"), sem("mt_ready"), sem("mt_out")
        st_ready, exp_done, pv_done = sem("st_ready"), sem("exp_done"), sem("pv_done")
        ot_out, ot_turned, rec_done, head_norm = sem("ot_out"), sem("ot_turned"), sem("rec_done"), sem("head_norm")
        mc_step = sem("mc_step")
        N_W = 6 + 4 * bool(rope) + 4 * bool(rope)
        N_STACK = 2 * len(STACKS) + bool(rope)
        scores_at = SCORES_AT_ROPE if rope else SCORES_AT
        later = lambda n, first: not (isinstance(n, int) and n < first)

        def steps(eng, body, first):
            first()
            with eng.Fori(0, B // 2 - 1) as j:
                body(2 * j, 0, j, True, True)
                body(2 * j + 1, 1, j, True, True)
            body(B - 2, 0, B // 2 - 1, True, False)
            body(B - 1, 1, B // 2 - 1, False, False)

        block = ctx.enter_context(nc.Block())

        @block.sync
        def _(sp):
            def wait(semaphore, value):
                sp.wait_ge(semaphore, value)
                if not isinstance(value, int):
                    sp.sem_inc(waited, 1)

            def load_rows(n, p):
                if later(n, 2):
                    wait(t_ready, n - 1)
                sp.dma_start(yb[:, p, :, :], sequence_rows(src, n)).then_inc(x_loaded[p], 16)
                if cross:
                    if later(n, 2):
                        wait(tc_ready, n - 1)
                    sp.dma_start(cin[:, p, :, :], sequence_rows(ctx_in, n)).then_inc(c_loaded[p], 16)
                if rope:
                    if later(n, 2):
                        wait(mc_step, 2 * n - 3)
                    sp.dma_start(mcu[:, p, :], rope["keys"][bass.ds(n, 1), :].rearrange("o (u p) -> p (o u)", p=P),
                                 allow_slow_non_contiguous=True).then_inc(mc_loaded[p], 16)

            def spread_parts(n, p, k):
                if later(n, 2):
                    wait(stacked[p], 16 * N_STACK * k)
                for side, (parts, dram) in enumerate(((pq, q_dram), (pk, k_dram))):
                    wait(part3, 2 * n + 1 + side)
                    sp.dma_start(dram[p].rearrange("s (c r) t -> r s c t", r=P), parts[:, :, :, :]).then_inc(spread[side], 16)

            def stack(n, p, k):
                wait(pv_done, H * n + 4 - H if later(n, 1) else 4)
                for side, (dram, dst) in enumerate(((q_dram, QS), (k_dram, KS))):
                    wait(spread[side], 16 * (n + 1))
                    for row, q_run, k_run in STACKS:
                        a, b = (q_run, k_run)[side]
                        sp.dma_start(dst[row:row + (b - a) * DK, p, :, :],
                                     dram[p, a:b].rearrange("s (d h) t -> (s d) h t", d=DK)).then_inc(stacked[p], 16)
                if rope:
                    sp.dma_start(KS[ROW_KEY:ROW_KEY + 1, p, :, :],
                                 rope["key_off"][bass.ds(n, 1), :].unsqueeze(1).broadcast_to([1, H, SEQ])).then_inc(stacked[p], 16)

            def first():
                for n in range(2):
                    load_rows(n, n)
                for a, d in ((wq, w["wq"]), (wk, w["wk"]), (wv, w["wv"])):
                    sp.dma_start(a[:, :, :], d.rearrange("(c p) n -> p c n", p=P)).then_inc(w_loaded, 16)
                for a, d in ((bq, w["bq"]), (bk, w["bk"])):
                    sp.dma_start(a[:, :], d.rearrange("(c p) -> p c", p=P), allow_slow_non_contiguous=True).then_inc(w_loaded, 16)
                sp.dma_start(bv[:, :], w["bv"].partition_broadcast(P)).then_inc(w_loaded, 16)
                if rope:
                    for a, d in ((wqs, w["wqs"]), (wks, w["wks"])):
                        sp.dma_start(a[:, :, :], d.rearrange("(c p) n -> p c n", p=P)).then_inc(w_loaded, 16)
                    for a, d in ((bqs, w["bqs"]), (bks, w["bks"])):
                        sp.dma_start(a[:, :], d.rearrange("(c p) -> p c", p=P), allow_slow_non_contiguous=True).then_inc(w_loaded, 16)
                    for a, d in ((cosq, "cosq"), (sinq, "sinq"), (cosk, "cosk"), (sink, "sink")):
                        sp.dma_start(a[:, :, :], rope[d].rearrange("(c p) t -> p c t", p=P)).then_inc(w_loaded, 16)
                spread_parts(0, 0, 0)
                wait(ready0, 2)
                stack(0, 0, 0)
                spread_parts(1, 1, 0)

            def body(n, p, k, more, more2):
                if more2:
                    load_rows(n + 2, p)
                wait(mt_out, n + 1)
                sp.dma_start(m_dram.rearrange("j h t -> (j h) t"), MT[:, :]).then_inc(m_spread, 16)
                wait(m_spread, 16 * (n + 1))
                sp.dma_start(QS[ROW_MAX:ROW_MAX + 2, p, :, :], m_dram).then_inc(max_rows[p], 16)
                if more:
                    stack(n + 1, 1 - p, k + p)
                if more2:
                    spread_parts(n + 2, p, k + 1)

            steps(sp, body, first)

        @block.tensor
        def _(pe):
            ident = c["ident"]
            identb = c["identb"]
            last_a, last_b = (kr_out, k_out) if rope else (k_out, q_out)

            def turn(n, p, k):
                pe.wait_ge(x_loaded[p], 16 * (k + 1))
                if later(n, 2):
                    pe.wait_ge(exp_done, H * n - 31)
                if later(n, 1):
                    pe.wait_ge(t_out, n)
                for cc in range(NC):
                    for u in range(NU):
                        ins = nc.tensor.transpose(bankT[0][:, cc * SEQ + u * P:cc * SEQ + (u + 1) * P],
                                                  yb[:, p, u, cc * P:(cc + 1) * P], ident[:, :])
                ins.then_inc(t_ready, 1)
                if cross:
                    if later(n, 2):
                        pe.wait_ge(exp_done, H * n - 30)
                    if later(n, 1):
                        pe.wait_ge(tc_out, n)
                    pe.wait_ge(c_loaded[p], 16 * (k + 1))
                    for cc in range(NC):
                        for u in range(NU):
                            ins = nc.tensor.transpose(bankT[1][:, cc * SEQ + u * P:cc * SEQ + (u + 1) * P],
                                                      cin[:, p, u, cc * P:(cc + 1) * P], ident[:, :])
                    ins.then_inc(tc_ready, 1)

            def product(dst, wt, rhs, done):
                for cc in range(NC):
                    for kc in range(NC):
                        ins = nc.tensor.matmul(dst[:, cc * SEQ:(cc + 1) * SEQ], wt[:, kc, cc * P:(cc + 1) * P],
                                               rhs[:, kc, :], start=(kc == 0), stop=(kc == NC - 1))
                ins.then_inc(done, 1)

            def queries_and_keys(n, p):
                pe.wait_ge(t_out, n + 1)
                if later(n, 2):
                    pe.wait_ge(head_norm, QUADS * (n - 1))
                if later(n, 1):
                    pe.wait_ge(last_b, n)
                product(bankB, wq, yT[:, p], q_ready)
                if later(n, 1):
                    pe.wait_ge(v_out, n)
                if cross:
                    pe.wait_ge(tc_out, n + 1)
                if rope:
                    product(bankA, wqs, yT[:, p], qr_ready)
                    pe.wait_ge(q_out, n + 1)
                    product(bankB, wk, cT[:, p], k_ready)
                    pe.wait_ge(qr_out, n + 1)
                    product(bankA, wks, cT[:, p], kr_ready)
                else:
                    product(bankA, wk, cT[:, p], k_ready)

            def project_values(n, p):
                pe.wait_ge(last_a, n + 1)
                if later(n, 1):
                    pe.wait_ge(head_norm, QUADS * n - 1)
                for u in range(NU):
                    for kc in range(NC):
                        ins = nc.tensor.matmul(bankA[:, u * D:(u + 1) * D], cT[:, p, kc, u * P:(u + 1) * P], wv[:, kc, :],
                                               start=(kc == 0), stop=(kc == NC - 1))
                ins.then_inc(v_ready, 1)

            rows = ROW_KEY + 1 if rope else ROWS

            def scores(n, p, k, h):
                if h == 0:
                    pe.wait_ge(stacked[p], 16 * N_STACK * (k + 1))
                    if later(n, 1):
                        pe.wait_ge(mt_out, n)
                pe.wait_ge(max_done, H * n + h + 1)
                for u in range(NU):
                    ins = nc.tensor.matmul(bankS[h % 2][:, u * SEQ:(u + 1) * SEQ], QS[0:rows, p, h, u * P:(u + 1) * P],
                                           KS[0:rows, p, h, :], start=True, stop=True)
                ins.then_inc(s_ready, 1)

            def turn_max(n):
                pe.wait_ge(m_step, 2 * n + 2)
                for u in range(NU):
                    ins = nc.tensor.transpose(max_bank[0:2 * H, u * P:(u + 1) * P], MQ[:, u, :], identb[:, :])
                ins.then_inc(mt_ready, 1)

            def scores_T(n, p, k, h):
                if h == 0:
                    pe.wait_ge(max_rows[p], 16 * (k + 1))
                pe.wait_ge(exp_done, H * n + h + 1)
                bk_ = bankT[h % 2]
                if masked:
                    nc.tensor.matmul(bk_[:, :], identb[:, :], mask[1][:, :], start=True, stop=False)
                for u in range(NU):
                    ins = nc.tensor.matmul(bk_[:, u * SEQ:(u + 1) * SEQ], KS[0:ROWS_ALL, p, h, u * P:(u + 1) * P],
                                           QS[0:ROWS_ALL, p, h, :], start=not masked, stop=(not masked or u == NU - 1))
                ins.then_inc(st_ready, 1)

            def values(n, p, k, h):
                pe.wait_ge(exp_done, H * n + h + 3)
                if h == 0:
                    pe.wait_ge(v_out, n + 1)
                if h % 4 == 0:
                    pe.wait_ge(ot_out, QUADS * n + h // 4 + 1)
                o = bankO[(h // 4) % 2][32 * (h % 4):32 * (h % 4) + 32, 0:SEQ]
                for u in range(NU):
                    ins = nc.tensor.matmul(o, V[:, p, u, h * VW:h * VW + 32], PT[:, h % 4, u * SEQ:(u + 1) * SEQ],
                                           start=(u == 0), stop=(u == NU - 1))
                ins.then_inc(pv_done, 1)

            def turn_out(n, g, more, more2):
                pe.wait_ge(ot_out, QUADS * n + g + 3)
                pe.wait_ge(head_norm, QUADS * (n + 1) + g - 1)
                if g < 2 and more2:
                    pe.wait_ge((last_a, last_b)[g], n + 3)
                elif g == 0 and more:
                    pe.wait_ge(v_out, n + 2)
                bk_ = (bankA, bankB)[g % 2]
                for u in range(NU):
                    ins = nc.tensor.transpose(bk_[:, u * P:(u + 1) * P], OTS[:, g % 2, u * P:(u + 1) * P], ident[:, :])
                ins.then_inc(ot_turned, 1)

            def first():
                turn(0, 0, 0)
                pe.wait_ge(w_loaded, 16 * N_W)
                queries_and_keys(0, 0)
                project_values(0, 0)
                turn(1, 1, 0)
                queries_and_keys(1, 1)
                for h in range(H):
                    scores(0, 0, 0, h)
                turn_max(0)

            def body(n, p, k, more, more2):
                if more2:
                    turn(n + 2, p, k + 1)
                if more:
                    project_values(n + 1, 1 - p)
                if more2:
                    queries_and_keys(n + 2, p)
                for h in range(H):
                    scores_T(n, p, k, h)
                    if h >= 2:
                        values(n, p, k, h - 2)
                    if h in (7, 11, 15):
                        turn_out(n, (h - 7) // 4, more, more2)
                    if more:
                        for h1 in scores_at[h]:
                            scores(n + 1, 1 - p, k + p, h1)
                    if more and h == 15:
                        turn_max(n + 1)
                values(n, p, k, H - 2)
                values(n, p, k, H - 1)
                turn_out(n, QUADS - 1, more, more2)

            steps(pe, body, first)

        @block.scalar
        def _(act):
            def bring(n, p):
                act.wait_ge(t_ready, n + 1)
                if later(n, 2):
                    act.wait_ge(v_ready, n - 1)
                    act.wait_ge((kr_ready if rope else k_ready), n - 1)
                nc.scalar.activation(yT[:, p, :, :].rearrange("p c t -> p (c t)"), bankT[0][:, :], ACT.Copy).then_inc(t_out, 1)
                if cross:
                    act.wait_ge(tc_ready, n + 1)
                    nc.scalar.activation(cT[:, p, :, :].rearrange("p c t -> p (c t)"), bankT[1][:, :], ACT.Copy).then_inc(tc_out, 1)

            def first_part(n, side, f, parts, place):
                if rope:
                    act.wait_ge(f_sum, 2 * n + 1 + side)
                else:
                    act.wait_ge((q_out, k_out)[side], n + 1)
                if later(n, 1):
                    act.wait_ge(spread[side], 16 * n)
                nc.scalar.activation(parts[:, place[0], :, :].rearrange("p c t -> p (c t)"), f[:, :], ACT.Copy).then_inc(part1, 1)

            def second_part(n, side, r, parts, place):
                act.wait_ge(rest1, 2 * n + 1 + side)
                nc.scalar.activation(parts[:, place[1], :, :].rearrange("p c t -> p (c t)"), r[:, :], ACT.Copy).then_inc(part2, 1)

            def keys(n):
                if rope:
                    return
                act.wait_ge(k_ready, n + 1)
                if later(n, 1):
                    act.wait_ge(rest1, 2 * n)
                for cc in range(NC):
                    ins = nc.scalar.activation(fk[:, cc * SEQ:(cc + 1) * SEQ], bankA[:, cc * SEQ:(cc + 1) * SEQ],
                                               ACT.Identity, bias=bk[:, cc:cc + 1])
                ins.then_inc(k_out, 1)

            def exps(n, h):
                act.wait_ge(st_ready, H * n + h + 1)
                act.wait_ge(pv_done, H * n + h + 1)
                nc.scalar.activation(PT[:, h % 4, :], bankT[h % 2][:, :], ACT.Exp).then_inc(exp_done, 1)

            def outputs(n, g):
                act.wait_ge(pv_done, H * n + 4 * g + 8)
                act.wait_ge(ot_turned, QUADS * n + g + 1)
                nc.scalar.activation(OTS[:, g % 2, :], bankO[g % 2][:, 0:SEQ], ACT.Copy).then_inc(ot_out, 1)

            def parts_of(n, p):
                bring(n, p)
                first_part(n, 0, fq, pq, q_place)
                keys(n)

            def first():
                act.sem_inc(exp_done, 2)
                act.sem_inc(ot_out, 2)
                act.wait_ge(w_loaded, 16 * N_W)
                for n in range(2):
                    parts_of(n, n)
                    first_part(n, 1, fk, pk, k_place)
                    second_part(n, 0, rq, pq, q_place)
                    second_part(n, 1, rk, pk, k_place)

            def body(n, p, k, more, more2):
                if more2:
                    parts_of(n + 2, p)
                for h in range(H):
                    exps(n, h)
                    if more2:
                        if h == 0:
                            first_part(n + 2, 1, fk, pk, k_place)
                        elif h == 2:
                            second_part(n + 2, 0, rq, pq, q_place)
                        elif h == 3:
                            second_part(n + 2, 1, rk, pk, k_place)
                    if h in (6, 10, 14):
                        outputs(n, (h - 6) // 4)
                outputs(n, QUADS - 1)

            steps(act, body, first)

        @block.gpsimd
        def _(pool):
            def split(n):
                if rope:
                    for side, (f, t) in enumerate(((fq, tq), (fk, tk))):
                        pool.wait_ge((qr_out, kr_out)[side], n + 1)
                        nc.gpsimd.tensor_tensor(f[:, :], f[:, :], t[:, :], ALU.add).then_inc(f_sum, 1)
                for side, (f, r, parts, place) in enumerate(((fq, rq, pq, q_place), (fk, rk, pk, k_place))):
                    pool.wait_ge(part1, 2 * n + 1 + side)
                    nc.gpsimd.tensor_tensor(r[:, :], f[:, :], parts[:, place[0], :, :].rearrange("p c t -> p (c t)"),
                                            ALU.subtract).then_inc(rest1, 1)
                for side, (r, parts, place) in enumerate(((rq, pq, q_place), (rk, pk, k_place))):
                    pool.wait_ge(part2, 2 * n + 1 + side)
                    nc.gpsimd.tensor_tensor(parts[:, place[2], :, :].rearrange("p c t -> p (c t)"), r[:, :],
                                            parts[:, place[1], :, :].rearrange("p c t -> p (c t)"), ALU.subtract).then_inc(part3, 1)

            def first():
                nc.gpsimd.memset(V[:, :, :, :], 1.0).then_inc(ready0, 1)
                split(0)
                split(1)

            def body(n, p, k, more, more2):
                if more2:
                    split(n + 2)

            steps(pool, body, first)

        @block.vector
        def _(dve):
            def queries(n):
                dve.wait_ge(q_ready, n + 1)
                if later(n, 1):
                    dve.wait_ge(rest1, 2 * n - 1)
                for cc in range(NC):
                    cols = slice(cc * SEQ, (cc + 1) * SEQ)
                    ins = nc.vector.scalar_tensor_tensor(fq[:, cols], bankB[:, cols], bq[:, cc:cc + 1],
                                                         cosq[:, cc, :] if rope else mask[2][:, :], ALU.add, ALU.mult)
                ins.then_inc(q_out, 1)
                if rope:
                    for src_, b_, tab, dst, rdy, out in ((bankA, bqs, sinq, tq, qr_ready, qr_out),
                                                         (bankB, bk, cosk, fk, k_ready, k_out),
                                                         (bankA, bks, sink, tk, kr_ready, kr_out)):
                        dve.wait_ge(rdy, n + 1)
                        if dst is fk and later(n, 1):
                            dve.wait_ge(rest1, 2 * n)
                        for cc in range(NC):
                            cols = slice(cc * SEQ, (cc + 1) * SEQ)
                            ins = nc.vector.scalar_tensor_tensor(dst[:, cols], src_[:, cols], b_[:, cc:cc + 1],
                                                                 tab[:, cc, :], ALU.add, ALU.mult)
                        ins.then_inc(out, 1)

            def value_rows(n, p, k):
                if rope:
                    dve.wait_ge(mc_loaded[p], 16 * (k + 1))
                    nc.vector.tensor_copy(mcf[:, p, :], mcu[:, p, :]).then_inc(mc_step, 1)
                    dve.wait_ge(mc_step, 2 * n + 1)
                dve.wait_ge(v_ready, n + 1)
                if later(n, 2):
                    dve.wait_ge(pv_done, H * n - 12)
                heads = [V[:, p, u, 0:H * VW].rearrange("p (h e) -> p h e", e=VW) for u in range(NU)]
                for u in range(NU):
                    ins = nc.vector.tensor_tensor(heads[u][:, :, 0:DK], bankA[:, u * D:(u + 1) * D].rearrange("p (h e) -> p h e", e=DK),
                                                  bv[:, :].rearrange("p (h e) -> p h e", e=DK), ALU.add)
                if rope:
                    ins.then_inc(mc_step, 1)
                    dve.wait_ge(mc_step, 2 * n + 2)
                    for u in range(NU):
                        nc.vector.tensor_copy(heads[u][:, :, DK], mcf[:, p, u:u + 1].broadcast_to([P, H]))
                        ins = nc.vector.tensor_scalar(heads[u][:, :, 0:DK], heads[u][:, :, 0:DK], mcf[:, p, u:u + 1],
                                                      None, ALU.mult)
                ins.then_inc(v_out, 1)

            def maxima(n, h):
                dve.wait_ge(s_ready, H * n + h + 1)
                if h == 0 and later(n, 1):
                    dve.wait_ge(m_step, 2 * n)
                if not masked:
                    nc.vector.tensor_reduce(mx[:, :, h:h + 1], bankS[h % 2][:, :].rearrange("p (u k) -> p u k", u=NU),
                                            AXX, ALU.max).then_inc(max_done, 1)
                    return
                dve.wait_ge(max_done, H * n + h + 1)
                dve.sem_inc(waited_dve, 1)
                for u in range(NU):
                    ins = nc.vector.tensor_tensor_reduce(masked_scores[:, h % 2, u, :], bankS[h % 2][:, u * SEQ:(u + 1) * SEQ],
                                                         mask[0][:, u * SEQ:(u + 1) * SEQ], 1.0, LOWEST, ALU.add, ALU.max,
                                                         accum_out=mx[:, u, h:h + 1])
                ins.then_inc(max_done, 1)

            def minus_maxima(n):
                dve.wait_ge(max_done, H * n + H + 2)
                nc.vector.tensor_scalar(MQ[:, :, 0:H], mx[:, :, :], -1.0, None, ALU.mult).then_inc(m_step, 1)
                dve.wait_ge(m_step, 2 * n + 1)
                nc.vector.scalar_tensor_tensor(MQ[:, :, H:2 * H], mx[:, :, :], -1.0, MQ[:, :, 0:H],
                                               ALU.mult, ALU.subtract).then_inc(m_step, 1)

            def max_columns(n):
                dve.wait_ge(mt_ready, n + 1)
                if later(n, 1):
                    dve.wait_ge(m_spread, 16 * n)
                nc.vector.tensor_copy(MT[:, :], max_bank[0:2 * H, 0:SEQ]).then_inc(mt_out, 1)

            def normalise(n, p, k, g):
                dve.wait_ge(ot_turned, QUADS * n + g + 3)
                o = (bankA, bankB)[g % 2][:, 0:NU * P].rearrange("p (g e) -> p g e", e=32)
                dve.wait_ge(head_norm, QUADS * n + g + 4)
                nc.vector.reciprocal(rec[:, :, :].rearrange("p u h -> p (u h)"), o[:, :, DK]).then_inc(rec_done, 1)
                dve.wait_ge(rec_done, QUADS * n + g + 1)
                for u in range(NU):
                    dst = out_ao[:, bass.ds(n * NU + u, 1), g * 4 * DK:(g + 1) * 4 * DK].rearrange("p o (h e) -> p (o h) e", e=DK)
                    ins = nc.vector.tensor_tensor(dst, o[:, 4 * u:4 * u + 4, 0:DK],
                                                  rec[:, u, :].unsqueeze(2).broadcast_to([P, 4, DK]), ALU.mult)
                ins.then_inc(head_norm, 1)

            def first():
                dve.sem_inc(max_done, 2)
                dve.sem_inc(head_norm, QUADS)
                dve.sem_inc(ot_turned, 2)
                dve.sem_inc(pv_done, 4)
                nc.vector.memset(QS[ROW_KEY:ROWS_ALL, :, :, :], 1.0 if rope else 0.0)
                nc.vector.memset(KS[ROW_KEY:ROWS_ALL, :, :, :], 1.0).then_inc(ready0, 1)
                dve.wait_ge(w_loaded, 16 * N_W)
                queries(0)
                dve.wait_ge(ready0, 2)
                value_rows(0, 0, 0)
                queries(1)
                for h in range(H):
                    maxima(0, h)
                minus_maxima(0)
                max_columns(0)

            def body(n, p, k, more, more2):
                if more:
                    value_rows(n + 1, 1 - p, k + p)
                if more2:
                    queries(n + 2)
                for h in range(H):
                    if h in (7, 11, 15):
                        normalise(n, p, k, (h - 7) // 4)
                    if more:
                        for h1 in scores_at[h]:
                            maxima(n + 1, h1)
                        if h == 13:
                            minus_maxima(n + 1)
                    if more and h == 15:
                        max_columns(n + 1)
                normalise(n, p, k, QUADS - 1)

            steps(dve, body, first)


def by_sequence(eng, first, body):
    first()
    with eng.Fori(0, B // 2 - 1) as j:
        body(2 * j, 0, j, True, True)
        body(2 * j + 1, 1, j, True, True)
    body(B - 2, 0, B // 2 - 1, True, False)
    body(B - 1, 1, B // 2 - 1, False, False)


def token_block(nc, tag, c, X, Y, AO, w, affine, gate, ffn):
    with ExitStack() as ctx:
        sb = lambda n, s, d=F32: ctx.enter_context(nc.sbuf_tensor(f"{tag}_{n}", s, d))
        sem = ctx.enter_context(stage_semaphores(nc, tag))
        pair = lambda n: [sem(n + "0"), sem(n + "1")]
        bank = lambda n: ctx.enter_context(nc.psum_tensor(f"{tag}_{n}", [P, 512], F32))
        ident = c["ident"]

        ab = sb("ab", [P, 2, NU, D])
        aT = sb("aT", [P, 2, NC, SEQ])
        if ffn:
            w1, w2 = sb("w1", [P, NC, FF]), sb("w2", [P, NF, D])
            b1 = sb("b1", [P, NF])
            hT = sb("hT", [P, 2, NF, SEQ])
            bankH = [bank(f"H{j}") for j in range(NF // 2)]
        else:
            wo = sb("wo", [P, NC, D])
        bias = sb("bias", [P, D])
        z = sb("z", [P, 2, NU, D])
        if affine:
            yb_bias = sb("ybb", [P, 2, NU, D])
            gain, shift = sb("gain", [P, D]), sb("shift", [P, D])
            zn, zg = sb("zn", [P, 2, NU, D]), sb("zg", [P, 2, NU, D])
            t1 = norm_tiles(lambda n, s: sb("a" + n, s))
        if gate is not None:
            t2 = norm_tiles(lambda n, s: sb("g" + n, s))
            xo = sb("xo", [P, 2, NU, D])
            wb = sb("wb", [P, 2, NU, D])
        bankT = [bank("T0"), bank("T1")]
        bankZ = [bank("Z0"), bank("Z1")]
        flat = lambda a: a.rearrange("p u d -> p (u d)")
        rows = lambda a: a[:, :].unsqueeze(1).broadcast_to([P, NU, D])
        here = lambda a, n: a[:, bass.ds(n * NU, NU), :]

        w_loaded = sem("w_loaded")
        a_loaded, x_stored = pair("a_loaded"), pair("x_stored")
        waited, waited_dve, waited_pool = sem("waited"), sem("waited_dve"), sem("waited_pool")
        turned, t_out, h_ready, h_out = sem("turned"), sem("t_out"), sem("h_ready"), sem("h_out")
        z_ready, z_done, ybb_done = sem("z_ready"), sem("z_done"), sem("ybb_done")
        step1, root1, normed1, gained, shifted = sem("step1"), sem("root1"), sem("normed1"), sem("gained"), sem("shifted")
        step2, root2, x_new, finished = sem("step2"), sem("root2"), sem("x_new"), sem("finished")
        n_w = 16 * (4 if ffn else 2) + 16 * 2 * affine

        block = ctx.enter_context(nc.Block())

        @block.sync
        def _(sp):
            def wait(semaphore, value):
                sp.wait_ge(semaphore, value)
                if not isinstance(value, int):
                    sp.sem_inc(waited, 1)

            def load(n, p):
                sp.dma_start(ab[:, p, :, :], here(Y if ffn else AO, n)).then_inc(a_loaded[p], 16)

            def first():
                for n in range(2):
                    load(n, n)
                if ffn:
                    sp.dma_start(w1[:, :, :], w["w1"].rearrange("(c p) n -> p c n", p=P)).then_inc(w_loaded, 16)
                    sp.dma_start(w2[:, :, :], w["w2"].rearrange("(c p) n -> p c n", p=P)).then_inc(w_loaded, 16)
                    sp.dma_start(b1[:, :], w["b1"].rearrange("(c p) -> p c", p=P), allow_slow_non_contiguous=True).then_inc(w_loaded, 16)
                else:
                    sp.dma_start(wo[:, :, :], w["wo"].rearrange("(c p) n -> p c n", p=P)).then_inc(w_loaded, 16)
                sp.dma_start(bias[:, :], w["b"].partition_broadcast(P)).then_inc(w_loaded, 16)
                if affine:
                    sp.dma_start(gain[:, :], w["g"].partition_broadcast(P)).then_inc(w_loaded, 16)
                    sp.dma_start(shift[:, :], w["beta"].partition_broadcast(P)).then_inc(w_loaded, 16)

            def body(n, p, k, more, more2):
                if more2:
                    wait(turned, n + 1)
                    load(n + 2, p)
                if gate is not None:
                    wait(x_new, n + 1)
                    sp.dma_start(here(X, n), xo[:, p, :, :]).then_inc(x_stored[p], 16)

            by_sequence(sp, first, body)
            if gate is not None:
                for p in range(2):
                    sp.wait_ge(x_stored[p], 16 + 16 * (B // 2))

        @block.tensor
        def _(pe):
            def turn(n, p, k):
                pe.wait_ge(a_loaded[p], 16 * (k + 1))
                pe.wait_ge(t_out, n + 1)
                for cc in range(NC):
                    for u in range(NU):
                        ins = nc.tensor.transpose(bankT[p][:, cc * SEQ + u * P:cc * SEQ + (u + 1) * P],
                                                  ab[:, p, u, cc * P:(cc + 1) * P], ident[:, :])
                ins.then_inc(turned, 1)

            def project(n, p):
                pe.wait_ge(t_out, n + 3)
                pe.wait_ge(z_done, n + 1)
                for u in range(NU):
                    for kc in range(NC):
                        ins = nc.tensor.matmul(bankZ[p][:, u * D:(u + 1) * D], aT[:, p, kc, u * P:(u + 1) * P],
                                               wo[:, kc, :], start=(kc == 0), stop=(kc == NC - 1))
                ins.then_inc(z_ready, 1)

            def up(n, p):
                pe.wait_ge(t_out, n + 3)
                for j in range(NF // 2):
                    pe.wait_ge(h_out, NF // 2 * n + j + 1)
                    for f in (2 * j, 2 * j + 1):
                        for kc in range(NC):
                            ins = nc.tensor.matmul(bankH[j][:, (f % 2) * SEQ:(f % 2 + 1) * SEQ],
                                                   w1[:, kc, f * P:(f + 1) * P], aT[:, p, kc, :],
                                                   start=(kc == 0), stop=(kc == NC - 1))
                    ins.then_inc(h_ready, 1)

            def down(n, p):
                pe.wait_ge(h_out, NF // 2 * (n + 2))
                pe.wait_ge(z_done, n + 1)
                for u in range(NU):
                    for f in range(NF):
                        ins = nc.tensor.matmul(bankZ[p][:, u * D:(u + 1) * D], hT[:, p, f, u * P:(u + 1) * P],
                                               w2[:, f, :], start=(f == 0), stop=(f == NF - 1))
                ins.then_inc(z_ready, 1)

            def first():
                turn(0, 0, 0)
                turn(1, 1, 0)
                pe.wait_ge(w_loaded, n_w)
                if ffn:
                    up(0, 0)

            def body(n, p, k, more, more2):
                if not ffn:
                    project(n, p)
                else:
                    if more:
                        up(n + 1, 1 - p)
                    down(n, p)
                if more2:
                    turn(n + 2, p, k + 1)

            by_sequence(pe, first, body)

        @block.scalar
        def _(act):
            def bring(n, p):
                act.wait_ge(turned, n + 1)
                act.wait_ge(z_ready, n + 1)
                nc.scalar.activation(flat(aT[:, p, :, :]), bankT[p][:, :], ACT.Copy).then_inc(t_out, 1)

            def hidden(n, p):
                act.wait_ge(z_ready, n + 1)
                for j in range(NF // 2):
                    act.wait_ge(h_ready, NF // 2 * n + j + 1)
                    for f in (2 * j, 2 * j + 1):
                        ins = nc.scalar.activation(hT[:, p, f, :], bankH[j][:, (f % 2) * SEQ:(f % 2 + 1) * SEQ],
                                                   ACT.Relu, bias=b1[:, f:f + 1])
                    ins.then_inc(h_out, 1)

            def first():
                act.sem_inc(t_out, 2)
                act.sem_inc(z_ready, 2)
                if ffn:
                    act.sem_inc(h_out, NF // 2)
                bring(0, 0)
                bring(1, 1)
                if ffn:
                    act.wait_ge(w_loaded, n_w)
                    hidden(0, 0)

            def body(n, p, k, more, more2):
                if ffn and more:
                    hidden(n + 1, 1 - p)
                if more2:
                    bring(n + 2, p)
                if affine:
                    norm_root(nc, act, t1, step1, root1, n)
                if gate is not None:
                    norm_root(nc, act, t2, step2, root2, n)

            by_sequence(act, first, body)

        @block.gpsimd
        def _(pool):
            def add_bias(n, p):
                pool.wait_ge(z_done, n + 1)
                pool.sem_inc(waited_pool, 1)
                nc.gpsimd.tensor_tensor(yb_bias[:, p, :, :], here(Y, n), rows(bias), ALU.add).then_inc(ybb_done, 1)

            def first():
                pool.wait_ge(w_loaded, n_w)
                add_bias(0, 0)

            def body(n, p, k, more, more2):
                if more:
                    add_bias(n + 1, 1 - p)
                pool.wait_ge(normed1, n + 1)
                nc.gpsimd.tensor_tensor(zg[:, p, :, :], zn[:, p, :, :], rows(gain), ALU.mult).then_inc(gained, 1)
                pool.wait_ge(gained, n + 3)
                pool.sem_inc(waited_pool, 1)
                if gate is None:
                    nc.gpsimd.tensor_tensor(here(Y, n), zg[:, p, :, :], rows(shift), ALU.add).then_inc(finished, 1)
                else:
                    nc.gpsimd.tensor_tensor(wb[:, p, :, :], zg[:, p, :, :], rows(shift), ALU.add).then_inc(shifted, 1)

            if affine:
                by_sequence(pool, first, body)

        @block.vector
        def _(dve):
            def first():
                dve.sem_inc(z_done, 2)
                dve.sem_inc(gained, 2)
                if gate is not None:
                    for p in range(2):
                        dve.sem_inc(x_stored[p], 16)
                dve.wait_ge(w_loaded, n_w)

            def body(n, p, k, more, more2):
                zb = bankZ[p][:, :].rearrange("p (u d) -> p u d", u=NU)
                dve.wait_ge(z_ready, n + 3)
                if affine:
                    dve.wait_ge(ybb_done, n + 1)
                    nc.vector.tensor_tensor(z[:, p, :, :], zb, yb_bias[:, p, :, :], ALU.add).then_inc(z_done, 1)
                    dve.wait_ge(z_done, n + 3)
                    dve.wait_ge(gained, n + 1)
                    norm_rows(nc, dve, z[:, p], zn[:, p], t1, step1, root1, n, waited_dve).then_inc(normed1, 1)
                    w_rows = wb[:, p, :, :] if gate is not None else None
                else:
                    nc.vector.tensor_tensor(z[:, p, :, :], zb, rows(bias), ALU.add).then_inc(z_done, 1)
                    w_rows = z[:, p, :, :]
                if gate is None:
                    return
                dve.wait_ge(x_stored[p], 16 * (k + 1))
                if affine:
                    dve.wait_ge(shifted, n + 1)
                else:
                    dve.wait_ge(z_done, n + 3)
                nc.vector.scalar_tensor_tensor(xo[:, p, :, :], w_rows, gate, here(X, n), ALU.mult, ALU.add).then_inc(x_new, 1)
                dve.wait_ge(x_new, n + 1)
                norm_rows(nc, dve, xo[:, p], here(Y, n), t2, step2, root2, n, waited_dve).then_inc(finished, 1)

            by_sequence(dve, first, body)


def router(nc, tag, c, Y, wg, bg, L):
    with ExitStack() as ctx:
        sb = lambda n, s, d=F32: ctx.enter_context(nc.sbuf_tensor(f"{tag}_{n}", s, d))
        sem = ctx.enter_context(stage_semaphores(nc, tag))
        pair = lambda n: [sem(n + "0"), sem(n + "1")]
        bank = lambda n: ctx.enter_context(nc.psum_tensor(f"{tag}_{n}", [P, 512], F32))
        yb, yT = sb("yb", [P, 2, NU, D]), sb("yT", [P, 2, NC, SEQ])
        w, b = sb("w", [P, NC, NE]), sb("b", [P, NE])
        bankT, bankL = [bank("T0"), bank("T1")], [bank("L0"), bank("L1")]
        w_loaded, loaded = sem("w_loaded"), pair("loaded")
        turned, t_out, l_ready, l_out, waited = sem("turned"), sem("t_out"), sem("l_ready"), sem("l_out"), sem("waited")
        block = ctx.enter_context(nc.Block())

        @block.sync
        def _(sp):
            def wait(semaphore, value):
                sp.wait_ge(semaphore, value)
                if not isinstance(value, int):
                    sp.sem_inc(waited, 1)

            def load(n, p):
                sp.dma_start(yb[:, p, :, :], sequence_rows(Y, n)).then_inc(loaded[p], 16)

            def first():
                load(0, 0)
                load(1, 1)
                sp.dma_start(w[:, :, :], wg.rearrange("(c p) e -> p c e", p=P)).then_inc(w_loaded, 16)
                sp.dma_start(b[:, :], bg.partition_broadcast(P)).then_inc(w_loaded, 16)

            def body(n, p, k, more, more2):
                if more2:
                    wait(turned, n + 1)
                    load(n + 2, p)

            by_sequence(sp, first, body)

        @block.tensor
        def _(pe):
            def turn(n, p, k):
                pe.wait_ge(loaded[p], 16 * (k + 1))
                pe.wait_ge(t_out, n + 1)
                for cc in range(NC):
                    for u in range(NU):
                        ins = nc.tensor.transpose(bankT[p][:, cc * SEQ + u * P:cc * SEQ + (u + 1) * P],
                                                  yb[:, p, u, cc * P:(cc + 1) * P], c["ident"][:, :])
                ins.then_inc(turned, 1)

            def body(n, p, k, more, more2):
                pe.wait_ge(t_out, n + 3)
                pe.wait_ge(l_out, n + 1)
                for u in range(NU):
                    for kc in range(NC):
                        ins = nc.tensor.matmul(bankL[p][:, u * NE:(u + 1) * NE], yT[:, p, kc, u * P:(u + 1) * P],
                                               w[:, kc, :], start=(kc == 0), stop=(kc == NC - 1))
                ins.then_inc(l_ready, 1)
                if more2:
                    turn(n + 2, p, k + 1)

            def first():
                turn(0, 0, 0)
                turn(1, 1, 0)
                pe.wait_ge(w_loaded, 32)

            by_sequence(pe, first, body)

        @block.scalar
        def _(act):
            def bring(n, p):
                act.wait_ge(turned, n + 1)
                act.wait_ge(l_ready, n + 1)
                nc.scalar.activation(yT[:, p, :, :].rearrange("p c t -> p (c t)"), bankT[p][:, :], ACT.Copy).then_inc(t_out, 1)

            def body(n, p, k, more, more2):
                if more2:
                    bring(n + 2, p)

            def first():
                act.sem_inc(t_out, 2)
                act.sem_inc(l_ready, 2)
                bring(0, 0)
                bring(1, 1)

            by_sequence(act, first, body)

        @block.vector
        def _(dve):
            def body(n, p, k, more, more2):
                dve.wait_ge(l_ready, n + 3)
                nc.vector.tensor_tensor(L[:, bass.ds(n * NU, NU), :], bankL[p][:, 0:NU * NE].rearrange("p (u e) -> p u e", u=NU),
                                        b[:, :].unsqueeze(1).broadcast_to([P, NU, NE]), ALU.add).then_inc(l_out, 1)

            def first():
                dve.sem_inc(l_out, 2)
                dve.wait_ge(w_loaded, 32)

            by_sequence(dve, first, body)


def expert_memory(nc, ctx, tag):
    sb = lambda n, s, d=F32: ctx.enter_context(nc.sbuf_tensor(f"{tag}_{n}", s, d))
    sem = ctx.enter_context(stage_semaphores(nc, tag))
    return {"W1": sb("W1", [P, NE, NC, FF]), "W2": sb("W2", [P, NE, NF, D]), "bp": sb("bp", [3, NE * (FF + D)], BF16),
            "b_loaded": sem("b_loaded"), "e_loaded": [sem(f"e_loaded{e}") for e in range(NE)]}


EARLY = 1


def load_experts(eng, em, w1_in, w2_in, which):
    for e in which:
        eng.dma_start(em["W1"][:, e, :, :], w1_in[e].rearrange("(c p) n -> p c n", p=P)).then_inc(em["e_loaded"][e], 16)
        eng.dma_start(em["W2"][:, e, :, :], w2_in[e].rearrange("(c p) n -> p c n", p=P)).then_inc(em["e_loaded"][e], 16)


def route(nc, tag, c, L, Y, top, slots, xd, dest, weight, slot_expert, gate, em, w1_in, w2_in, parts):
    with ExitStack() as ctx:
        sb = lambda n, s, d=F32: ctx.enter_context(nc.sbuf_tensor(f"{tag}_{n}", s, d))
        sem = ctx.enter_context(stage_semaphores(nc, tag))
        full = [P, NT, NE]
        left, eq, rev, expd = sb("left", full), sb("eq", full), sb("rev", full), sb("expd", full)
        hot = [sb(f"hot{i}", full) for i in range(top)]
        m = [sb(f"m{i}", [P, NT]) for i in range(top)]
        rm, total, inv = sb("rm", [P, NT]), sb("total", [P, NT]), sb("inv", [P, NT])
        prob = [sb(f"prob{i}", [P, NT]) for i in range(top)]
        psum_, pinv = sb("psum", [P, NT]), sb("pinv", [P, NT])
        padded = sb("padded", [P, 2 * NT * NE], BF16)
        chosen = padded[:, NT * NE:2 * NT * NE]
        pos = sb("pos", full)
        count_i, tiles_i = sb("count_i", [P, NE], I32), sb("tiles_i", [P, NE], I32)
        tiles, last, start, zero8 = sb("tiles", [P, NE]), sb("last", [P, NE]), sb("start", [P, NE]), sb("zero8", [P, NE])
        destf = [sb(f"destf{i}", [P, NT]) for i in range(top)]
        slot_no, passed, slot_f = sb("slot_no", [1, slots]), sb("passed", [1, slots, NE]), sb("slot_f", [1, slots])
        rank = ctx.enter_context(nc.psum_tensor(f"{tag}_rank", [P, 512], F32))
        count = ctx.enter_context(nc.psum_tensor(f"{tag}_count", [P, 512], F32))
        ranked, step, exp_done, scattered, iota_done = sem("ranked"), sem("step"), sem("exp_done"), sem("scattered"), sem("iota_done")
        block = ctx.enter_context(nc.Block())
        per_expert = lambda a: a[:, :].unsqueeze(2).broadcast_to(full)

        marks = {}

        @block.sync
        def _(sp):
            sp.dma_start(em["bp"][:, :], parts.rearrange("s e n -> s (e n)")).then_inc(em["b_loaded"], 16)
            load_experts(sp, em, w1_in, w2_in, range(EARLY))

        @block.vector
        def _(dve):
            n = [0]

            def then(ins):
                n[0] += 1
                ins.then_inc(step, 1)
                dve.wait_ge(step, n[0])

            for e in range(NE):
                ins = nc.vector.memset(rev[:, :, e:e + 1], float(NE - e))
            nc.vector.memset(padded[:, 0:NT * NE], 0.0)
            then(nc.vector.memset(zero8[:, :], 0.0))
            for i in range(top):
                lg = L if i == 0 else left
                then(nc.vector.tensor_reduce(m[i][:, :], lg[:, :, :], AXX, ALU.max))
                then(nc.vector.tensor_tensor(eq[:, :, :], lg[:, :, :], per_expert(m[i]), ALU.is_equal))
                then(nc.vector.tensor_tensor(hot[i][:, :, :], eq[:, :, :], rev[:, :, :], ALU.mult))
                then(nc.vector.tensor_reduce(rm[:, :], hot[i][:, :, :], AXX, ALU.max))
                then(nc.vector.tensor_tensor(hot[i][:, :, :], rev[:, :, :], per_expert(rm), ALU.is_equal))
                if i + 1 < top:
                    then(nc.vector.scalar_tensor_tensor(left[:, :, :], hot[i][:, :, :], OFF, lg[:, :, :], ALU.mult, ALU.add))
            if top == 2:
                then(nc.vector.tensor_tensor(chosen[:, :].rearrange("p (t e) -> p t e", e=NE), hot[0][:, :, :], hot[1][:, :, :], ALU.add))
            else:
                then(nc.vector.tensor_copy(chosen[:, :].rearrange("p (t e) -> p t e", e=NE), hot[0][:, :, :]))
            marks["chosen"] = n[0]
            then(nc.vector.tensor_tensor(eq[:, :, :], L[:, :, :], per_expert(m[0]), ALU.subtract))
            marks["centred"] = n[0]

            dve.wait_ge(ranked, 1)
            then(nc.vector.tensor_scalar(count_i[:, :], count[:, 0:NE], float(P - 1), None, ALU.add))
            then(nc.vector.tensor_scalar(tiles_i[:, :], count_i[:, :], 7, None, ALU.arith_shift_right))
            then(nc.vector.tensor_copy(tiles[:, :], tiles_i[:, :]))
            then(nc.vector.tensor_tensor_scan(last[:, :], tiles[:, :], zero8[:, :], 0.0, ALU.add, ALU.add))
            then(nc.vector.tensor_tensor(start[:, :], last[:, :], tiles[:, :], ALU.subtract))
            then(nc.vector.scalar_tensor_tensor(pos[:, :, :], start[:, :].unsqueeze(1).broadcast_to(full), float(P),
                                                rank[:, 0:NT * NE].rearrange("p (t e) -> p t e", e=NE), ALU.mult, ALU.add))
            for i in range(top):
                then(nc.vector.tensor_tensor(left[:, :, :], hot[i][:, :, :], pos[:, :, :], ALU.mult))
                then(nc.vector.tensor_reduce(destf[i][:, :], left[:, :, :], AXX, ALU.add))
                then(nc.vector.tensor_copy(dest[i][:, :], destf[i][:, :]))
            marks["dest"] = n[0]
            dve.wait_ge(iota_done, 1)
            then(nc.vector.tensor_tensor(passed[:, :, :], last[0:1, :].unsqueeze(1).broadcast_to([1, slots, NE]),
                                         slot_no[:, :].unsqueeze(2).broadcast_to([1, slots, NE]), ALU.is_le))
            then(nc.vector.tensor_reduce(slot_f[:, :], passed[:, :, :], AXX, ALU.add))
            then(nc.vector.tensor_scalar(slot_expert[:, 0:slots], slot_f[:, :], float(NE - 1), None, ALU.min))

            dve.wait_ge(exp_done, 1)
            then(nc.vector.tensor_reduce(total[:, :], expd[:, :, :], AXX, ALU.add))
            then(nc.vector.reciprocal(inv[:, :], total[:, :]))
            for i in range(top):
                then(nc.vector.tensor_tensor(left[:, :, :], hot[i][:, :, :], expd[:, :, :], ALU.mult))
                then(nc.vector.tensor_reduce(m[i][:, :], left[:, :, :], AXX, ALU.add))
                then(nc.vector.tensor_tensor(prob[i][:, :], m[i][:, :], inv[:, :], ALU.mult))
            if top == 2:
                then(nc.vector.tensor_tensor(psum_[:, :], prob[0][:, :], prob[1][:, :], ALU.add))
                then(nc.vector.reciprocal(pinv[:, :], psum_[:, :]))
                for i in range(top):
                    then(nc.vector.tensor_tensor(prob[i][:, :], prob[i][:, :], pinv[:, :], ALU.mult))
            for i in range(top):
                then(nc.vector.tensor_scalar(weight[i][:, :], prob[i][:, :], gate, None, ALU.mult))

        @block.scalar
        def _(act):
            act.wait_ge(step, marks["centred"])
            nc.scalar.activation(expd[:, :, :], eq[:, :, :], ACT.Exp).then_inc(exp_done, 1)

        @block.tensor
        def _(pe):
            pe.wait_ge(step, marks["chosen"])
            nc.tensor.matmul(rank[:, 0:NT * NE], c["before"][:, :], chosen[:, :], start=True, stop=False)
            for j in range(1, NT):
                nc.tensor.matmul(rank[:, 0:NT * NE], c["ones"][:, :], padded[:, (NT - j) * NE:(2 * NT - j) * NE],
                                 start=False, stop=(j == NT - 1))
            for j in range(NT):
                ins = nc.tensor.matmul(count[:, 0:NE], c["ones"][:, :], chosen[:, j * NE:(j + 1) * NE],
                                       start=(j == 0), stop=(j == NT - 1))
            ins.then_inc(ranked, 1)

        @block.gpsimd
        def _(pool):
            pool.iota(slot_no[:, :], pattern=[[1, slots]], base=0, channel_multiplier=0,
                      allow_small_or_imprecise_dtypes=True).then_inc(iota_done, 1)
            pool.wait_ge(step, marks["dest"])
            for t in range(NT):
                for i in range(top):
                    pool.indirect_dma_start(out=xd, out_offset=bass.IndirectOffsetOnAxis(ap=dest[i][:, t:t + 1], axis=0),
                                            in_=Y[:, t, :], in_offset=None).then_inc(scattered, 16)
            pool.wait_ge(scattered, 16 * NT * top)


def experts(nc, tag, c, slots, xd, yd, slot_expert, em, w1_in, w2_in):
    with ExitStack() as ctx:
        sb = lambda n, s, d=F32: ctx.enter_context(nc.sbuf_tensor(f"{tag}_{n}", s, d))
        sem = ctx.enter_context(stage_semaphores(nc, tag))
        pair = lambda n: [sem(n + "0"), sem(n + "1")]
        bank = lambda n, w=512: ctx.enter_context(nc.psum_tensor(f"{tag}_{n}", [P, w], F32))
        W1, W2, bp = em["W1"], em["W2"], em["bp"]
        xs, xT, hs, hT, ys = sb("xs", [P, 2, D]), sb("xT", [P, 2, D]), sb("hs", [P, FF]), sb("hT", [P, FF]), sb("ys", [P, 2, D])
        bankX, bankY = bank("X"), bank("Y")
        bankH, bankHT = bank("H", FF), bank("HT", FF)
        b_loaded, e_loaded, w_ready = em["b_loaded"], em["e_loaded"], sem("w_ready")
        x_loaded, y_stored, waited = pair("x_loaded"), pair("y_stored"), sem("waited")
        x_turned, x_out, h_ready, h_out = sem("x_turned"), sem("x_out"), sem("h_ready"), sem("h_out")
        h_turned, ht_out, y_ready, y_out = sem("h_turned"), sem("ht_out"), sem("y_ready"), sem("y_out")
        block = ctx.enter_context(nc.Block())
        ident = c["ident"]
        odd = slots % 2
        assert odd

        def by_slot(eng, first, body, lastly):
            first()
            with eng.Fori(0, (slots - 3) // 2) as j:
                body(2 * j + 1, 1, j, True)
                body(2 * j + 2, 0, j + 1, True)
            body(slots - 2, 1, (slots - 3) // 2, True)
            body(slots - 1, 0, (slots - 1) // 2, False)
            lastly()

        @block.sync
        def _(sp):
            def wait(semaphore, value):
                sp.wait_ge(semaphore, value)
                if not isinstance(value, int):
                    sp.sem_inc(waited, 1)

            def load(s, p):
                sp.dma_start(xs[:, p, :], xd[bass.ds(s * P, P), :]).then_inc(x_loaded[p], 16)

            def store(s, p):
                sp.dma_start(yd[bass.ds(s * P, P), :], ys[:, p, :]).then_inc(y_stored[p], 16)

            load(0, 0)
            load(1, 1)

            def first():
                sp.wait_ge(x_turned, 1)
                load(2, 0)

            def body(s, p, k, more):
                wait(y_out, s + 1)
                store(s - 1, 1 - p)
                if more and not (isinstance(s, int) and s + 2 >= slots):
                    wait(x_turned, s + 1)
                    load(s + 2, p)

            def lastly():
                sp.wait_ge(y_out, slots + 1)
                store(slots - 1, 0)

            by_slot(sp, first, body, lastly)
            sp.wait_ge(y_stored[0], 16 + 16 * ((slots + 1) // 2))
            sp.wait_ge(y_stored[1], 16 + 16 * (slots // 2))

        @block.gpsimd
        def _(pool):
            for e in range(NE):
                if e >= EARLY:
                    load_experts(pool, em, w1_in, w2_in, (e,))
                pool.wait_ge(e_loaded[e], 32)
                pool.sem_inc(w_ready, 1)

        @block.tensor
        def _(pe):
            def turn_x(s, p, k):
                pe.wait_ge(x_loaded[p], 16 * (k + 1))
                pe.wait_ge(x_out, s + 1)
                for cc in range(NC):
                    ins = nc.tensor.transpose(bankX[:, cc * P:(cc + 1) * P], xs[:, p, cc * P:(cc + 1) * P], ident[:, :])
                ins.then_inc(x_turned, 1)

            def expert_of(s):
                return nc.tensor.value_load(slot_expert[0:1, bass.ds(s, 1)], min_val=0, max_val=NE - 1)

            def up(s, p, e):
                pe.wait_ge(w_ready, e + 1)
                pe.wait_ge(x_out, s + 2)
                pe.wait_ge(h_out, s + 1)
                w1e = W1[:, bass.ds(e, 1), :, :].rearrange("p o c n -> p (o c) n")
                for half in range(2):
                    cols = slice(half * 512, (half + 1) * 512)
                    nc.tensor.matmul(bankH[:, cols], c["ones"][0:3, :], bp[:, bass.ds(e * (FF + D) + half * 512, 512)],
                                     start=True, stop=False)
                    for cc in range(NC):
                        ins = nc.tensor.matmul(bankH[:, cols], xT[:, p, cc * P:(cc + 1) * P], w1e[:, cc, cols],
                                               start=False, stop=(cc == NC - 1))
                ins.then_inc(h_ready, 1)

            def turn_h(s):
                pe.wait_ge(h_out, s + 2)
                pe.wait_ge(ht_out, s + 1)
                for f in range(NF):
                    ins = nc.tensor.transpose(bankHT[:, f * P:(f + 1) * P], hs[:, f * P:(f + 1) * P], ident[:, :])
                ins.then_inc(h_turned, 1)

            def down(s, e):
                pe.wait_ge(ht_out, s + 2)
                pe.wait_ge(y_out, s + 1)
                w2e = W2[:, bass.ds(e, 1), :, :].rearrange("p o c n -> p (o c) n")
                nc.tensor.matmul(bankY[:, 0:D], c["ones"][0:3, :], bp[:, bass.ds(e * (FF + D) + FF, D)], start=True, stop=False)
                for f in range(NF):
                    ins = nc.tensor.matmul(bankY[:, 0:D], hT[:, f * P:(f + 1) * P], w2e[:, f, :],
                                           start=False, stop=(f == NF - 1))
                ins.then_inc(y_ready, 1)

            def first():
                pe.wait_ge(b_loaded, 16)
                turn_x(0, 0, 0)
                up(0, 0, expert_of(0))
                turn_x(1, 1, 0)
                turn_h(0)

            def body(s, p, k, more):
                up(s, p, expert_of(s))
                down(s - 1, expert_of(s - 1))
                if more:
                    turn_x(s + 1, 1 - p, k + p)
                turn_h(s)

            by_slot(pe, first, body, lambda: down(slots - 1, expert_of(slots - 1)))

        @block.scalar
        def _(act):
            def bring_x(s, p):
                act.wait_ge(x_turned, s + 1)
                if not (isinstance(s, int) and s < 2):
                    act.wait_ge(h_ready, s - 1)
                nc.scalar.activation(xT[:, p, :], bankX[:, 0:D], ACT.Copy).then_inc(x_out, 1)

            def bring_h(s):
                act.wait_ge(h_turned, s + 2)
                act.wait_ge(y_ready, s + 1)
                nc.scalar.activation(hT[:, :], bankHT[:, :], ACT.Copy).then_inc(ht_out, 1)

            def first():
                act.sem_inc(x_out, 1)
                act.sem_inc(ht_out, 1)
                act.sem_inc(y_ready, 1)
                bring_x(0, 0)
                bring_x(1, 1)
                bring_h(0)

            def body(s, p, k, more):
                if more:
                    bring_x(s + 1, 1 - p)
                bring_h(s)

            by_slot(act, first, body, lambda: None)

        @block.vector
        def _(dve):
            def relu(s):
                dve.wait_ge(h_ready, s + 1)
                dve.wait_ge(h_turned, s + 1)
                nc.vector.tensor_scalar(hs[:, :], bankH[:, :], 0.0, None, ALU.max).then_inc(h_out, 1)

            def out_rows(s, p, k):
                dve.wait_ge(y_ready, s + 2)
                dve.wait_ge(y_stored[p], 16 * (k + 1))
                nc.vector.tensor_copy(ys[:, p, :], bankY[:, 0:D]).then_inc(y_out, 1)

            def first():
                dve.sem_inc(h_out, 1)
                dve.sem_inc(h_turned, 1)
                dve.sem_inc(y_out, 1)
                for p in range(2):
                    dve.sem_inc(y_stored[p], 16)
                relu(0)

            def body(s, p, k, more):
                relu(s)
                out_rows(s - 1, 1 - p, k - 1 + p)

            by_slot(dve, first, body, lambda: out_rows(slots - 1, 0, (slots - 1) // 2))


def combine(nc, tag, X, Y, top, yd, dest, weight, out=None):
    with ExitStack() as ctx:
        sb = lambda n, s, d=F32: ctx.enter_context(nc.sbuf_tensor(f"{tag}_{n}", s, d))
        sem = ctx.enter_context(stage_semaphores(nc, tag))
        RING = 8
        g = sb("g", [P, RING, D])
        t = norm_tiles(sb)
        gathered = [sem(f"gathered{r}") for r in range(RING)]
        added, step, root, waited, stored, normed = sem("added"), sem("step"), sem("root"), sem("waited"), sem("stored"), sem("normed")
        block = ctx.enter_context(nc.Block())

        @block.gpsimd
        def _(pool):
            for q in range(NT * top):
                i, t_ = q // NU % top, q // (NU * top) * NU + q % NU
                if q >= RING:
                    pool.wait_ge(added, q - RING + 1)
                pool.indirect_dma_start(out=g[:, q % RING, :], out_offset=None, in_=yd,
                                        in_offset=bass.IndirectOffsetOnAxis(ap=dest[i][:, t_:t_ + 1], axis=0)
                                        ).then_inc(gathered[q % RING], 16)

        @block.vector
        def _(dve):
            for n in range(B):
                for i in range(top):
                    for u in range(NU):
                        tt = n * NU + u
                        q = (n * top + i) * NU + u
                        dve.wait_ge(gathered[q % RING], 16 * (q // RING + 1))
                        if i:
                            dve.wait_ge(added, q - NU + 1)
                        nc.vector.scalar_tensor_tensor(X[:, tt, :], g[:, q % RING, :], weight[i][:, tt:tt + 1], X[:, tt, :],
                                                       ALU.mult, ALU.add).then_inc(added, 1)
                if out is None:
                    dve.wait_ge(added, (n + 1) * NU * top)
                    norm_rows(nc, dve, X[:, n * NU:(n + 1) * NU, :], Y[:, n * NU:(n + 1) * NU, :], t, step, root, n, waited).then_inc(normed, 1)
                    dve.wait_ge(normed, n + 1)

        @block.scalar
        def _(act):
            if out is None:
                for n in range(B):
                    norm_root(nc, act, t, step, root, n)

        @block.sync
        def _(sp):
            if out is not None:
                for n in range(B):
                    sp.wait_ge(added, (n + 1) * NU * top)
                    sp.dma_start(sequence_rows(out, n), X[:, n * NU:(n + 1) * NU, :]).then_inc(stored, 16)
                sp.wait_ge(stored, 16 * B)


SLOTS0 = (2 * T + (P - 1) * NE) // P
SLOTS1 = (T + (P - 1) * NE) // P


def flamingo(nc, a, out):
    dram = lambda n, s, d=F32: nc.dram_tensor(n, s, d, kind="Internal").ap()
    xd0, yd0 = dram("xd0", (SLOTS0 * P, D)), dram("yd0", (SLOTS0 * P, D))
    xd1, yd1 = dram("xd1", (SLOTS1 * P, D)), dram("yd1", (SLOTS1 * P, D))
    parts0, parts1 = dram("parts0", (3, NE, FF + D), BF16), dram("parts1", (3, NE, FF + D), BF16)
    key_off = dram("key_off", (B, SEQ), BF16)
    ctx_in = a["ctx_1024"]

    with ExitStack() as ctx:
        sb = lambda n, s, d=F32: ctx.enter_context(nc.sbuf_tensor(n, s, d))
        ident, identb = sb("ident", [P, P]), sb("identb", [P, P], BF16)
        before, ones = sb("before", [P, P], BF16), sb("ones", [P, P], BF16)
        gates = sb("gates", [P, 4])
        L = sb("L", [P, NT, NE])
        dest = [sb(f"dest{i}", [P, NT], U32) for i in range(2)]
        weight = [sb(f"weight{i}", [P, NT]) for i in range(2)]
        slot_expert = sb("slot_expert", [1, SLOTS0], I32)
        X, Y = sb("X", [P, NT, D]), sb("Y", [P, NT, D])
        c = {"ident": ident, "identb": identb, "before": before, "ones": ones}
        gate_x0, gate_x1, gate_f0, gate_f1 = (gates[:, i:i + 1] for i in range(4))

        c["gates"] = gates
        masks_memory = ExitStack()
        mb = lambda n, s, d: masks_memory.enter_context(nc.sbuf_tensor(n, s, d))
        masks = [(a[m], mb(f"Bm{i}", [P, NU * SEQ], BF16), mb(f"BmT{i}", [P, NU * SEQ], BF16), mb(f"R{i}", [P, SEQ], F32))
                 for i, m in ((1, "mask_1x1xSxS2_ik0"), (2, "mask_1x1xSxS2_if1"))]
        prepare(nc, a, c, masks, X, Y, key_off, ((a["L0_ffn_b1"], a["L0_ffn_b2"], parts0), (a["L1_ffn_b1"], a["L1_ffn_b2"], parts1)),
                (xd0, xd1))

        def xattn_weights(pre):
            return {"wq": a[f"c_{pre}wq"], "bq": a[f"c_{pre}bq"], "wk": a[f"c_{pre}wk"], "bk": a[f"c_{pre}bk"],
                    "wv": a[pre + "wv"], "bv": a[pre + "bv"]}

        with nc.sbuf_tensor("AO0", [P, NT, D], F32) as AO:
            for i in (1, 2):
                pre = f"L0_xattn_m{i}_"
                attention(nc, f"att{i}", c, Y, ctx_in if i == 2 else None, xattn_weights(pre), AO, mask=masks[i - 1][1:])
                token_block(nc, f"mid{i}", c, X, Y, AO, {"wo": a[pre + "wo"], "b": a[pre + "bo"], "g": a[f"L0_xattn_ln{i}_g"],
                                                          "beta": a[f"L0_xattn_ln{i}_b"]}, affine=True, gate=None, ffn=False)
        masks_memory.close()
        token_block(nc, "ffn", c, X, Y, None, {"w1": a["L0_xattn_ff_w1"], "b1": a["L0_xattn_ff_b1"], "w2": a["L0_xattn_ff_w2"],
                                               "b": a["L0_xattn_ff_b2"], "g": a["L0_xattn_ln3_g"], "beta": a["L0_xattn_ln3_b"]},
                    affine=True, gate=gate_x0, ffn=True)
        router(nc, "router0", c, Y, a["L0_ffn_Wg"], a["L0_ffn_bg"], L)
        with ExitStack() as s:
            em = expert_memory(nc, s, "em0")
            route(nc, "route0", c, L, Y, 2, SLOTS0, xd0, dest, weight, slot_expert, gate_f0,
                  em, a["L0_ffn_W1"], a["L0_ffn_W2"], parts0)
            experts(nc, "exp0", c, SLOTS0, xd0, yd0, slot_expert, em, a["L0_ffn_W1"], a["L0_ffn_W2"])
        combine(nc, "comb0", X, Y, 2, yd0, dest, weight)
        with nc.sbuf_tensor("AO1", [P, NT, D], F32) as AO:
            wkv, bkv = a["L1_xattn_Wkv"], a["L1_xattn_bkv"]
            w = {"wv": wkv[:, D:2 * D], "bv": bkv[D:2 * D], **{k: a["c_L1_" + k] for k in ("wq", "bq", "wk", "bk")},
                 "wqs": a["c_wq_pairs"], "bqs": a["c_bq_pairs"], "wks": a["c_wk_pairs"], "bks": a["c_bk_pairs"]}
            attention(nc, "att3", c, Y, ctx_in, w, AO, rope={"keys": a["mask_BxS2_bf1"], "key_off": key_off, **{
                k: a["c_" + k] for k in ("cosq", "sinq", "cosk", "sink")}})
            token_block(nc, "out", c, X, Y, AO, {"wo": a["L1_xattn_Wo"], "b": a["L1_xattn_bo"]}, affine=False, gate=gate_x1, ffn=False)
        router(nc, "router1", c, Y, a["L1_ffn_router_W"], a["L1_ffn_router_b"], L)
        with ExitStack() as s:
            em = expert_memory(nc, s, "em1")
            route(nc, "route1", c, L, Y, 1, SLOTS1, xd1, dest, weight, slot_expert, gate_f1,
                  em, a["L1_ffn_W1"], a["L1_ffn_W2"], parts1)
            experts(nc, "exp1", c, SLOTS1, xd1, yd1, slot_expert, em, a["L1_ffn_W1"], a["L1_ffn_W2"])
        combine(nc, "comb1", X, Y, 1, yd1, dest, weight, out=out)


def constants():
    import numpy as np
    f = np.float32
    inv = (f(1.0) / f(10000.0) ** (np.arange(0, DK, 2, dtype=f) / f(DK))).astype(f)
    pos = (f(10.0) * (np.arange(SEQ, dtype=f) / f(SEQ))).astype(f)
    angle = (pos[:, None] * inv).astype(f)
    feature = np.arange(D) // H
    cos, sin = np.cos(angle).T[feature // 2].astype(f), np.sin(angle).T[feature // 2].astype(f)
    sign = np.where(feature % 2 == 0, f(-1), f(1))[:, None]
    return {"c_ident": np.eye(P, dtype=f), "c_before": np.triu(np.ones((P, P), f), 1),
            "c_cosk": cos, "c_sink": sin * sign, "c_cosq": cos * f(0.125), "c_sinq": sin * sign * f(0.125)}


def kernel(**inputs):
    import numpy as np
    import concourse.bacc as bacc
    from concourse.bass_utils import run_bass_kernel_spmd

    def by_feature(w):
        return np.swapaxes(w.reshape(w.shape[:-1] + (H, DK)), -1, -2).reshape(w.shape)

    def pairs(w):
        return w.reshape(w.shape[:-1] + (-1, 2))[..., ::-1].reshape(w.shape)

    given = {k: np.asarray(v) for k, v in inputs.items()}
    given["mask_BxS2_bf1"] = given["mask_BxS2_bf1"].view(np.uint8)
    for pre in ("L0_xattn_m1_", "L0_xattn_m2_"):
        for k in ("wq", "bq", "wk", "bk"):
            given[f"c_{pre}{k}"] = by_feature(given.pop(pre + k))
    wkv, bkv = given["L1_xattn_Wkv"], given["L1_xattn_bkv"]
    for k, v in (("q", given.pop("L1_xattn_Wq")), ("k", np.ascontiguousarray(wkv[:, :D]))):
        given[f"c_L1_w{k}"], given[f"c_w{k}_pairs"] = by_feature(v), by_feature(pairs(v))
    for k, v in (("q", given.pop("L1_xattn_bq")), ("k", bkv[:D])):
        given[f"c_L1_b{k}"], given[f"c_b{k}_pairs"] = by_feature(v), by_feature(pairs(v))
    given.update(constants())
    nc = bacc.Bacc("TRN2", target_bir_lowering=False, num_devices=1)
    arrays, aps = {}, {}
    for name, v in given.items():
        v = np.ascontiguousarray(v)
        arrays[f"in_{name}"] = v
        aps[name] = nc.dram_tensor(f"in_{name}", v.shape, mybir.dt.from_np(v.dtype), kind="ExternalInput").ap()
    out = nc.dram_tensor("out_0", (B, SEQ, D), F32, kind="ExternalOutput").ap()
    flamingo(nc, aps, out)
    return run_bass_kernel_spmd(nc, [arrays], core_ids=[0]).results[0]["out_0"]
```
